# Optimizing a Trainium2 kernel written in Bass

```python
import numpy as np
import jax
import jax.numpy as jnp

def _softmax(x, axis=-1):
    return jax.nn.softmax(x, axis=axis)

def _gelu(x):
    return jax.nn.gelu(x, approximate=True)

def _silu(x):
    return jax.nn.silu(x)

def _sigmoid(x):
    return jax.nn.sigmoid(x)

def _layernorm(x, axis=-1, eps=1e-05):
    m = jnp.mean(x, axis=axis, keepdims=True)
    v = jnp.var(x, axis=axis, keepdims=True)
    return (x - m) / jnp.sqrt(v + eps)

def _scatter_add(tgt, idx, src, axis=0):
    return tgt.at[idx].add(src)

def _segment_sum(src, seg, n):
    return jax.ops.segment_sum(src, seg, n)
kernel_name = 'mk_hybrid_d1_jaxref_r8_cec7c7'

def setup_inputs(seed: int=0):
    np.random.seed(seed)
    _w = jnp.asarray

    def _L0_attn_a_setup():
        import jax, jax.numpy as jnp
        import numpy as np
        import math
        from jax import lax
        B, L, D = (8, 512, 128)
        FILTER_ORDER = 64
        EMB_DIM = 3
        SHIFT = 0.05
        KSIZE = 3

        def _implicit_filter(f_w1, f_b1, freq1, f_w2, f_b2, freq2, f_w3, f_b3, freq3, f_wout):
            t = jnp.linspace(0.0, 1.0, L)
            t_resc = jnp.linspace(0.0, L - 1.0, L)
            w = 2.0 * jnp.pi * t_resc / L
            bands = (EMB_DIM - 1) // 2
            f = jnp.linspace(0.0001, bands - 1.0, bands)
            fw = f[None, :] * w[:, None]
            z = jnp.concatenate([t[:, None], jnp.cos(fw), -jnp.sin(fw)], axis=-1)
            h = jnp.sin(freq1 * (z @ f_w1 + f_b1))
            h = jnp.sin(freq2 * (h @ f_w2 + f_b2))
            h = jnp.sin(freq3 * (h @ f_w3 + f_b3))
            h = h @ f_wout
            max_decay = math.log(0.01) / 0.3
            min_decay = math.log(0.01) / 1.5
            deltas = jnp.linspace(min_decay, max_decay, D)
            decay = jnp.exp(-t[:, None] * jnp.abs(deltas)[None, :])
            return h * (decay + SHIFT)
        key = jax.random.key(seed)
        ks = jax.random.split(key, 12)
        s = 0.02
        return {'u': jax.random.normal(ks[0], (B, L, D), jnp.float32), 'w_in': jax.random.normal(ks[1], (D, 3 * D), jnp.float32) * s, 'b_in': jnp.zeros((3 * D,), jnp.float32), 'sf_w': jax.random.normal(ks[2], (3 * D, KSIZE), jnp.float32) * 0.3, 'sf_b': jnp.zeros((3 * D,), jnp.float32), 'f_w1': jax.random.normal(ks[3], (EMB_DIM, FILTER_ORDER), jnp.float32) * 0.5, 'f_b1': jnp.zeros((FILTER_ORDER,), jnp.float32), 'freq1': jnp.ones((FILTER_ORDER,), jnp.float32), 'f_w2': jax.random.normal(ks[4], (FILTER_ORDER, FILTER_ORDER), jnp.float32) * 0.12, 'f_b2': jnp.zeros((FILTER_ORDER,), jnp.float32), 'freq2': jnp.ones((FILTER_ORDER,), jnp.float32), 'f_w3': jax.random.normal(ks[5], (FILTER_ORDER, FILTER_ORDER), jnp.float32) * 0.12, 'f_b3': jnp.zeros((FILTER_ORDER,), jnp.float32), 'freq3': jnp.ones((FILTER_ORDER,), jnp.float32), 'f_wout': jax.random.normal(ks[6], (FILTER_ORDER, D), jnp.float32) * s, 'filt_bias': jax.random.normal(ks[7], (D,), jnp.float32), 'w_out': jax.random.normal(ks[8], (D, D), jnp.float32) * s, 'b_out': jnp.zeros((D,), jnp.float32)}
    _L0_attn_a_in = _L0_attn_a_setup()

    def _L0_attn_b_setup():
        import jax, jax.numpy as jnp
        import numpy as np
        HID = 128
        EXP = 512

        def _min_gru(x_in, Wz, bz, Wh, bh):
            z = jax.nn.sigmoid(jnp.einsum('bse,ef->bsf', x_in, Wz) + bz)
            h_tilde = jnp.einsum('bse,ef->bsf', x_in, Wh) + bh
            a = 1.0 - z
            b = z * h_tilde

            def combine(c1, c2):
                a1, b1 = c1
                a2, b2 = c2
                return (a2 * a1, a2 * b1 + b2)
            _, h = jax.lax.associative_scan(combine, (a, b), axis=1)
            return h
        key = jax.random.key(seed)
        ks = jax.random.split(key, 11)
        s = lambda fan_in: 1.0 / np.sqrt(fan_in)
        return {'x': jax.random.normal(ks[0], (4, 256, HID), dtype=jnp.float32), 'W1': jax.random.uniform(ks[1], (HID, EXP), jnp.float32, -s(HID), s(HID)), 'b1': jax.random.uniform(ks[2], (EXP,), jnp.float32, -s(HID), s(HID)), 'W2': jax.random.uniform(ks[3], (HID, EXP), jnp.float32, -s(HID), s(HID)), 'b2': jax.random.uniform(ks[4], (EXP,), jnp.float32, -s(HID), s(HID)), 'Wz': jax.random.uniform(ks[5], (EXP, EXP), jnp.float32, -s(EXP), s(EXP)), 'bz': jax.random.uniform(ks[6], (EXP,), jnp.float32, -s(EXP), s(EXP)), 'Wh': jax.random.uniform(ks[7], (EXP, EXP), jnp.float32, -s(EXP), s(EXP)), 'bh': jax.random.uniform(ks[8], (EXP,), jnp.float32, -s(EXP), s(EXP)), 'Wo': jax.random.uniform(ks[9], (EXP, HID), jnp.float32, -s(EXP), s(EXP)), 'bo': jax.random.uniform(ks[10], (HID,), jnp.float32, -s(EXP), s(EXP))}
    _L0_attn_b_in = _L0_attn_b_setup()

    def _L0_ffn_setup():
        import jax, jax.numpy as jnp
        import numpy as np
        B, S, D, H, E = (8, 256, 128, 512, 16)
        key = jax.random.key(seed)
        ks = jax.random.split(key, 4)
        sd = 1.0 / np.sqrt(D).astype(np.float32)
        sh = 1.0 / np.sqrt(H).astype(np.float32)
        return {'x': jax.random.normal(ks[0], (B, S, D), jnp.float32), 'Wg': jax.random.normal(ks[1], (D, E), jnp.float32) * sd, 'bg': jnp.zeros((E,), jnp.float32), 'W1': jax.random.normal(ks[2], (E, D, H), jnp.float32) * sd, 'b1': jnp.zeros((E, H), jnp.float32), 'W2': jax.random.normal(ks[3], (E, H, D), jnp.float32) * sh, 'b2': jnp.zeros((E, D), jnp.float32)}
    _L0_ffn_in = _L0_ffn_setup()
    _d = {'L0_attn_a_u': _L0_attn_a_in['u'], 'L0_attn_a_w_in': _L0_attn_a_in['w_in'], 'L0_attn_a_b_in': _L0_attn_a_in['b_in'], 'L0_attn_a_sf_w': _L0_attn_a_in['sf_w'], 'L0_attn_a_sf_b': _L0_attn_a_in['sf_b'], 'L0_attn_a_f_w1': _L0_attn_a_in['f_w1'], 'L0_attn_a_f_b1': _L0_attn_a_in['f_b1'], 'L0_attn_a_freq1': _L0_attn_a_in['freq1'], 'L0_attn_a_f_w2': _L0_attn_a_in['f_w2'], 'L0_attn_a_f_b2': _L0_attn_a_in['f_b2'], 'L0_attn_a_freq2': _L0_attn_a_in['freq2'], 'L0_attn_a_f_w3': _L0_attn_a_in['f_w3'], 'L0_attn_a_f_b3': _L0_attn_a_in['f_b3'], 'L0_attn_a_freq3': _L0_attn_a_in['freq3'], 'L0_attn_a_f_wout': _L0_attn_a_in['f_wout'], 'L0_attn_a_filt_bias': _L0_attn_a_in['filt_bias'], 'L0_attn_a_w_out': _L0_attn_a_in['w_out'], 'L0_attn_a_b_out': _L0_attn_a_in['b_out'], 'L0_attn_b_W1': _L0_attn_b_in['W1'], 'L0_attn_b_b1': _L0_attn_b_in['b1'], 'L0_attn_b_W2': _L0_attn_b_in['W2'], 'L0_attn_b_b2': _L0_attn_b_in['b2'], 'L0_attn_b_Wz': _L0_attn_b_in['Wz'], 'L0_attn_b_bz': _L0_attn_b_in['bz'], 'L0_attn_b_Wh': _L0_attn_b_in['Wh'], 'L0_attn_b_bh': _L0_attn_b_in['bh'], 'L0_attn_b_Wo': _L0_attn_b_in['Wo'], 'L0_attn_b_bo': _L0_attn_b_in['bo'], 'L0_ffn_Wg': _L0_ffn_in['Wg'], 'L0_ffn_bg': _L0_ffn_in['bg'], 'L0_ffn_W1': _L0_ffn_in['W1'], 'L0_ffn_b1': _L0_ffn_in['b1'], 'L0_ffn_W2': _L0_ffn_in['W2'], 'L0_ffn_b2': _L0_ffn_in['b2']}
    _x0 = _d['L0_attn_a_u']
    _d['L0_attn_a_u'] = jax.random.normal(jax.random.fold_in(jax.random.key(seed), 1), (8, 1024, 128), dtype=_x0.dtype)
    del _x0
    return _d

def reference(L0_attn_a_u, L0_attn_a_w_in, L0_attn_a_b_in, L0_attn_a_sf_w, L0_attn_a_sf_b, L0_attn_a_f_w1, L0_attn_a_f_b1, L0_attn_a_freq1, L0_attn_a_f_w2, L0_attn_a_f_b2, L0_attn_a_freq2, L0_attn_a_f_w3, L0_attn_a_f_b3, L0_attn_a_freq3, L0_attn_a_f_wout, L0_attn_a_filt_bias, L0_attn_a_w_out, L0_attn_a_b_out, L0_attn_b_W1, L0_attn_b_b1, L0_attn_b_W2, L0_attn_b_b2, L0_attn_b_Wz, L0_attn_b_bz, L0_attn_b_Wh, L0_attn_b_bh, L0_attn_b_Wo, L0_attn_b_bo, L0_ffn_Wg, L0_ffn_bg, L0_ffn_W1, L0_ffn_b1, L0_ffn_W2, L0_ffn_b2):

    def _L0_attn_a_ref(u, w_in, b_in, sf_w, sf_b, f_w1, f_b1, freq1, f_w2, f_b2, freq2, f_w3, f_b3, freq3, f_wout, filt_bias, w_out, b_out):
        import jax, jax.numpy as jnp
        import numpy as np
        import math
        from jax import lax
        B, L, D = (8, 512, 128)
        FILTER_ORDER = 64
        EMB_DIM = 3
        SHIFT = 0.05
        KSIZE = 3

        def _implicit_filter(f_w1, f_b1, freq1, f_w2, f_b2, freq2, f_w3, f_b3, freq3, f_wout):
            t = jnp.linspace(0.0, 1.0, L)
            t_resc = jnp.linspace(0.0, L - 1.0, L)
            w = 2.0 * jnp.pi * t_resc / L
            bands = (EMB_DIM - 1) // 2
            f = jnp.linspace(0.0001, bands - 1.0, bands)
            fw = f[None, :] * w[:, None]
            z = jnp.concatenate([t[:, None], jnp.cos(fw), -jnp.sin(fw)], axis=-1)
            h = jnp.sin(freq1 * (z @ f_w1 + f_b1))
            h = jnp.sin(freq2 * (h @ f_w2 + f_b2))
            h = jnp.sin(freq3 * (h @ f_w3 + f_b3))
            h = h @ f_wout
            max_decay = math.log(0.01) / 0.3
            min_decay = math.log(0.01) / 1.5
            deltas = jnp.linspace(min_decay, max_decay, D)
            decay = jnp.exp(-t[:, None] * jnp.abs(deltas)[None, :])
            return h * (decay + SHIFT)
        b, l, d = u.shape
        up = (u @ w_in + b_in).transpose(0, 2, 1)
        uc = lax.conv_general_dilated(up, sf_w[:, None, :], (1,), [(KSIZE - 1, KSIZE - 1)], feature_group_count=3 * d, dimension_numbers=('NCH', 'OIH', 'NCH'))[..., :l] + sf_b[None, :, None]
        x0, x1, v = jnp.split(uc, 3, axis=1)
        k = _implicit_filter(f_w1, f_b1, freq1, f_w2, f_b2, freq2, f_w3, f_b3, freq3, f_wout).T
        v = v * x1
        n = 2 * l
        y = jnp.fft.irfft(jnp.fft.rfft(v, n=n) * jnp.fft.rfft(k, n=n), n=n)[..., :l]
        v = y + v * filt_bias[None, :, None]
        out = (v * x0).transpose(0, 2, 1)
        return out @ w_out + b_out

    def _L0_attn_b_ref(x, W1, b1, W2, b2, Wz, bz, Wh, bh, Wo, bo):
        import jax, jax.numpy as jnp
        import numpy as np
        HID = 128
        EXP = 512

        def _min_gru(x_in, Wz, bz, Wh, bh):
            z = jax.nn.sigmoid(jnp.einsum('bse,ef->bsf', x_in, Wz) + bz)
            h_tilde = jnp.einsum('bse,ef->bsf', x_in, Wh) + bh
            a = 1.0 - z
            b = z * h_tilde

            def combine(c1, c2):
                a1, b1 = c1
                a2, b2 = c2
                return (a2 * a1, a2 * b1 + b2)
            _, h = jax.lax.associative_scan(combine, (a, b), axis=1)
            return h
        x_in = jax.nn.silu(jnp.einsum('bsd,de->bse', x, W1) + b1)
        x_skip = jax.nn.silu(jnp.einsum('bsd,de->bse', x, W2) + b2)
        h = _min_gru(x_in, Wz, bz, Wh, bh)
        return jnp.einsum('bse,ed->bsd', x_skip + h, Wo) + bo

    def _L0_ffn_ref(x, Wg, bg, W1, b1, W2, b2):
        import jax, jax.numpy as jnp
        import numpy as np
        B, S, D, H, E = (8, 256, 128, 512, 16)
        d = x.shape[-1]
        xf = x.reshape(-1, d)
        n_tok = xf.shape[0]
        n_exp = Wg.shape[1]
        cap = -(-n_tok // n_exp)
        score = jax.nn.softmax(xf @ Wg + bg, axis=-1)
        gate = jnp.max(score, axis=-1)
        idx = jnp.argmax(score, axis=-1)
        onehot = jax.nn.one_hot(idx, n_exp, dtype=jnp.int32)
        pos = jnp.sum((jnp.cumsum(onehot, axis=0) - 1) * onehot, axis=-1)
        keep = pos < cap
        safe_pos = jnp.where(keep, pos, cap - 1)
        buf = jnp.zeros((n_exp, cap, d), x.dtype).at[idx, safe_pos].add(jnp.where(keep[:, None], xf, 0.0))
        h = jax.nn.relu(jnp.einsum('ecd,edh->ech', buf, W1) + b1[:, None, :])
        y = jnp.einsum('ech,ehd->ecd', h, W2) + b2[:, None, :]
        out = y[idx, safe_pos] * gate[:, None]
        out = jnp.where(keep[:, None], out, 0.0)
        return out.reshape(x.shape)
    x = L0_attn_a_u
    x = x + _L0_attn_a_ref(_layernorm(x, axis=-1), L0_attn_a_w_in, L0_attn_a_b_in, L0_attn_a_sf_w, L0_attn_a_sf_b, L0_attn_a_f_w1, L0_attn_a_f_b1, L0_attn_a_freq1, L0_attn_a_f_w2, L0_attn_a_f_b2, L0_attn_a_freq2, L0_attn_a_f_w3, L0_attn_a_f_b3, L0_attn_a_freq3, L0_attn_a_f_wout, L0_attn_a_filt_bias, L0_attn_a_w_out, L0_attn_a_b_out)
    x = x + _L0_ffn_ref(_layernorm(x, axis=-1), L0_ffn_Wg, L0_ffn_bg, L0_ffn_W1, L0_ffn_b1, L0_ffn_W2, L0_ffn_b2)
    x = x + _L0_attn_b_ref(_layernorm(x, axis=-1), L0_attn_b_W1, L0_attn_b_b1, L0_attn_b_W2, L0_attn_b_b2, L0_attn_b_Wz, L0_attn_b_bz, L0_attn_b_Wh, L0_attn_b_bh, L0_attn_b_Wo, L0_attn_b_bo)
    x = x + _L0_ffn_ref(_layernorm(x, axis=-1), L0_ffn_Wg, L0_ffn_bg, L0_ffn_W1, L0_ffn_b1, L0_ffn_W2, L0_ffn_b2)
    return x

_drawn_inputs = setup_inputs


def setup_inputs(seed=0):
    import zlib

    import numpy as np

    out = dict(_drawn_inputs(seed))
    spreads = {'L0_attn_a_b_in': (0.0, 0.391),
     'L0_attn_a_sf_b': (0.0, 0.337),
     'L0_attn_a_f_b1': (0.0, 0.8),
     'L0_attn_a_freq1': (1.0, 0.6),
     'L0_attn_a_f_b2': (0.0, 0.8),
     'L0_attn_a_freq2': (1.0, 0.6),
     'L0_attn_a_f_b3': (0.0, 0.8),
     'L0_attn_a_freq3': (1.0, 0.6),
     'L0_attn_a_b_out': (0.0, 0.8),
     'L0_ffn_bg': (0.0, 0.8),
     'L0_ffn_b1': (0.0, 0.8),
     'L0_ffn_b2': (0.0, 0.8)}
    factors = {'L0_attn_a_w_in': 4.877,
     'L0_attn_a_sf_w': 3.33,
     'L0_attn_a_f_w1': 3.18,
     'L0_attn_a_f_w2': 3.621,
     'L0_attn_a_f_w3': 3.982,
     'L0_attn_a_f_wout': 3.498,
     'L0_attn_a_filt_bias': 8.0,
     'L0_attn_a_w_out': 2.742,
     'L0_attn_b_b1': 23.544,
     'L0_attn_b_Wz': 34.128,
     'L0_attn_b_bz': 64.0,
     'L0_attn_b_W1': 8.0,
     'L0_attn_b_W2': 8.0,
     'L0_attn_b_b2': 8.0,
     'L0_attn_b_Wh': 8.0,
     'L0_attn_b_bh': 8.0,
     'L0_attn_b_Wo': 8.0,
     'L0_attn_b_bo': 44.711,
     'L0_ffn_Wg': 8.0,
     'L0_ffn_W1': 8.0,
     'L0_ffn_W2': 8.0}
    for name, (base, spread) in spreads.items():
        noise = np.random.default_rng([zlib.crc32(name.encode()), seed]).standard_normal(out[name].shape)
        drawn = base * np.exp(spread * noise) if base else spread * noise
        out[name] = jnp.asarray(drawn.astype(out[name].dtype))
    for name, factor in factors.items():
        out[name] = (out[name] * factor).astype(out[name].dtype)
    return out
```

```python
import math
from contextlib import ExitStack

import numpy as np

import concourse.bass as bass
from concourse import mybir

F32 = mybir.dt.float32
F32R = mybir.dt.float32r
BF16 = mybir.dt.bfloat16
F16 = mybir.dt.float16
I32 = mybir.dt.int32
ALU = mybir.AluOpType
ACT = mybir.ActivationFunctionType
AX = mybir.AxisListType

P = 128
B, L, D = 8, 1024, 128
PARTS = ((0, 0), (0, 1), (1, 0))
NT = B * L // P
TB = L // P
FL, FO = 512, 64
SHIFT = 0.05
EPS = 1e-5
NE, CAP, HID = 16, 512, 512
HC = HID // P
SC = CAP // P
ROW = 132
C_MEAN, C_RSTD, C_GATE, C_TOK = 128, 129, 130, 131
NO_TOKEN = 1 << 20
EX = 512
EC = EX // P
CH = 8
NG = D // CH
RING = 4
RW = 768
TW = 640
FREE = 512

V_BIN, V_SFB, V_FBIAS, V_B1, V_B2, V_BZ, V_BH, V_FFN, V_F, V_FB2, V_BO = 0, 3, 6, 7, 11, 15, 19, 23, 87, 93, 109
N_VEC = 110
N_VEC_DMAS = 1 + 3 + 4 + 3 + 6
TWO_PI = 2.0 * math.pi
TURN_PARTS = (6.28125, float(np.float32(TWO_PI - 6.28125)))
ROUNDER = 1.5 * 2.0 ** 23
PI_BELOW = 3.1415925


def constants():
    t = np.linspace(0.0, 1.0, FL).astype(np.float32)
    tr = np.linspace(0.0, FL - 1.0, FL).astype(np.float32)
    w = (np.float32(2.0 * np.pi) * tr / np.float32(FL)).astype(np.float32)
    fw = (np.float32(1e-4) * w).astype(np.float32)
    z = np.stack([t, np.cos(fw), -np.sin(fw)]).astype(np.float32)
    deltas = np.abs(np.linspace(math.log(0.01) / 1.5, math.log(0.01) / 0.3, D).astype(np.float32))
    decay = (np.exp(-t[None, :] * deltas[:, None]) + np.float32(SHIFT)).astype(np.float32)
    e = np.arange(NE, dtype=np.float32)
    slot0 = np.concatenate([CAP * e - 1, CAP * (e + 1) - 1, NE - e])
    return {
        "c_z": np.ascontiguousarray(z[:, ::-1]),
        "c_decay": np.ascontiguousarray(decay[:, ::-1]),
        "c_ident": np.eye(P, dtype=np.float32),
        "c_tri": np.triu(np.ones((P, P), np.float32)),
        "c_slot": np.ascontiguousarray(np.broadcast_to(slot0, (P, 3 * NE)).astype(np.float32)),
    }


class Chain:

    def __init__(self, eng, sem, base=0):
        self.eng, self.sem, self.base, self.n = eng, sem, base, 0

    def step(self, ins):
        self.n += 1
        ins.then_inc(self.sem, 1)

    def wait(self):
        self.eng.wait_ge(self.sem, self.base + self.n)

    def link(self, ins):
        self.step(ins)
        self.wait()


def f32(ap):
    return ap.bitcast(F32)


def reversed_tiles(ap2, n):
    a = ap2.rearrange("p (j m) -> p j m", j=n)
    return bass.AP(tensor=a.tensor, offset=a.offset + P - 1,
                   ap=[list(a.ap[0]), list(a.ap[1]), [-1, P]])


def rsqrt_steps(nc, ch, y, t, v, half_magic=1597463007.0):
    vi, yi = v.bitcast(I32), y.bitcast(I32)
    ch.link(nc.vector.tensor_scalar(yi, vi, 1, None, ALU.logical_shift_right))
    ch.link(nc.vector.tensor_scalar(yi, yi, -1.0, half_magic, ALU.mult, ALU.add))
    for _ in range(3):
        ch.link(nc.vector.tensor_tensor(t, y, y, ALU.mult))
        ch.link(nc.vector.scalar_tensor_tensor(t, t, -0.5, v, ALU.mult, ALU.mult))
        ch.link(nc.vector.scalar_tensor_tensor(y, t, 1.5, y, ALU.add, ALU.mult))


RSQRT_STEPS = 11


def power_of_two_scale(nc, ch, top, p, scale):
    ch.link(nc.vector.tensor_scalar(p, top, 2.0 ** -100, None, ALU.max))
    ch.link(nc.vector.tensor_scalar(p.bitcast(I32), p.bitcast(I32), 0x7F800000, None, ALU.bitwise_and))
    ch.link(nc.vector.tensor_scalar(p, p, 2.0 ** -13, None, ALU.mult))
    ch.link(nc.vector.reciprocal(scale, p))


SCALE_STEPS = 4


def row_stats(nc, ch, x_of, n, st, sm):
    for j in range(n):
        ch.step(nc.vector.bn_stats(st[:, j, :], x_of(j)))
    ch.wait()
    mean, rstd, var, tmp = (sm[:, k, :] for k in range(4))
    ch.step(nc.vector.tensor_tensor(mean, st[:, :, 1], st[:, :, 4], ALU.add))
    ch.step(nc.vector.tensor_tensor(tmp, st[:, :, 1], st[:, :, 4], ALU.subtract))
    ch.link(nc.vector.tensor_tensor(var, st[:, :, 2], st[:, :, 5], ALU.add))
    ch.step(nc.vector.tensor_scalar(mean, mean, 0.5, None, ALU.mult))
    ch.step(nc.vector.tensor_tensor(tmp, tmp, tmp, ALU.mult))
    ch.link(nc.vector.tensor_scalar(var, var, 1.0 / D, EPS, ALU.mult, ALU.add))
    ch.link(nc.vector.scalar_tensor_tensor(var, tmp, 0.25, var, ALU.mult, ALU.add))
    rsqrt_steps(nc, ch, rstd, tmp, var)


TAPS_STEPS = 2
SPLIT_STEPS = 1 + SCALE_STEPS


def row_stats_steps(n):
    return n + 7 + RSQRT_STEPS


class Router:

    def __init__(self, nc, ctx, n, bufs, R, w, slots, tables, pT, pL, pC):
        sb = lambda name, shape, d=F32: ctx.enter_context(nc.sbuf_tensor(f"{name}{n}", shape, d))
        sem = lambda name: ctx.enter_context(nc.semaphore(f"{name}_{n}"))
        self.bufs = bufs
        self.nc, self.n, self.R, self.w, self.slots, self.t = nc, n, R, w, slots, tables
        self.pT = pT
        self.pL = pL[:, 0:n * NE].rearrange("p (j e) -> p j e", e=NE)
        self.pC = pC[:, 128:128 + n * NE]
        self.pD = pC[:, 256:256 + NE]
        self.XN = sb("r_xn", [P, n, D])
        self.XNT = sb("r_xnt", [P, n * P])
        self.st = sb("r_st", [P, n, 6])
        self.sm = sb("r_sm", [P, 8, n])
        self.lg = sb("r_lg", [P, 4, n, NE])
        self.oh = sb("r_oh", [P, n * NE], BF16)
        self.base = sb("r_base", [P, NE])
        self.idx = sb("r_idx", [P, bufs, n], I32)
        self.stats, self.xn, self.xt_ps, self.xt, self.lg_ps, self.small, self.onehot, self.expin, self.exped, \
            self.count_ps, self.done = (sem("r_" + x) for x in (
                "stats", "xn", "xt_ps", "xt", "lg_ps", "small", "onehot", "expin", "exped", "count_ps", "done"))
        self.sent, self.rows_free = sem("r_sent"), sem("r_rows_free")

    STEPS2 = 5
    STEPS3 = 8

    def dve_start(self, dve):
        self.nc.vector.tensor_copy(self.base[:], self.t["slot"][:, 0:NE]).then_inc(self.small, 1)
        dve.wait_ge(self.small, 1)

    def dve_norm(self, dve, r, par):
        nc, n, R = self.nc, self.n, self.R[:, par]
        ch = Chain(dve, self.stats, r * row_stats_steps(n))
        row_stats(nc, ch, lambda j: R[:, j, 0:D], n, self.st, self.sm)
        assert ch.n == row_stats_steps(n)
        for j in range(n):
            nc.vector.tensor_scalar(self.XN[:, j, :], R[:, j, 0:D], self.sm[:, 0, j:j + 1], self.sm[:, 1, j:j + 1],
                                    ALU.subtract, ALU.mult)
        nc.vector.tensor_copy(R[:, :, C_MEAN], self.sm[:, 0, :])
        nc.vector.tensor_copy(R[:, :, C_RSTD], self.sm[:, 1, :])
        nc.vector.tensor_copy(R[:, :, C_TOK].bitcast(I32), self.t["token"][:, bass.ds(r * n, n)]).then_inc(self.xn, 1)

    def pe_transpose(self, pe, r):
        pe.wait_ge(self.xn, r + 1)
        for j in range(self.n):
            last = pe.transpose(self.pT[:, P * j:P * j + P], self.XN[:, j, :], self.t["ident"][:])
        last.then_inc(self.xt_ps, 1)

    def pe_logits(self, pe, r):
        pe.wait_ge(self.xt, r + 1)
        for j in range(self.n):
            last = pe.matmul(self.pL[:, j, :], self.XNT[:, P * j:P * j + P], self.w["gate"][:], start=True, stop=True)
        last.then_inc(self.lg_ps, 1)

    def act_transposed(self, act, r):
        act.wait_ge(self.xt_ps, r + 1)
        act.activation(self.XNT[:], self.pT[:], ACT.Copy).then_inc(self.xt, 1)

    def dve_onehot(self, dve, r):
        nc, n, t = self.nc, self.n, self.t
        wide = lambda ap: ap.unsqueeze(1).broadcast_to([P, n, NE])
        tall = lambda ap: ap.unsqueeze(2).broadcast_to([P, n, NE])
        lg, top, first = self.lg, self.sm[:, 4, :], self.sm[:, 5, :]
        ch = Chain(dve, self.small, 1 + r * (self.STEPS2 + self.STEPS3 + 1))
        dve.wait_ge(self.lg_ps, r + 1)
        ch.link(nc.vector.tensor_tensor(lg[:, 0], self.pL, wide(self.w["gate_b"][:]), ALU.add))
        ch.link(nc.vector.tensor_reduce(top, lg[:, 0], AX.X, ALU.max))
        nc.vector.tensor_tensor(lg[:, 1], lg[:, 0], tall(top), ALU.subtract).then_inc(self.expin, 1)
        ch.link(nc.vector.tensor_tensor(lg[:, 2], lg[:, 0], tall(top), ALU.is_equal))
        ch.link(nc.vector.tensor_tensor(lg[:, 2], lg[:, 2], wide(t["slot"][:, 2 * NE:3 * NE]), ALU.mult))
        ch.link(nc.vector.tensor_reduce(first, lg[:, 2], AX.X, ALU.max))
        assert ch.n == self.STEPS2
        nc.vector.tensor_tensor(self.oh[:].rearrange("p (j e) -> p j e", e=NE), lg[:, 2], tall(first),
                                ALU.is_equal).then_inc(self.onehot, 1)

    def act_tanh(self, act, r):
        act.wait_ge(self.expin, r + 1)
        act.activation(self.lg[:, 1], self.lg[:, 1], ACT.Tanh, scale=0.5).then_inc(self.exped, 1)

    def pe_counts(self, pe, r):
        pe.wait_ge(self.onehot, r + 1)
        n, oh, t = self.n, self.oh, self.t
        for k in range(n):
            pe.matmul(self.pC[:, NE * k:], t["tri16"][:] if k == 0 else t["ones16"][:], oh[:, 0:NE * (n - k)],
                      start=k == 0, stop=k == n - 1)
        for k in range(n):
            last = pe.matmul(self.pD, t["ones16"][:], oh[:, NE * k:NE * k + NE], start=k == 0, stop=k == n - 1)
        last.then_inc(self.count_ps, 1)

    def dve_slots(self, dve, r, par):
        nc, n, t, lg = self.nc, self.n, self.t, self.lg
        wide = lambda ap: ap.unsqueeze(1).broadcast_to([P, n, NE])
        base = 1 + r * (self.STEPS2 + self.STEPS3 + 1) + self.STEPS2
        ch = Chain(dve, self.small, base)
        q, over = lg[:, 2], lg[:, 3]
        dve.wait_ge(self.exped, r + 1)
        dve.wait_ge(self.count_ps, r + 1)
        ch.link(nc.vector.tensor_scalar(q, lg[:, 1], -1.0, 1.0, ALU.mult, ALU.add))
        ch.link(nc.vector.reciprocal(over, q))
        ch.link(nc.vector.scalar_tensor_tensor(over, lg[:, 1], 1.0, over, ALU.add, ALU.mult))
        ch.link(nc.vector.tensor_reduce(self.sm[:, 6, :], over, AX.X, ALU.add))
        nc.vector.reciprocal(self.R[:, par, :, C_GATE], self.sm[:, 6, :])
        ch.link(nc.vector.tensor_tensor(q, self.pC.rearrange("p (j e) -> p j e", e=NE), wide(self.base[:]), ALU.add))
        ch.step(nc.vector.tensor_tensor(self.base[:], self.base[:], self.pD, ALU.add))
        ch.link(nc.vector.tensor_tensor(over, q, wide(t["slot"][:, NE:2 * NE]), ALU.is_gt))
        ch.link(nc.vector.scalar_tensor_tensor(q, over, float(NO_TOKEN), q, ALU.mult, ALU.add))
        assert ch.n == self.STEPS3
        ch.link(nc.vector.tensor_tensor(q, q, self.oh[:].rearrange("p (j e) -> p j e", e=NE), ALU.mult))
        nc.vector.tensor_reduce(self.idx[:, par, :], q, AX.X, ALU.max).then_inc(self.done, 1)

    def pool_start(self, pool):
        limit = pool.alloc_register(f"last_slot{self.n}")
        pool.reg_mov(limit, NE * CAP - 1)
        self.last_slot = pool.snap(limit)
        pool.sem_inc(self.rows_free, self.bufs)

    def pool_send(self, pool, r, par):
        pool.wait_ge(self.done, r + 1)
        pool.nop(nofuse=True)
        for j in range(self.n):
            pool.indirect_dma_start(out=self.slots, out_offset=bass.IndirectOffsetOnAxis(ap=self.idx[:, par, j:j + 1], axis=0),
                                    in_=self.R[:, par, j, :], in_offset=None, bounds_check=self.last_slot,
                                    oob_is_err=False).then_inc(self.sent, 16)

    def pool_release(self, pool, r):
        pool.wait_ge(self.sent, 16 * self.n * (r + 1))
        pool.sem_inc(self.rows_free, 1)


def build_mixer_out(nc, ins, scr, keep):
    X0T, Y, ident, ascale = keep["X0T"], keep["Y"], keep["ident"], keep["ascale"]
    u = ins["L0_attn_a_u"].rearrange("b (j p) d -> b p j d", p=P)
    xout = scr["x1"].rearrange("(b j p) d -> b p j d", p=P, j=TB)
    BUFS = 3
    with ExitStack() as ctx:
        sb = lambda n, s, d=F32: ctx.enter_context(nc.sbuf_tensor(n, s, d))
        sem = lambda n: ctx.enter_context(nc.semaphore(n))
        ps = lambda n, s: ctx.enter_context(nc.psum_tensor(n, s, F32))
        w_out, b_out = sb("w_out", [P, D]), sb("b_out", [P, D])
        U = sb("o_u", [P, BUFS, TB, D])
        R = sb("o_rows", [P, BUFS, TB, ROW])
        YS, ZT = sb("o_ys", [P, TB, D]), sb("o_zt", [P, L])
        pZ, pO, pX, pS, pC = ps("pZ", [P, L]), ps("pO", [P, L]), ps("pX", [P, L]), ps("pS", [P, FREE]), ps("pC", [P, FREE])
        w_landed, ys_ready, z_ps, z_ready, o_ps, ub_ready, rows_ready = (
            sem("o_" + x) for x in ("w_landed", "ys_ready", "z_ps", "z_ready", "o_ps", "ub_ready", "rows_ready"))
        u_landed, stored = ([sem(f"o_{x}{k}") for k in range(BUFS)] for x in ("u_landed", "stored"))
        rt = Router(nc, ctx, TB, BUFS, R, keep["gatew"], scr["slots1"], keep["tables"], pX, pS, pC)
        block = ctx.enter_context(nc.Block())

        def batches(eng, step):
            step(0, 0, 0, True, False)
            with eng.Fori(0, (B - 2) // BUFS) as i:
                for j in range(1, BUFS + 1):
                    step(BUFS * i + j, j % BUFS, i + j // BUFS, False, False)
            step(B - 1, (B - 1) % BUFS, (B - 1) // BUFS, False, True)

        before = lambda k: (k + BUFS - 1) % BUFS
        after = lambda k: (k + 1) % BUFS
        one = lambda ap, b: ap[b] if isinstance(b, int) else ap[bass.ds(b, 1)].rearrange("b p j d -> (b p) j d")

        @block.sync
        def _(sp):
            sp.dma_start(U[:, 0], u[0]).then_inc(u_landed[0], 16)
            sp.dma_start(w_out[:], ins["L0_attn_a_w_out"]).then_inc(w_landed, 16)
            sp.dma_start(b_out[:], row_to_all(ins["L0_attn_a_b_out"], D)).then_inc(w_landed, 16)
            for k in range(BUFS):
                sp.sem_inc(stored[k], 16)

            def step(b, k, n, first, last):
                if not last:
                    sp.dma_start(U[:, after(k)], one(u, b + 1)).then_inc(u_landed[after(k)], 16)
                sp.wait_ge(rows_ready, b + 1)
                sp.dma_start(one(xout, b), R[:, k, :, 0:D]).then_inc(stored[k], 16)

            batches(sp, step)
            for k in range(BUFS):
                sp.wait_ge(stored[k], 16 + 16 * len(range(k, B, BUFS)))

        @block.gpsimd
        def _(pool):
            rt.pool_start(pool)

            def add_bias(b, k, n):
                pool.wait_ge(u_landed[k], 16 * n + 16)
                pool.tensor_tensor(U[:, k], U[:, k], b_out[:].unsqueeze(1).broadcast_to([P, TB, D]), ALU.add).then_inc(ub_ready, 1)

            def step(b, k, n, first, last):
                if not last:
                    add_bias(b + 1, after(k), n + (k == BUFS - 1))
                if not first:
                    rt.pool_send(pool, b - 1, before(k))
                    rt.pool_release(pool, b - 1)

            pool.wait_ge(w_landed, 32)
            add_bias(0, 0, 0)
            batches(pool, step)
            rt.pool_send(pool, B - 1, (B - 1) % BUFS)
            rt.pool_release(pool, B - 1)

        @block.scalar
        def _(act):
            def copy_y(b):
                act.wait_ge(z_ps, b + 1)
                act.activation(YS[:], Y[:].rearrange("p (j b) d -> p j b d", b=B)[:, :, bass.ds(b, 1), :]
                               .rearrange("p j b d -> p j (b d)"), ACT.Copy).then_inc(ys_ready, 1)

            def step(b, k, n, first, last):
                if not last:
                    copy_y(b + 1)
                rt.act_transposed(act, b)
                if not first:
                    rt.act_tanh(act, b - 1)

            copy_y(0)
            batches(act, step)
            rt.act_tanh(act, B - 1)

        @block.tensor
        def _(pe):
            def transpose_y(b):
                pe.wait_ge(ys_ready, b + 1)
                for j in range(TB):
                    last = pe.transpose(pZ[:, P * j:P * j + P], YS[:, j, :], ident[:])
                last.then_inc(z_ps, 1)

            def step(b, k, n, first, last):
                pe.wait_ge(z_ready, b + 1)
                for j in range(TB):
                    mm = pe.matmul(pO[:, P * j:P * j + P], ZT[:, P * j:P * j + P], w_out[:], start=True, stop=True)
                mm.then_inc(o_ps, 1)
                if not last:
                    transpose_y(b + 1)
                if not first:
                    rt.pe_logits(pe, b - 1)
                rt.pe_transpose(pe, b)
                if not first:
                    rt.pe_counts(pe, b - 1)

            pe.wait_ge(w_landed, 32)
            pe.sem_inc(z_ps, 1)
            transpose_y(0)
            batches(pe, step)
            rt.pe_logits(pe, B - 1)
            rt.pe_counts(pe, B - 1)

        @block.vector
        def _(dve):
            rt.dve_start(dve)

            def gate_y(b):
                dve.wait_ge(z_ps, b + 2)
                nc.vector.scalar_tensor_tensor(
                    ZT[:].rearrange("p (j m) -> p j m", j=TB), reversed_tiles(pZ[:], TB), ascale[:, bass.ds(b, 1)],
                    X0T[:, bass.ds(b * L, L)].rearrange("p (j m) -> p j m", j=TB), ALU.mult, ALU.mult
                ).then_inc(z_ready, 1)

            def step(b, k, n, first, last):
                dve.wait_ge(o_ps, b + 1)
                dve.wait_ge(ub_ready, b + 1)
                dve.wait_ge(stored[k], 16 * n + 16)
                dve.wait_ge(rt.rows_free, b + 1)
                nc.vector.tensor_tensor(R[:, k, :, 0:D], pO[:].rearrange("p (j d) -> p j d", j=TB), U[:, k],
                                        ALU.add).then_inc(rows_ready, 1)
                dve.wait_ge(rows_ready, b + 1)
                rt.dve_norm(dve, b, k)
                if not first:
                    rt.dve_onehot(dve, b - 1)
                if not last:
                    gate_y(b + 1)
                if not first:
                    rt.dve_slots(dve, b - 1, before(k))

            gate_y(0)
            batches(dve, step)
            rt.dve_onehot(dve, B - 1)
            rt.dve_slots(dve, B - 1, (B - 1) % BUFS)


def row_to_all(ap, n):
    return bass.AP(tensor=ap.tensor, offset=ap.offset, ap=[[0, P], [1, n]])


def build_mixer(nc, ins, scr, keep):
    u = ins["L0_attn_a_u"].rearrange("b (j p) d -> b p j d", p=P)
    with ExitStack() as ctx:
        sb = lambda n, s, d=F32: ctx.enter_context(nc.sbuf_tensor(n, s, d))
        sem = lambda n: ctx.enter_context(nc.semaphore(n))
        X0T, ident, cols = keep["X0T"], keep["ident"], keep["cols"]
        Y = keep["Y"]
        VT = sb("VT", [P, 2, TB, B, D], F16)
        toep = sb("toep", [P, RING, CH, 2, TW], F16)
        ascale = keep["ascale"]
        toep_landed = [sem(f"toep_landed{r}") for r in range(RING)]
        filt_written = sem("filt_written")

        def load_toeplitz(eng, g, r):
            a = scr["filt"]
            src = bass.AP(tensor=a.tensor, offset=a.offset + g * (CH * 2 * RW), ap=[[1, P], [RW, 2 * CH], [1, TW]])
            eng.dma_start(toep[:, r].rearrange("p c h x -> p (c h) x"), src).then_inc(toep_landed[r], 16)

        with ExitStack() as c1:
            sb1 = lambda n, s, d=F32: c1.enter_context(nc.sbuf_tensor(n, s, d))
            ps1 = lambda n, s: c1.enter_context(nc.psum_tensor(n, s, F32))
            sem1 = lambda n: c1.enter_context(nc.semaphore(n))
            fw1 = sb1("fw1", [3, FO])
            fw23 = sb1("fw23", [FO, 2, FO])
            fwout = sb1("fwout", [FO, D])
            fparts = sb1("fparts", [P, 2, RW], F16)
            fscale = sb1("fscale", [P, 4])
            vscale = sb1("vscale", [P, 4])
            VP = sb1("VP", [P, 2, L], F16)
            X0TMP = sb1("X0TMP", [P, L])
            ident16 = sb1("ident16", [P, P], F16)
            sfw = sb1("sfw", [P, 3, 3])
            U = sb1("U", [P, 2, TB, D])
            XN = sb1("XN", [P, TB, D])
            XNT = sb1("XNT", [P, L])
            spare = Y[:].rearrange("p n d -> p (n d)")
            TAP = spare[:, 0:3 * L].rearrange("p (g l) -> p g l", g=3)
            VV = spare[:, 3 * L:4 * L]
            w_in = spare[:, TB * B * D - 3 * D:TB * B * D]
            UP = spare[:, 4 * L:4 * L + 3 * (L + 2)].rearrange("p (g l) -> p g l", g=3)
            vecs = X0TMP[0:N_VEC, 0:P]
            z = VV[0:3, 0:FL]
            decay = TAP[:, 0, 0:FL]
            fh = TAP[0:FO, 1, :].rearrange("f (n t) -> f n t", n=2)
            fq = TAP[0:FO, 2, :].rearrange("f (n t) -> f n t", n=2)
            frow = XNT[:, 0:RW]
            st = sb1("st", [P, TB, 6])
            sm = sb1("sm", [P, 4, TB])
            pT = ps1("pT", [P, 2 * FREE])
            pV = pT[:].bitcast(F16).rearrange("p (h j d) -> p h j d", h=2, j=TB)
            pP = [ps1(f"pP{g}", [P, 2 * FREE]) for g in range(3)]

            vecs_zeroed, consts_in, filt_in = sem1("vecs_zeroed"), sem1("consts_in"), sem1("filt_in")
            cols_ps, cols_ready, fl_ps, fl_ready = (sem1(n) for n in ("cols_ps", "cols_ready", "fl_ps", "fl_ready"))
            fl_chain, fl_arg, frow_zeroed, frow_ready = (sem1(n) for n in ("fl_chain", "fl_arg", "frow_zeroed", "frow_ready"))
            w_landed = sem1("w_landed")
            u_landed = [sem1("u_landed0"), sem1("u_landed1")]
            xn_ready, xnt_ps, xnt_ready, proj_ps, up_ready = (
                sem1(n) for n in ("xn_ready", "xnt_ps", "xnt_ready", "proj_ps", "up_ready"))
            tap0_ready, tap_done, vv_ready, vt_ps, vt_ready = (
                sem1(n) for n in ("tap0_ready", "tap_done", "vv_ready", "vt_ps", "vt_ready"))
            n_chain, t_chain, s_chain, p_chain = (sem1(n) for n in ("n_chain", "t_chain", "s_chain", "p_chain"))
            x0_done, vhi_ready, vlo_ready, vscale_ready, pads_zeroed = (
                sem1(n) for n in ("x0_done", "vhi_ready", "vlo_ready", "vscale_ready", "pads_zeroed"))
            block = c1.enter_context(nc.Block())
            ORDER = (1, 2, 0)

            @block.sync
            def _(sp):
                sp.wait_ge(vecs_zeroed, 1)
                row = lambda name, r, n: sp.dma_start(
                    vecs[r:r + n, :], ins[name].rearrange("(k p) -> k p", p=P)).then_inc(consts_in, 16)
                sp.dma_start(ident[:], ins["c_ident"]).then_inc(consts_in, 16)
                row("L0_attn_a_b_in", V_BIN, 3)
                row("L0_attn_a_sf_b", V_SFB, 3)
                row("L0_attn_a_filt_bias", V_FBIAS, 1)
                row("L0_attn_b_b1", V_B1, EC)
                row("L0_attn_b_b2", V_B2, EC)
                row("L0_attn_b_bz", V_BZ, EC)
                row("L0_attn_b_bh", V_BH, EC)
                sp.dma_start(vecs[V_FFN:V_FFN + NE * HC, :],
                             ins["L0_ffn_b1"].rearrange("e (k p) -> (e k) p", p=P)).then_inc(consts_in, 16)
                sp.dma_start(vecs[V_FB2:V_FB2 + NE, :], ins["L0_ffn_b2"]).then_inc(consts_in, 16)
                row("L0_attn_b_bo", V_BO, 1)
                for n, name in enumerate(("f_b1", "freq1", "f_b2", "freq2", "f_b3", "freq3")):
                    sp.dma_start(vecs[V_F + n:V_F + n + 1, 0:FO],
                                 ins["L0_attn_a_" + name].rearrange("(a n) -> a n", a=1)).then_inc(consts_in, 16)
                for dst, name in ((z[:], "c_z"), (decay[:], "c_decay"), (fw1[:], "L0_attn_a_f_w1"),
                                  (fw23[:, 0, :], "L0_attn_a_f_w2"), (fw23[:, 1, :], "L0_attn_a_f_w3"),
                                  (fwout[:], "L0_attn_a_f_wout")):
                    sp.dma_start(dst, ins[name]).then_inc(filt_in, 16)
                sp.dma_start(w_in[:], ins["L0_attn_a_w_in"]).then_inc(w_landed, 16)
                sp.dma_start(sfw[:], ins["L0_attn_a_sf_w"].rearrange("(g p) k -> p g k", p=P)).then_inc(w_landed, 16)
                for par in range(2):
                    sp.dma_start(U[:, par], u[par]).then_inc(u_landed[par], 16)
                sp.wait_ge(frow_ready, 1)
                sp.dma_start(scr["filt"], fparts[:]).then_inc(filt_written, 16)
                sp.wait_ge(filt_written, 16)
                for r in range(RING):
                    load_toeplitz(sp, r, r)
                with sp.Fori(1, B // 2) as i:
                    for par in range(2):
                        sp.wait_ge(xn_ready, 4 * i + 2 * par - 2)
                        sp.dma_start(U[:, par], u[bass.ds(2 * i + par, 1)].rearrange("b p j d -> (b p) j d")
                                     ).then_inc(u_landed[par], 16)


            @block.gpsimd
            def _(pool):
                pool.memset(vecs[:], 0.0).then_inc(vecs_zeroed, 1)
                pool.memset(frow[:], 0.0).then_inc(frow_zeroed, 1)
                pool.memset(UP[:, :, 0:2], 0.0).then_inc(pads_zeroed, 1)
                pool.wait_ge(w_landed, 32)
                pool.sem_inc(vv_ready, 1)
                pool.sem_inc(x0_done, 1)
                with pool.Fori(0, B) as b:
                    ch = Chain(pool, p_chain, 3 * b)
                    pool.wait_ge(tap_done, 2 * b + 4)
                    pool.wait_ge(vhi_ready, b + 1)
                    pool.wait_ge(vlo_ready, b + 1)
                    pool.tensor_tensor(VV, TAP[:, 1, :], TAP[:, 2, :], ALU.mult).then_inc(vv_ready, 1)
                    pool.wait_ge(tap0_ready, 3 * b + 3)
                    ch.link(pool.tensor_tensor(X0TMP[:], UP[:, 0, 1:L + 1], sfw[:, 0, 1:2].broadcast_to([P, L]), ALU.mult))
                    ch.link(pool.tensor_tensor(TAP[:, 0, :], TAP[:, 0, :], X0TMP[:], ALU.add))
                    ch.link(pool.tensor_tensor(X0TMP[:], UP[:, 0, 0:L], sfw[:, 0, 0:1].broadcast_to([P, L]), ALU.mult))
                    pool.tensor_tensor(X0T[:, bass.ds(b * L, L)], TAP[:, 0, :], X0TMP[:], ALU.add).then_inc(x0_done, 1)

            @block.tensor
            def _(pe):
                pe.wait_ge(consts_in, 16 * N_VEC_DMAS)
                pe.transpose(pT[:, 0:N_VEC], vecs[:], ident[0:N_VEC, 0:N_VEC]).then_inc(cols_ps, 1)
                pe.wait_ge(filt_in, 16 * 6)
                pe.matmul(pP[0][0:FO, 0:FL], fw1[:], z[:], start=True, stop=True).then_inc(fl_ps, 1)
                for n in range(2):
                    pe.wait_ge(fl_ready, n + 1)
                    pe.matmul(pP[0][0:FO, 0:FL], fw23[:, n, :], fh[:, n % 2, :], start=True, stop=True).then_inc(fl_ps, 1)
                pe.wait_ge(fl_ready, 3)
                pe.matmul(pP[0][:, 0:FL], fwout[:], fh[:, 0, :], start=True, stop=True).then_inc(fl_ps, 1)
                pe.wait_ge(cols_ready, 2)
                pe.wait_ge(frow_ready, 1)
                pe.wait_ge(w_landed, 32)
                pe.sem_inc(vt_ps, 1)
                pe.sem_inc(xnt_ps, 2)
                pe.sem_inc(proj_ps, 3)
                with pe.Fori(0, B) as b:
                    for h in range(2):
                        pe.wait_ge(xn_ready, 2 * b + h + 1)
                        if h == 0:
                            pe.wait_ge(vt_ready, b + 1)
                        for j in range(4 * h, 4 * h + 4):
                            last = pe.transpose(pT[:, P * j:P * j + P], XN[:, j, :], ident[:])
                        last.then_inc(xnt_ps, 1)
                    for n, g in enumerate(ORDER):
                        pe.wait_ge(up_ready, 3 * b + n + 1)
                        for h in range(2):
                            if n == 0:
                                pe.wait_ge(xnt_ready, 2 * b + h + 1)
                            last = pe.matmul(pP[g][:, FREE * h:FREE * h + FREE], w_in[:, g * D:g * D + D],
                                             XNT[:, FREE * h:FREE * h + FREE], start=True, stop=True)
                        last.then_inc(proj_ps, 1)
                    pe.wait_ge(vhi_ready, b + 2)
                    for h in range(2):
                        if h:
                            pe.wait_ge(vlo_ready, b + 2)
                        for j in range(TB):
                            last = pe.transpose(pV[:, h, j, :], VP[:, h, P * j:P * j + P], ident16[:])
                    last.then_inc(vt_ps, 1)

            @block.scalar
            def _(act):
                for n in range(3):
                    act.wait_ge(fl_arg, n + 1)
                    act.activation(fh[:, n % 2, :], fq[:, 0, :], ACT.Sin).then_inc(fl_ready, 1)
                act.wait_ge(cols_ready, 1)
                act.wait_ge(pads_zeroed, 1)
                act.wait_ge(w_landed, 32)
                act.sem_inc(vt_ready, 1)
                act.sem_inc(up_ready, 3)
                act.sem_inc(vhi_ready, 1)
                with act.Fori(0, B) as b:
                    for h in range(2):
                        act.wait_ge(xnt_ps, 2 * b + h + 3)
                        if h == 0:
                            act.wait_ge(proj_ps, 3 * b + 3)
                        act.activation(XNT[:, FREE * h:FREE * h + FREE], pT[:, FREE * h:FREE * h + FREE],
                                       ACT.Copy).then_inc(xnt_ready, 1)
                    for n, g in enumerate(ORDER):
                        act.wait_ge(proj_ps, 3 * b + n + 4)
                        if g:
                            act.wait_ge(tap_done, 2 * b + n + 1)
                        else:
                            act.wait_ge(x0_done, b + 1)
                        act.activation(UP[:, g, 2:L + 2], pP[g][:], ACT.Identity,
                                       bias=cols[:, V_BIN + g:V_BIN + g + 1]).then_inc(up_ready, 1)
                        act.wait_ge(up_ready, 3 * b + n + 4)
                        if n == 0:
                            act.wait_ge(vv_ready, b + 1)
                        act.activation(TAP[:, g, :], UP[:, g, 2:L + 2], ACT.Identity, scale=sfw[:, g, 2:3],
                                       bias=cols[:, V_SFB + g:V_SFB + g + 1]).then_inc(tap0_ready, 1)
                    act.wait_ge(vscale_ready, b + 1)
                    act.wait_ge(vt_ps, b + 1)
                    act.activation(VP[:, 0, :], VV, ACT.Copy, scale=vscale[:, 2:3]).then_inc(vhi_ready, 1)
                    act.wait_ge(vt_ps, b + 2)
                    act.activation(VT[:, :, :, bass.ds(b, 1), :].rearrange("p h j b d -> p (h j) (b d)"),
                                   pV.rearrange("p h j d -> p (h j) d"), ACT.Copy).then_inc(vt_ready, 1)

            @block.vector
            def _(dve):
                dve.wait_ge(cols_ps, 1)
                nc.vector.tensor_copy(cols[:], pT[:, 0:N_VEC]).then_inc(cols_ready, 1)
                dve.wait_ge(cols_ready, 1)
                nc.vector.tensor_copy(ident16[:], ident[:]).then_inc(cols_ready, 1)
                ch = Chain(dve, fl_chain)
                for n in range(3):
                    fb = cols[0:FO, V_F + 2 * n:V_F + 2 * n + 1]
                    fr = cols[0:FO, V_F + 2 * n + 1:V_F + 2 * n + 2]
                    dve.wait_ge(fl_ps, n + 1)
                    if n:
                        dve.wait_ge(fl_ready, n)
                    ch.link(nc.vector.tensor_scalar(fq[:, 0, :], pP[0][0:FO, 0:FL], fb, fr, ALU.add, ALU.mult))
                    ch.link(nc.vector.tensor_scalar(fq[:, 1, :], fq[:, 0, :], 1.0 / TWO_PI, ROUNDER, ALU.mult, ALU.add))
                    ch.link(nc.vector.tensor_scalar(fq[:, 1, :], fq[:, 1, :], ROUNDER, None, ALU.subtract))
                    for c in TURN_PARTS:
                        ch.link(nc.vector.scalar_tensor_tensor(fq[:, 0, :], fq[:, 1, :], -c, fq[:, 0, :], ALU.mult, ALU.add))
                    nc.vector.tensor_scalar(fq[:, 0, :], fq[:, 0, :], PI_BELOW, -PI_BELOW, ALU.min, ALU.max).then_inc(fl_arg, 1)
                dve.wait_ge(fl_ps, 4)
                dve.wait_ge(frow_zeroed, 1)
                ch.link(nc.vector.tensor_tensor(frow[:, P:P + FL], pP[0][:, 0:FL], decay[:], ALU.mult))
                ch.link(nc.vector.tensor_tensor(frow[:, P + FL - 1:P + FL], frow[:, P + FL - 1:P + FL],
                                                cols[:, V_FBIAS:V_FBIAS + 1], ALU.add))
                ch.link(nc.vector.tensor_reduce(fscale[:, 0:1], frow[:, P:P + FL], AX.X, ALU.max, apply_absolute_value=True))
                power_of_two_scale(nc, ch, fscale[:, 0:1], fscale[:, 1:2], fscale[:, 2:3])
                ch.link(nc.vector.tensor_scalar(fparts[:, 0, :], frow[:], fscale[:, 2:3], None, ALU.mult))
                nc.vector.scalar_tensor_tensor(fparts[:, 1, :], frow[:], fscale[:, 2:3], fparts[:, 0, :],
                                               ALU.mult, ALU.subtract).then_inc(frow_ready, 1)
                dve.wait_ge(w_landed, 32)
                dve.sem_inc(tap_done, 2)
                dve.sem_inc(vlo_ready, 1)

                def norm(b, par, landed):
                    ch = Chain(dve, n_chain, b * row_stats_steps(TB))
                    dve.wait_ge(u_landed[par], landed)
                    row_stats(nc, ch, lambda j: U[:, par, j, :], TB, st, sm)
                    assert ch.n == row_stats_steps(TB)
                    dve.wait_ge(xnt_ps, 2 * b + 2)
                    for j in range(TB):
                        last = nc.vector.tensor_scalar(XN[:, j, :], U[:, par, j, :], sm[:, 0, j:j + 1], sm[:, 1, j:j + 1],
                                                       ALU.subtract, ALU.mult)
                        if j % 4 == 3:
                            last.then_inc(xn_ready, 1)

                def taps(b):
                    ch = Chain(dve, t_chain, b * TAPS_STEPS)
                    for n, g in enumerate(ORDER[:2]):
                        dve.wait_ge(tap0_ready, 3 * b + n + 1)
                        ch.link(nc.vector.scalar_tensor_tensor(TAP[:, g, :], UP[:, g, 1:L + 1], sfw[:, g, 1:2],
                                                               TAP[:, g, :], ALU.mult, ALU.add))
                        nc.vector.scalar_tensor_tensor(TAP[:, g, :], UP[:, g, 0:L], sfw[:, g, 0:1],
                                                       TAP[:, g, :], ALU.mult, ALU.add).then_inc(tap_done, 1)

                def split(b):
                    ch = Chain(dve, s_chain, b * SPLIT_STEPS)
                    dve.wait_ge(vv_ready, b + 2)
                    ch.link(nc.vector.tensor_reduce(vscale[:, 0:1], VV, AX.X, ALU.max, apply_absolute_value=True))
                    dve.wait_ge(vhi_ready, b + 1)
                    power_of_two_scale(nc, ch, vscale[:, 0:1], vscale[:, 1:2], vscale[:, 2:3])
                    nc.vector.tensor_tensor(ascale[:, bass.ds(b, 1)], vscale[:, 1:2], fscale[:, 1:2], ALU.mult).then_inc(vscale_ready, 1)
                    dve.wait_ge(vhi_ready, b + 2)
                    nc.vector.scalar_tensor_tensor(VP[:, 1, :], VV, vscale[:, 2:3], VP[:, 0, :],
                                                   ALU.mult, ALU.subtract).then_inc(vlo_ready, 1)

                norm(0, 0, 16)
                with dve.Fori(0, B // 2 - 1) as i:
                    for par in range(2):
                        norm(2 * i + par + 1, 1 - par, 16 * i + 16 * (1 + par))
                        taps(2 * i + par)
                        split(2 * i + par)
                norm(B - 1, 1, 16 * (B // 2))
                for b in (B - 2, B - 1):
                    taps(b)
                    split(b)

        with ExitStack() as c2:
            sem2 = lambda n: c2.enter_context(nc.semaphore(n))
            VG = c2.enter_context(nc.sbuf_tensor("VG", [P, RING, 2, CH, TB * B], F16))
            pY = [c2.enter_context(nc.psum_tensor(f"pY{r}", [P, CH, TB * B], F32)) for r in range(RING)]
            vg_ready, conv_done, y_ready = sem2("vg_ready"), sem2("conv_done"), sem2("y_ready")
            block = c2.enter_context(nc.Block())

            @block.sync
            def _(sp):
                with sp.Fori(1, NG // RING) as i:
                    for r in range(RING):
                        sp.wait_ge(conv_done, RING * (i - 1) + r + 1 + RING)
                        load_toeplitz(sp, RING * i + r, r)

            @block.vector
            def _(dve):
                dve.sem_inc(vg_ready, 1)
                with dve.Fori(0, NG // RING) as i:
                    for r in range(RING):
                        dve.wait_ge(conv_done, RING * i + r + 1)
                        for h in range(2):
                            last = nc.vector.tensor_copy(
                                VG[:, r, h], VT[:, h, :, :, bass.ds((RING * i + r) * CH, CH)].rearrange("p j b c -> p c (j b)"))
                        last.then_inc(vg_ready, 1)

            @block.tensor
            def _(pe):
                pe.sem_inc(conv_done, RING)
                with pe.Fori(0, NG // RING) as i:
                    for r in range(RING):
                        pe.wait_ge(toep_landed[r], 16 * i + 16)
                        pe.wait_ge(vg_ready, RING * i + r + 2)
                        pe.wait_ge(y_ready, RING * i + r + 1)
                        for c in range(CH):
                            for d in range(TB // 2 + 1):
                                for k, v in PARTS:
                                    last = pe.matmul(pY[r][:, c, B * d:], toep[:, r, c, k, FL - P * d:FL - P * d + P],
                                                     VG[:, r, v, c, 0:B * (TB - d)],
                                                     start=d == 0 and (k, v) == PARTS[0],
                                                     stop=d == TB // 2 and (k, v) == PARTS[-1])
                        last.then_inc(conv_done, 1)

            @block.scalar
            def _(act):
                act.sem_inc(y_ready, RING)
                with act.Fori(0, NG // RING) as i:
                    for r in range(RING):
                        act.wait_ge(conv_done, RING * i + r + 1 + RING)
                        act.activation(Y[:, :, bass.ds((RING * i + r) * CH, CH)],
                                       pY[r][:].rearrange("p c n -> p n c"), ACT.Copy).then_inc(y_ready, 1)


def build_experts(nc, ins, slots, out, keep, tag):
    ident, cols = keep["ident"], keep["cols"]
    w1, w2 = ins["L0_ffn_W1"], ins["L0_ffn_W2"].rearrange("e (k p) d -> e p k d", p=P)
    with ExitStack() as ctx:
        sb = lambda n, s, d=F32: ctx.enter_context(nc.sbuf_tensor(tag + n, s, d))
        sem = lambda n: ctx.enter_context(nc.semaphore(tag + n))
        ps = lambda n: ctx.enter_context(nc.psum_tensor(tag + n, [P, FREE], F32))
        G = sb("rows", [P, NE, SC, ROW])
        W1, W2 = sb("w1", [P, 2, HID]), sb("w2", [P, 2, HC, D])
        XN, XT, HT, YT, O = sb("xn", [P, SC, D]), sb("xt", [P, CAP]), sb("ht", [P, HC, CAP]), sb("yt", [P, CAP]), sb("o", [P, 2, SC, D])
        token = sb("token", [P, 2, SC], I32)
        pX, pH, pY, pO = ps("pX"), [ps("pH0"), ps("pH1")], ps("pY"), ps("pO")
        first_rows, other_rows, xn_ready, xt_ps, xt_ready, h_ps, h_ready, y_ps, y_ready, o_ps, o_ready = (
            sem(x) for x in ("first_rows", "other_rows", "xn_ready", "xt_ps", "xt_ready", "h_ps", "h_ready",
                             "y_ps", "y_ready", "o_ps", "o_ready"))
        w1_landed, w2_landed = ([sem(x + "0"), sem(x + "1")] for x in ("w1_", "w2_"))
        sent, rows_free = sem("sent"), sem("rows_free")
        block = ctx.enter_context(nc.Block())
        rows = slots.rearrange("(e p j) d -> p e j d", e=NE, j=SC)

        @block.sync
        def _(sp):
            sp.dma_start(G[:, 0:2], rows[:, 0:2]).then_inc(first_rows, 16)
            for par in range(2):
                sp.dma_start(W1[:, par], w1[par]).then_inc(w1_landed[par], 16)
                sp.dma_start(W2[:, par], w2[par]).then_inc(w2_landed[par], 16)
            sp.dma_start(G[:, 2:NE], rows[:, 2:NE]).then_inc(other_rows, 16)
            with sp.Fori(1, NE // 2) as i:
                for par in range(2):
                    e = 2 * i + par
                    sp.wait_ge(h_ps, HC * (e - 1))
                    sp.dma_start(W1[:, par], w1[bass.ds(e, 1)].rearrange("e p n -> (e p) n")).then_inc(w1_landed[par], 16)
                    sp.wait_ge(y_ps, e - 1)
                    sp.dma_start(W2[:, par], w2[bass.ds(e, 1)].rearrange("e p k d -> (e p) k d")).then_inc(w2_landed[par], 16)

        @block.gpsimd
        def _(pool):
            limit = pool.alloc_register(tag + "last_token")
            pool.reg_mov(limit, B * L - 1)
            last_token = pool.snap(limit)
            pool.sem_inc(rows_free, 2)
            with pool.Fori(0, NE // 2) as i:
                for par in range(2):
                    e = 2 * i + par
                    pool.wait_ge(o_ready, e + 2)
                    pool.nop(nofuse=True)
                    for j in range(SC):
                        pool.indirect_dma_start(
                            out=out, out_offset=bass.IndirectOffsetOnAxis(
                                ap=token[:, par, j:j + 1], axis=0),
                            in_=O[:, par, j, :], in_offset=None, bounds_check=last_token, oob_is_err=False
                        ).then_inc(sent, 16)
                    pool.wait_ge(sent, 16 * SC * (e + 1))
                    pool.sem_inc(rows_free, 1)

        def expert_loop(eng, step):
            with eng.Fori(0, NE // 2 - 1) as i:
                step(2 * i + 1, 1)
                step(2 * i + 2, 0)
            step(NE - 1, 1)

        @block.tensor
        def _(pe):
            def transpose_rows(e):
                pe.wait_ge(xn_ready, e + 1)
                pe.wait_ge(xt_ready, e + 1)
                for j in range(SC):
                    last = pe.transpose(pX[:, P * j:P * j + P], XN[:, j, :], ident[:])
                last.then_inc(xt_ps, 1)

            def hidden(e, par, landed):
                pe.wait_ge(xt_ready, e + 2)
                pe.wait_ge(w1_landed[par], landed)
                for k in range(HC):
                    pe.wait_ge(h_ready, HC * e + k + HC - 1)
                    pe.matmul(pH[k % 2][:], W1[:, par, P * k:P * k + P], XT[:], start=True, stop=True).then_inc(h_ps, 1)

            def outer(e, par, landed):
                pe.wait_ge(w2_landed[par], landed)
                for k in range(HC):
                    pe.wait_ge(h_ready, HC * e + k + 1 + HC)
                    last = pe.matmul(pY[:], W2[:, par, k, :], HT[:, k, :], start=k == 0, stop=k == HC - 1)
                last.then_inc(y_ps, 1)

            def transpose_out(e):
                pe.wait_ge(y_ready, e + 1)
                pe.wait_ge(o_ready, e + 1)
                for j in range(SC):
                    last = pe.transpose(pO[:, P * j:P * j + P], YT[:, P * j:P * j + P], ident[:])
                last.then_inc(o_ps, 1)

            transpose_rows(0)
            hidden(0, 0, 16)

            def step(e, par):
                transpose_rows(e)
                outer(e - 1, 1 - par, landed(e - 1, 1 - par))
                hidden(e, par, landed(e, par))
                transpose_out(e - 1)

            def landed(e, par):
                return (e - par) * 8 + 16

            expert_loop(pe, step)
            outer(NE - 1, 1, landed(NE - 1, 1))
            transpose_out(NE - 1)

        @block.scalar
        def _(act):
            act.sem_inc(xt_ready, 1)
            act.sem_inc(h_ready, HC)

            def columns(e):
                act.wait_ge(xt_ps, e + 1)
                act.activation(XT[:], pX[:], ACT.Copy).then_inc(xt_ready, 1)

            def relus(e):
                for k in range(HC):
                    act.wait_ge(h_ps, HC * e + k + 1)
                    act.activation(HT[:, k, :], pH[k % 2][:], ACT.Relu,
                                   bias=cols[:, bass.ds(V_FFN + e * HC + k, 1)]).then_inc(h_ready, 1)

            def outs(e):
                act.wait_ge(y_ps, e + 1)
                act.activation(YT[:], pY[:], ACT.Identity, bias=cols[:, bass.ds(V_FB2 + e, 1)]).then_inc(y_ready, 1)

            columns(0)
            relus(0)

            def step(e, par):
                columns(e)
                outs(e - 1)
                relus(e)

            expert_loop(act, step)
            outs(NE - 1)

        @block.vector
        def _(dve):
            Ge = G[:].rearrange("p e j d -> p (e j) d")

            def norm(e):
                for j in range(SC):
                    g = Ge[:, bass.ds(e * SC + j, 1), :].rearrange("p a d -> p (a d)")
                    last = nc.vector.tensor_scalar(XN[:, j, :], g[:, 0:D], g[:, C_MEAN:C_MEAN + 1], g[:, C_RSTD:C_RSTD + 1],
                                                   ALU.subtract, ALU.mult)
                last.then_inc(xn_ready, 1)

            dve.sem_inc(o_ready, 1)

            def add(e, par):
                dve.wait_ge(o_ps, e + 1)
                dve.wait_ge(rows_free, e + 1)
                nc.vector.tensor_copy(token[:, par, :], Ge[:, bass.ds(e * SC, SC), C_TOK].bitcast(I32))
                for j in range(SC):
                    g = Ge[:, bass.ds(e * SC + j, 1), :].rearrange("p a d -> p (a d)")
                    last = nc.vector.scalar_tensor_tensor(O[:, par, j, :], pO[:, P * j:P * j + P], g[:, C_GATE:C_GATE + 1],
                                                          g[:, 0:D], ALU.mult, ALU.add)
                last.then_inc(o_ready, 1)

            dve.wait_ge(first_rows, 16)
            norm(0)
            dve.wait_ge(xt_ps, 1)
            norm(1)
            dve.wait_ge(other_rows, 16)

            def step(e, par):
                if not (isinstance(e, int) and e == NE - 1):
                    dve.wait_ge(xt_ps, e + 1)
                    norm(e + 1)
                add(e - 1, 1 - par)

            expert_loop(dve, step)
            add(NE - 1, 1)


def build(nc, ins, out):
    x1 = nc.dram_tensor("x1", (B * L, D), F32).ap()
    scr = {"filt": nc.dram_tensor("filt_rows", (P, 2, RW), F16).ap(), "x1": x1,
           "slots1": nc.dram_tensor("slots1", (NE * CAP, ROW), F32).ap(),
           "slots2": nc.dram_tensor("slots2", (NE * CAP, ROW), F32).ap()}
    with ExitStack() as ctx:
        sb = lambda n, s, d=F32: ctx.enter_context(nc.sbuf_tensor(n, s, d))
        ident, cols = sb("ident", [P, P]), sb("cols", [P, N_VEC])
        tables = {"ident": ident, "slot": sb("t_slot", [P, 3 * NE]), "token": sb("t_token", [P, NT], I32),
                  "tri16": sb("t_tri", [P, P], BF16), "ones16": sb("t_ones", [P, P], BF16)}
        gatew = {"gate": sb("gate_w", [P, NE]), "gate_b": sb("gate_b", [P, NE])}
        keep = {"ident": ident, "cols": cols, "tables": tables, "gatew": gatew}
        build_tables(nc, ins, scr, keep)
        with ExitStack() as c1:
            keep["ascale"] = c1.enter_context(nc.sbuf_tensor("ascale", [P, B], F32))
            keep["X0T"] = c1.enter_context(nc.sbuf_tensor("X0T", [P, B * L], F32))
            keep["Y"] = c1.enter_context(nc.sbuf_tensor("Y", [P, TB * B, D], F32))
            build_mixer(nc, ins, scr, keep)
            build_mixer_out(nc, ins, scr, keep)
        build_experts(nc, ins, scr["slots1"], x1, keep, "e1_")
        build_recurrent(nc, ins, x1, out, scr["slots2"], keep)
        build_experts(nc, ins, scr["slots2"], out, keep, "e2_")


def build_tables(nc, ins, scr, keep):
    t, g = keep["tables"], keep["gatew"]
    with ExitStack() as ctx:
        tri = ctx.enter_context(nc.sbuf_tensor("tri", [P, P], F32))
        empty = ctx.enter_context(nc.sbuf_tensor("empty", [P, ROW], F32))
        landed, zeroed, marked, cleared, made = (ctx.enter_context(nc.semaphore("tb_" + n)) for n in (
            "landed", "zeroed", "marked", "cleared", "made"))
        block = ctx.enter_context(nc.Block())

        @block.sync
        def _(sp):
            sp.dma_start(tri[:], ins["c_tri"]).then_inc(landed, 16)
            sp.dma_start(t["slot"][:], ins["c_slot"]).then_inc(landed, 16)
            sp.dma_start(g["gate"][:], ins["L0_ffn_Wg"]).then_inc(landed, 16)
            sp.dma_start(g["gate_b"][:], row_to_all(ins["L0_ffn_bg"], NE)).then_inc(landed, 16)
            sp.wait_ge(marked, 1)
            for n in ("slots1", "slots2"):
                sp.dma_start(scr[n].rearrange("(p q) d -> p q d", p=P),
                             empty[:].unsqueeze(1).broadcast_to([P, NE * CAP // P, ROW])).then_inc(cleared, 16)
            sp.wait_ge(cleared, 32)

        @block.gpsimd
        def _(pool):
            pool.memset(empty[:], 0.0).then_inc(zeroed, 1)
            pool.memset(t["ones16"][:], 1.0)
            pool.iota(t["token"][:], pattern=[[P, NT]], base=0, channel_multiplier=1)
            pool.wait_ge(zeroed, 1)
            pool.iota(empty[:, C_TOK:C_TOK + 1].bitcast(I32), pattern=[[0, 1]], base=NO_TOKEN, channel_multiplier=0
                      ).then_inc(marked, 1)

        @block.vector
        def _(dve):
            dve.wait_ge(landed, 64)
            nc.vector.tensor_copy(t["tri16"][:], tri[:]).then_inc(made, 1)
            dve.wait_ge(made, 1)


def build_recurrent(nc, ins, x, out, slots, keep):
    ident, cols = keep["ident"], keep["cols"]
    CT = 4
    CW = CT * P
    NC = B * L // CW
    xin = x.rearrange("(c j p) d -> c p j d", p=P, j=CT)
    xout = out.rearrange("(c j p) d -> c p j d", p=P, j=CT)
    with ExitStack() as ctx:
        sb = lambda n, s, d=F32: ctx.enter_context(nc.sbuf_tensor("b_" + n, s, d))
        sem = lambda n: ctx.enter_context(nc.semaphore("b_" + n))
        ps = lambda n: ctx.enter_context(nc.psum_tensor("b_" + n, [P, FREE], F32))
        parts = lambda n, s: (sb(n + "h", s, F32R), sb(n + "l", s, F32R))
        W1, W2, WZ, WH, WO = parts("w1", [P, EX]), parts("w2", [P, EX]), parts("wz", [P, EC, EX]), parts("wh", [P, EC, EX]), parts("wo", [P, EC, D])
        XB, XN = sb("xb", [P, 2, CT, D]), sb("xn", [P, CT, D])
        XT, XI, S = parts("xt", [P, 2, CW]), parts("xi", [P, 2, EC, CW]), parts("s", [P, EC, CW])
        XF, SF, YT = sb("xf", [P, EC, CW]), sb("sf", [P, EC, CW]), sb("yt", [P, CW])
        SK, H = sb("sk", [P, 2, EC, CW]), sb("h", [P, 2, EC, CW])
        Z, A, BB = sb("z", [P, EC, CW]), sb("a", [P, EC, CW]), sb("bb", [P, EC, CW])
        R = sb("rows", [P, 2, CT, ROW])
        bz2 = sb("bz2", [P, EC])
        st, sm = sb("st", [P, CT, 6]), sb("sm", [P, 4, CT])
        pX, pU, pZ, pH, pY, pO, pS = ps("pX"), [ps("pU0"), ps("pU1")], ps("pZ"), ps("pH"), ps("pY"), ps("pO"), ps("pS")
        (w_landed, w_high, w_low, xn_ready, xt_ps, xth, xtl, up_ps, up_read, xih, xil, z_ps, z_read, a_ready, h_ps,
         b_done, scan_done, s_done, sh, sl, sum_read, y_ps, y_ready, o_ps, rows_ready, chain) = (sem(n) for n in (
             "w_landed w_high w_low xn_ready xt_ps xth xtl up_ps up_read xih xil z_ps z_read a_ready h_ps "
             "b_done scan_done s_done sh sl sum_read y_ps y_ready o_ps rows_ready chain").split())
        x_landed, r_landed, stored = ([sem(n + "0"), sem(n + "1")] for n in ("x_landed", "r_landed", "stored"))
        rt = Router(nc, ctx, CT, 2, R, keep["gatew"], slots, keep["tables"], pX, pS, pS)
        block = ctx.enter_context(nc.Block())
        raw = ((W1, BB[:, 0, :]), (W2, BB[:, 1, :]), (WO, BB[:, 2, :].rearrange("p (k d) -> p k d", k=EC)), (WZ, Z[:]), (WH, A[:]))
        N_RAW, N_UP = len(raw), 2

        def chunks(eng, step):
            step(0, 0)
            step(1, 1)
            with eng.Fori(1, NC // 2 - 1) as i:
                step(2 * i, 0)
                step(2 * i + 1, 1)
            step(NC - 2, 0)
            step(NC - 1, 1)

        def exists(c):
            return not isinstance(c, int) or 0 <= c < NC

        turn = lambda c, par: (c - par) * 8
        one = lambda ap, c: ap[c] if isinstance(c, int) else ap[bass.ds(c, 1)].rearrange("c p j d -> (c p) j d")

        @block.sync
        def _(sp):
            for par in range(2):
                sp.dma_start(XB[:, par], xin[par]).then_inc(x_landed[par], 16)
            for (w, dst), n in zip(raw, ("W1", "W2", "Wo", "Wz", "Wh")):
                src = ins["L0_attn_b_" + n]
                sp.dma_start(dst, src if n in ("W1", "W2") else src.rearrange("(k p) n -> p k n", p=P)).then_inc(w_landed, 16)
            for par in range(2):
                sp.dma_start(R[:, par, :, 0:D], xin[par]).then_inc(r_landed[par], 16)

            def store(c, par):
                sp.wait_ge(rows_ready, c + 1)
                sp.dma_start(one(xout, c), R[:, par, :, 0:D]).then_inc(stored[par], 16)

            def step(c, par):
                if exists(c + 2):
                    sp.wait_ge(xn_ready, c + 1)
                    sp.dma_start(XB[:, par], one(xin, c + 2)).then_inc(x_landed[par], 16)
                if exists(c - 2):
                    store(c - 2, par)
                    sp.wait_ge(stored[par], turn(c, par))
                    sp.wait_ge(rt.rows_free, c + 1)
                    sp.dma_start(R[:, par, :, 0:D], one(xin, c)).then_inc(r_landed[par], 16)

            chunks(sp, step)
            for par in range(2):
                store(NC - 2 + par, par)
            for par in range(2):
                sp.wait_ge(stored[par], 16 * (NC // 2))

        @block.gpsimd
        def _(pool):
            rt.pool_start(pool)

            def step(c, par):
                for m in range(EC):
                    pool.wait_ge(scan_done, EC * c + m + 1 + EC)
                    pool.tensor_tensor(SF[:, m, :], H[:, par, m, :], SK[:, par, m, :], ALU.add).then_inc(s_done, 1)
                    if m == 1 and exists(c - 2):
                        rt.pool_send(pool, c - 2, par)
                        rt.pool_release(pool, c - 2)

            chunks(pool, step)
            for par in range(2):
                rt.pool_send(pool, NC - 2 + par, par)
                rt.pool_release(pool, NC - 2 + par)

        @block.tensor
        def _(pe):
            def product(dst, w, x, start, stop):
                for n, (i, j) in enumerate(PARTS):
                    last = pe.matmul(dst, w[i], x[j], start=start and n == 0, stop=stop and n == len(PARTS) - 1)
                return last

            def transpose_in(c):
                pe.wait_ge(xn_ready, c + 1)
                for j in range(CT):
                    last = pe.transpose(pX[:, P * j:P * j + P], XN[:, j, :], ident[:])
                last.then_inc(xt_ps, 1)

            def up(c, par, m, q):
                if m == 0 and q == 0:
                    pe.wait_ge(xth, c + 1)
                    pe.wait_ge(xtl, c + 1)
                pe.wait_ge(up_read, 2 * EC * c + 2 * m + q + 1)
                W = (W1, W2)[q]
                product(pU[q][:], [w[:, P * m:P * m + P] for w in W], [x[:, par, :] for x in XT], True, True).then_inc(up_ps, 1)

            def gate_block(c, par, m, W, dst, done):
                for k in range(EC):
                    if m == 0 and W is WZ:
                        pe.wait_ge(xih, EC * c + k + 1)
                        pe.wait_ge(xil, EC * c + k + 1)
                    last = product(dst[:], [w[:, k, P * m:P * m + P] for w in W], [x[:, par, k, :] for x in XI],
                                   k == 0, k == EC - 1)
                last.then_inc(done, 1)

            def down(c, ks):
                for k in ks:
                    pe.wait_ge(sh, EC * c + k + 1)
                    pe.wait_ge(sl, EC * c + k + 1)
                    done = product(pY[:], [w[:, k, :] for w in WO], [x[:, k, :] for x in S], k == 0, k == EC - 1)
                done.then_inc(y_ps if k == EC - 1 else sum_read, 1)

            def transpose_out(c):
                pe.wait_ge(y_ready, c + 1)
                if exists(c - 1):
                    pe.wait_ge(rows_ready, c)
                for j in range(CT):
                    done = pe.transpose(pO[:, P * j:P * j + P], YT[:, P * j:P * j + P], ident[:])
                done.then_inc(o_ps, 1)

            def step(c, par):
                for m in range(EC):
                    pe.wait_ge(z_read, EC * c + m + 1)
                    gate_block(c, par, m, WZ, pZ, z_ps)
                    if exists(c - 1):
                        if m == 0:
                            down(c - 1, range(EC - 1))
                        elif m == 1:
                            down(c - 1, [EC - 1])
                        elif m == 3:
                            rt.pe_transpose(pe, c - 1)
                    if m == 1 and exists(c - 2):
                        rt.pe_counts(pe, c - 2)
                    if exists(c + 1):
                        up(c + 1, 1 - par, m, 0)
                    pe.wait_ge(b_done, EC * c + m + 1)
                    gate_block(c, par, m, WH, pH, h_ps)
                    if exists(c - 1):
                        if m == 1:
                            transpose_out(c - 1)
                        elif m == 3:
                            rt.pe_logits(pe, c - 1)
                    if exists(c + 1):
                        up(c + 1, 1 - par, m, 1)
                if exists(c + 2):
                    transpose_in(c + 2)

            pe.sem_inc(xt_ps, 1)
            transpose_in(0)
            pe.wait_ge(w_high, N_UP)
            pe.wait_ge(w_low, N_UP)
            for m in range(EC):
                for q in range(2):
                    up(0, 0, m, q)
            transpose_in(1)
            pe.wait_ge(w_high, N_RAW)
            pe.wait_ge(w_low, N_RAW)
            chunks(pe, step)
            down(NC - 1, range(EC - 1))
            down(NC - 1, [EC - 1])
            rt.pe_counts(pe, NC - 2)
            transpose_out(NC - 1)
            rt.pe_transpose(pe, NC - 1)
            rt.pe_logits(pe, NC - 1)
            rt.pe_counts(pe, NC - 1)

        @block.scalar
        def _(act):
            act.sem_inc(up_read, 2)
            act.sem_inc(z_read, 1)

            def high_weights(first, last):
                for n in range(first, last):
                    act.wait_ge(w_landed, 16 * N_RAW)
                    act.activation(raw[n][0][0][:], raw[n][1], ACT.Copy).then_inc(w_high, 1)

            def high_in(c, par):
                act.wait_ge(xt_ps, c + 2)
                act.activation(XT[0][:, par, :], pX[:], ACT.Copy).then_inc(xth, 1)

            def silu(c, par, m, q):
                act.wait_ge(up_ps, 2 * EC * c + 2 * m + q + 1)
                dst = SK[:, par, m, :] if q else XF[:, m, :]
                bias = (V_B1, V_B2)[q] + m
                act.activation(dst, pU[q][:], ACT.Silu, bias=cols[:, bias:bias + 1]).then_inc(up_read, 1)
                if q == 0:
                    act.wait_ge(up_read, 2 * EC * c + 2 * m + 3)
                    act.activation(XI[0][:, par, m, :], XF[:, m, :], ACT.Copy).then_inc(xih, 1)

            def high_sum(c, m):
                act.wait_ge(s_done, EC * c + m + 1)
                act.activation(S[0][:, m, :], SF[:, m, :], ACT.Copy).then_inc(sh, 1)

            def output(c):
                act.wait_ge(y_ps, c + 1)
                act.activation(YT[:], pY[:], ACT.Identity, bias=cols[:, V_BO:V_BO + 1]).then_inc(y_ready, 1)

            def step(c, par):
                for m in range(EC):
                    act.wait_ge(z_ps, EC * c + m + 1)
                    act.wait_ge(scan_done, EC * c + m + 1)
                    act.activation(Z[:, m, :], pZ[:], ACT.Tanh, scale=0.5, bias=bz2[:, m:m + 1]).then_inc(z_read, 1)
                    act.wait_ge(z_read, EC * c + m + 2)
                    act.activation(A[:, m, :], Z[:, m, :], ACT.Copy, scale=-0.5, bias=0.5)
                    act.activation(Z[:, m, :], Z[:, m, :], ACT.Copy, scale=0.5, bias=0.5).then_inc(a_ready, 1)
                    if m:
                        if m == 1 and exists(c - 1):
                            act.wait_ge(sum_read, c)
                        high_sum(c, m - 1)
                    elif exists(c - 1):
                        high_sum(c - 1, EC - 1)
                    if m == 1 and exists(c - 1):
                        output(c - 1)
                    if exists(c + 1):
                        silu(c + 1, 1 - par, m, 0)
                    if m == 0 and exists(c - 2):
                        rt.act_tanh(act, c - 2)
                    if m == 3 and exists(c - 1):
                        rt.act_transposed(act, c - 1)
                    if exists(c + 1):
                        silu(c + 1, 1 - par, m, 1)
                if exists(c + 2):
                    high_in(c + 2, par)

            high_weights(0, N_UP)
            high_in(0, 0)
            for m in range(EC):
                for q in range(2):
                    silu(0, 0, m, q)
            high_in(1, 1)
            high_weights(N_UP, N_RAW)
            chunks(act, step)
            high_sum(NC - 1, EC - 1)
            rt.act_tanh(act, NC - 2)
            output(NC - 1)
            rt.act_transposed(act, NC - 1)
            rt.act_tanh(act, NC - 1)

        @block.vector
        def _(dve):
            nc.vector.tensor_scalar(bz2[:], cols[:, V_BZ:V_BZ + EC], 0.5, None, ALU.mult)
            dve.sem_inc(b_done, 1)
            dve.sem_inc(scan_done, EC)
            rt.dve_start(dve)
            steps = row_stats_steps(CT)

            def low_weights(first, last):
                for n in range(first, last):
                    (_, low), src = raw[n]
                    dve.wait_ge(w_high, n + 1)
                    nc.vector.tensor_tensor(low[:], src, f32(raw[n][0][0][:]), ALU.subtract).then_inc(w_low, 1)

            def norm(c, par):
                ch = Chain(dve, chain, c * steps)
                dve.wait_ge(x_landed[par], turn(c, par) + 16)
                row_stats(nc, ch, lambda j: XB[:, par, j, :], CT, st, sm)
                assert ch.n == steps
                dve.wait_ge(xt_ps, c + 1)
                for j in range(CT):
                    last = nc.vector.tensor_scalar(XN[:, j, :], XB[:, par, j, :], sm[:, 0, j:j + 1], sm[:, 1, j:j + 1],
                                                   ALU.subtract, ALU.mult)
                last.then_inc(xn_ready, 1)

            def low_in(c, par):
                dve.wait_ge(xth, c + 1)
                nc.vector.tensor_tensor(XT[1][:, par, :], pX[:], f32(XT[0][:, par, :]), ALU.subtract).then_inc(xtl, 1)

            def low_x(c, par, m):
                dve.wait_ge(xih, EC * c + m + 1)
                nc.vector.tensor_tensor(XI[1][:, par, m, :], XF[:, m, :], f32(XI[0][:, par, m, :]), ALU.subtract).then_inc(xil, 1)

            def low_sum(c, m):
                dve.wait_ge(sh, EC * c + m + 1)
                nc.vector.tensor_tensor(S[1][:, m, :], SF[:, m, :], f32(S[0][:, m, :]), ALU.subtract).then_inc(sl, 1)

            def new_rows(c, par):
                dve.wait_ge(o_ps, c + 1)
                dve.wait_ge(r_landed[par], turn(c, par) + 16)
                nc.vector.tensor_tensor(R[:, par, :, 0:D], pO[:].rearrange("p (j d) -> p j d", j=CT), R[:, par, :, 0:D],
                                        ALU.add).then_inc(rows_ready, 1)
                dve.wait_ge(rows_ready, c + 1)
                rt.dve_norm(dve, c, par)

            def step(c, par):
                if exists(c + 1) and not (isinstance(c, int) and c == 0):
                    low_in(c + 1, 1 - par)
                for m in range(EC):
                    if m == 1 and exists(c + 2):
                        norm(c + 2, par)
                    if m == 2 and exists(c - 1):
                        new_rows(c - 1, 1 - par)
                    if m:
                        low_sum(c, m - 1)
                    elif exists(c - 1):
                        low_sum(c - 1, EC - 1)
                    if exists(c + 1):
                        low_x(c + 1, 1 - par, m)
                    dve.wait_ge(h_ps, EC * c + m + 1)
                    dve.wait_ge(a_ready, EC * c + m + 1)
                    nc.vector.scalar_tensor_tensor(BB[:, m, :], pH[:], cols[:, V_BH + m:V_BH + m + 1], Z[:, m, :],
                                                   ALU.add, ALU.mult).then_inc(b_done, 1)
                    dve.wait_ge(b_done, EC * c + m + 2)
                    dve.wait_ge(scan_done, EC * c + m + 1)
                    start = H[:, 0, m, CW - 1:CW] if par else 0.0
                    nc.vector.tensor_tensor_scan(H[:, par, m, :], A[:, m, :], BB[:, m, :], start, ALU.mult, ALU.add
                                                 ).then_inc(scan_done, 1)
                    if exists(c - 2):
                        if m == 0:
                            rt.dve_onehot(dve, c - 2)
                        elif m == 1:
                            rt.dve_slots(dve, c - 2, par)

            norm(0, 0)
            low_weights(0, N_UP)
            low_in(0, 0)
            norm(1, 1)
            for m in range(EC):
                low_x(0, 0, m)
            low_in(1, 1)
            low_weights(N_UP, N_RAW)
            chunks(dve, step)
            low_sum(NC - 1, EC - 1)
            rt.dve_onehot(dve, NC - 2)
            rt.dve_slots(dve, NC - 2, 0)
            new_rows(NC - 1, 1)
            rt.dve_onehot(dve, NC - 1)
            rt.dve_slots(dve, NC - 1, 1)


INPUTS = """L0_attn_a_u L0_attn_a_w_in L0_attn_a_b_in L0_attn_a_sf_w L0_attn_a_sf_b L0_attn_a_f_w1 L0_attn_a_f_b1
L0_attn_a_freq1 L0_attn_a_f_w2 L0_attn_a_f_b2 L0_attn_a_freq2 L0_attn_a_f_w3 L0_attn_a_f_b3 L0_attn_a_freq3
L0_attn_a_f_wout L0_attn_a_filt_bias L0_attn_a_w_out L0_attn_a_b_out L0_attn_b_W1 L0_attn_b_b1 L0_attn_b_W2
L0_attn_b_b2 L0_attn_b_Wz L0_attn_b_bz L0_attn_b_Wh L0_attn_b_bh L0_attn_b_Wo L0_attn_b_bo L0_ffn_Wg L0_ffn_bg
L0_ffn_W1 L0_ffn_b1 L0_ffn_W2 L0_ffn_b2""".split()


def kernel(**inputs):
    import concourse.bacc as bacc
    from concourse.bass_utils import run_bass_kernel_spmd

    nc = bacc.Bacc("TRN2", target_bir_lowering=False, num_devices=1)
    arrays = {n: np.ascontiguousarray(inputs[n]) for n in INPUTS}
    arrays.update(constants())
    ins = {n: nc.dram_tensor("in_" + n, a.shape, mybir.dt.from_np(a.dtype), kind="ExternalInput").ap()
           for n, a in arrays.items()}
    out = nc.dram_tensor("out_0", (B * L, D), F32, kind="ExternalOutput").ap()
    build(nc, ins, out)
    r = run_bass_kernel_spmd(nc, [{"in_" + n: a for n, a in arrays.items()}], core_ids=[0])
    return r.results[0]["out_0"].reshape(B, L, D)
```

```python
import math
from contextlib import ExitStack

import numpy as np

import concourse.bass as bass
from concourse import mybir

F32 = mybir.dt.float32
F32R = mybir.dt.float32r
BF16 = mybir.dt.bfloat16
F16 = mybir.dt.float16
I32 = mybir.dt.int32
ALU = mybir.AluOpType
ACT = mybir.ActivationFunctionType
AX = mybir.AxisListType

P = 128
B, L, D = 8, 1024, 128
PARTS = ((0, 0), (0, 1), (1, 0))
NT = B * L // P
TB = L // P
FL, FO = 512, 64
SHIFT = 0.05
EPS = 1e-5
NE, CAP, HID = 16, 512, 512
HC = HID // P
SC = CAP // P
ROW = 132
C_MEAN, C_RSTD, C_GATE, C_TOK = 128, 129, 130, 131
NO_TOKEN = 1 << 20
EX = 512
EC = EX // P
CH = 8
NG = D // CH
RING = 4
RW = 768
TW = 640
FREE = 512

V_BIN, V_SFB, V_FBIAS, V_B1, V_B2, V_BZ, V_BH, V_FFN, V_F, V_FB2, V_BO = 0, 3, 6, 7, 11, 15, 19, 23, 87, 93, 109
N_VEC = 110
N_VEC_DMAS = 1 + 3 + 4 + 3 + 6
N_W_DMAS = 6 + 2
TWO_PI = 2.0 * math.pi
TURN_PARTS = (6.28125, float(np.float32(TWO_PI - 6.28125)))
ROUNDER = 1.5 * 2.0 ** 23
PI_BELOW = 3.1415925


def constants():
    t = np.linspace(0.0, 1.0, FL).astype(np.float32)
    tr = np.linspace(0.0, FL - 1.0, FL).astype(np.float32)
    w = (np.float32(2.0 * np.pi) * tr / np.float32(FL)).astype(np.float32)
    fw = (np.float32(1e-4) * w).astype(np.float32)
    z = np.stack([t, np.cos(fw), -np.sin(fw)]).astype(np.float32)
    deltas = np.abs(np.linspace(math.log(0.01) / 1.5, math.log(0.01) / 0.3, D).astype(np.float32))
    decay = (np.exp(-t[None, :] * deltas[:, None]) + np.float32(SHIFT)).astype(np.float32)
    e = np.arange(NE, dtype=np.float32)
    slot0 = np.concatenate([CAP * e - 1, CAP * (e + 1) - 1, NE - e])
    return {
        "c_z": np.ascontiguousarray(z[:, ::-1]),
        "c_decay": np.ascontiguousarray(decay[:, ::-1]),
        "c_ident": np.eye(P, dtype=np.float32),
        "c_tri": np.triu(np.ones((P, P), np.float32)),
        "c_slot": np.ascontiguousarray(np.broadcast_to(slot0, (P, 3 * NE)).astype(np.float32)),
    }


class Chain:

    def __init__(self, eng, sem, base=0):
        self.eng, self.sem, self.base, self.n = eng, sem, base, 0

    def step(self, ins):
        self.n += 1
        ins.then_inc(self.sem, 1)

    def wait(self):
        self.eng.wait_ge(self.sem, self.base + self.n)

    def link(self, ins):
        self.step(ins)
        self.wait()


def f32(ap):
    return ap.bitcast(F32)


def reversed_tiles(ap2, n):
    a = ap2.rearrange("p (j m) -> p j m", j=n)
    return bass.AP(tensor=a.tensor, offset=a.offset + P - 1,
                   ap=[list(a.ap[0]), list(a.ap[1]), [-1, P]])


def rsqrt_steps(nc, ch, y, t, v, half_magic=1597463007.0):
    vi, yi = v.bitcast(I32), y.bitcast(I32)
    ch.link(nc.vector.tensor_scalar(yi, vi, 1, None, ALU.logical_shift_right))
    ch.link(nc.vector.tensor_scalar(yi, yi, -1.0, half_magic, ALU.mult, ALU.add))
    for _ in range(3):
        ch.link(nc.vector.tensor_tensor(t, y, y, ALU.mult))
        ch.link(nc.vector.scalar_tensor_tensor(t, t, -0.5, v, ALU.mult, ALU.mult))
        ch.link(nc.vector.scalar_tensor_tensor(y, t, 1.5, y, ALU.add, ALU.mult))


RSQRT_STEPS = 11


def power_of_two_scale(nc, ch, top, p, scale):
    ch.link(nc.vector.tensor_scalar(p, top, 2.0 ** -100, None, ALU.max))
    ch.link(nc.vector.tensor_scalar(p.bitcast(I32), p.bitcast(I32), 0x7F800000, None, ALU.bitwise_and))
    ch.link(nc.vector.tensor_scalar(p, p, 2.0 ** -13, None, ALU.mult))
    ch.link(nc.vector.reciprocal(scale, p))


SCALE_STEPS = 4


def row_stats(nc, ch, x_of, n, st, sm):
    for j in range(n):
        ch.step(nc.vector.bn_stats(st[:, j, :], x_of(j)))
    ch.wait()
    mean, rstd, var, tmp = (sm[:, k, :] for k in range(4))
    ch.step(nc.vector.tensor_tensor(mean, st[:, :, 1], st[:, :, 4], ALU.add))
    ch.step(nc.vector.tensor_tensor(tmp, st[:, :, 1], st[:, :, 4], ALU.subtract))
    ch.link(nc.vector.tensor_tensor(var, st[:, :, 2], st[:, :, 5], ALU.add))
    ch.step(nc.vector.tensor_scalar(mean, mean, 0.5, None, ALU.mult))
    ch.step(nc.vector.tensor_tensor(tmp, tmp, tmp, ALU.mult))
    ch.link(nc.vector.tensor_scalar(var, var, 1.0 / D, EPS, ALU.mult, ALU.add))
    ch.link(nc.vector.scalar_tensor_tensor(var, tmp, 0.25, var, ALU.mult, ALU.add))
    rsqrt_steps(nc, ch, rstd, tmp, var)


TAPS_STEPS = 2
SPLIT_STEPS = 1 + SCALE_STEPS


def row_stats_steps(n):
    return n + 7 + RSQRT_STEPS


class Router:

    def __init__(self, nc, ctx, n, bufs, R, w, slots, tables, pT, pL, pC):
        sb = lambda name, shape, d=F32: ctx.enter_context(nc.sbuf_tensor(f"{name}{n}", shape, d))
        sem = lambda name: ctx.enter_context(nc.semaphore(f"{name}_{n}"))
        self.bufs = bufs
        self.nc, self.n, self.R, self.w, self.slots, self.t = nc, n, R, w, slots, tables
        self.pT = pT
        self.pL = pL[:, 0:n * NE].rearrange("p (j e) -> p j e", e=NE)
        self.pC = pC[:, 128:128 + n * NE]
        self.pD = pC[:, 256:256 + NE]
        self.XN = sb("r_xn", [P, n, D])
        self.XNT = sb("r_xnt", [P, n * P])
        self.st = sb("r_st", [P, n, 6])
        self.sm = sb("r_sm", [P, 8, n])
        self.lg = sb("r_lg", [P, 4, n, NE])
        self.oh = sb("r_oh", [P, n * NE], BF16)
        self.base = sb("r_base", [P, NE])
        self.idx = sb("r_idx", [P, bufs, n], I32)
        self.stats, self.xn, self.xt_ps, self.xt, self.lg_ps, self.small, self.onehot, self.expin, self.exped, \
            self.count_ps, self.done = (sem("r_" + x) for x in (
                "stats", "xn", "xt_ps", "xt", "lg_ps", "small", "onehot", "expin", "exped", "count_ps", "done"))
        self.sent, self.rows_free = sem("r_sent"), sem("r_rows_free")

    STEPS2 = 5
    STEPS3 = 8

    def dve_start(self, dve):
        self.nc.vector.tensor_copy(self.base[:], self.t["slot"][:, 0:NE]).then_inc(self.small, 1)
        dve.wait_ge(self.small, 1)

    def dve_norm(self, dve, r, par):
        nc, n, R = self.nc, self.n, self.R[:, par]
        ch = Chain(dve, self.stats, r * row_stats_steps(n))
        row_stats(nc, ch, lambda j: R[:, j, 0:D], n, self.st, self.sm)
        assert ch.n == row_stats_steps(n)
        for j in range(n):
            nc.vector.tensor_scalar(self.XN[:, j, :], R[:, j, 0:D], self.sm[:, 0, j:j + 1], self.sm[:, 1, j:j + 1],
                                    ALU.subtract, ALU.mult)
        nc.vector.tensor_copy(R[:, :, C_MEAN], self.sm[:, 0, :])
        nc.vector.tensor_copy(R[:, :, C_RSTD], self.sm[:, 1, :])
        nc.vector.tensor_copy(R[:, :, C_TOK].bitcast(I32), self.t["token"][:, bass.ds(r * n, n)]).then_inc(self.xn, 1)

    def pe_transpose(self, pe, r):
        pe.wait_ge(self.xn, r + 1)
        for j in range(self.n):
            last = pe.transpose(self.pT[:, P * j:P * j + P], self.XN[:, j, :], self.t["ident"][:])
        last.then_inc(self.xt_ps, 1)

    def pe_logits(self, pe, r):
        pe.wait_ge(self.xt, r + 1)
        for j in range(self.n):
            last = pe.matmul(self.pL[:, j, :], self.XNT[:, P * j:P * j + P], self.w["gate"][:], start=True, stop=True)
        last.then_inc(self.lg_ps, 1)

    def act_transposed(self, act, r):
        act.wait_ge(self.xt_ps, r + 1)
        act.activation(self.XNT[:], self.pT[:], ACT.Copy).then_inc(self.xt, 1)

    def dve_onehot(self, dve, r):
        nc, n, t = self.nc, self.n, self.t
        wide = lambda ap: ap.unsqueeze(1).broadcast_to([P, n, NE])
        tall = lambda ap: ap.unsqueeze(2).broadcast_to([P, n, NE])
        lg, top, first = self.lg, self.sm[:, 4, :], self.sm[:, 5, :]
        ch = Chain(dve, self.small, 1 + r * (self.STEPS2 + self.STEPS3 + 1))
        dve.wait_ge(self.lg_ps, r + 1)
        ch.link(nc.vector.tensor_tensor(lg[:, 0], self.pL, wide(self.w["gate_b"][:]), ALU.add))
        ch.link(nc.vector.tensor_reduce(top, lg[:, 0], AX.X, ALU.max))
        nc.vector.tensor_tensor(lg[:, 1], lg[:, 0], tall(top), ALU.subtract).then_inc(self.expin, 1)
        ch.link(nc.vector.tensor_tensor(lg[:, 2], lg[:, 0], tall(top), ALU.is_equal))
        ch.link(nc.vector.tensor_tensor(lg[:, 2], lg[:, 2], wide(t["slot"][:, 2 * NE:3 * NE]), ALU.mult))
        ch.link(nc.vector.tensor_reduce(first, lg[:, 2], AX.X, ALU.max))
        assert ch.n == self.STEPS2
        nc.vector.tensor_tensor(self.oh[:].rearrange("p (j e) -> p j e", e=NE), lg[:, 2], tall(first),
                                ALU.is_equal).then_inc(self.onehot, 1)

    def act_tanh(self, act, r):
        act.wait_ge(self.expin, r + 1)
        act.activation(self.lg[:, 1], self.lg[:, 1], ACT.Tanh, scale=0.5).then_inc(self.exped, 1)

    def pe_counts(self, pe, r):
        pe.wait_ge(self.onehot, r + 1)
        n, oh, t = self.n, self.oh, self.t
        for k in range(n):
            pe.matmul(self.pC[:, NE * k:], t["tri16"][:] if k == 0 else t["ones16"][:], oh[:, 0:NE * (n - k)],
                      start=k == 0, stop=k == n - 1)
        for k in range(n):
            last = pe.matmul(self.pD, t["ones16"][:], oh[:, NE * k:NE * k + NE], start=k == 0, stop=k == n - 1)
        last.then_inc(self.count_ps, 1)

    def dve_slots(self, dve, r, par):
        nc, n, t, lg = self.nc, self.n, self.t, self.lg
        wide = lambda ap: ap.unsqueeze(1).broadcast_to([P, n, NE])
        base = 1 + r * (self.STEPS2 + self.STEPS3 + 1) + self.STEPS2
        ch = Chain(dve, self.small, base)
        q, over = lg[:, 2], lg[:, 3]
        dve.wait_ge(self.exped, r + 1)
        dve.wait_ge(self.count_ps, r + 1)
        ch.link(nc.vector.tensor_scalar(q, lg[:, 1], -1.0, 1.0, ALU.mult, ALU.add))
        ch.link(nc.vector.reciprocal(over, q))
        ch.link(nc.vector.scalar_tensor_tensor(over, lg[:, 1], 1.0, over, ALU.add, ALU.mult))
        ch.link(nc.vector.tensor_reduce(self.sm[:, 6, :], over, AX.X, ALU.add))
        nc.vector.reciprocal(self.R[:, par, :, C_GATE], self.sm[:, 6, :])
        ch.link(nc.vector.tensor_tensor(q, self.pC.rearrange("p (j e) -> p j e", e=NE), wide(self.base[:]), ALU.add))
        ch.step(nc.vector.tensor_tensor(self.base[:], self.base[:], self.pD, ALU.add))
        ch.link(nc.vector.tensor_tensor(over, q, wide(t["slot"][:, NE:2 * NE]), ALU.is_gt))
        ch.link(nc.vector.scalar_tensor_tensor(q, over, float(NO_TOKEN), q, ALU.mult, ALU.add))
        assert ch.n == self.STEPS3
        ch.link(nc.vector.tensor_tensor(q, q, self.oh[:].rearrange("p (j e) -> p j e", e=NE), ALU.mult))
        nc.vector.tensor_reduce(self.idx[:, par, :], q, AX.X, ALU.max).then_inc(self.done, 1)

    def pool_start(self, pool):
        limit = pool.alloc_register(f"last_slot{self.n}")
        pool.reg_mov(limit, NE * CAP - 1)
        self.last_slot = pool.snap(limit)
        pool.sem_inc(self.rows_free, self.bufs)

    def pool_send(self, pool, r, par):
        pool.wait_ge(self.done, r + 1)
        pool.nop(nofuse=True)
        for j in range(self.n):
            pool.indirect_dma_start(out=self.slots, out_offset=bass.IndirectOffsetOnAxis(ap=self.idx[:, par, j:j + 1], axis=0),
                                    in_=self.R[:, par, j, :], in_offset=None, bounds_check=self.last_slot,
                                    oob_is_err=False).then_inc(self.sent, 16)

    def pool_release(self, pool, r):
        pool.wait_ge(self.sent, 16 * self.n * (r + 1))
        pool.sem_inc(self.rows_free, 1)


def build_mixer_out(nc, ins, scr, keep):
    X0T, Y, ident, ascale = keep["X0T"], keep["Y"], keep["ident"], keep["ascale"]
    u = ins["L0_attn_a_u"].rearrange("b (j p) d -> b p j d", p=P)
    xout = scr["x1"].rearrange("(b j p) d -> b p j d", p=P, j=TB)
    BUFS = 3
    with ExitStack() as ctx:
        sb = lambda n, s, d=F32: ctx.enter_context(nc.sbuf_tensor(n, s, d))
        sem = lambda n: ctx.enter_context(nc.semaphore(n))
        ps = lambda n, s: ctx.enter_context(nc.psum_tensor(n, s, F32))
        w_out, b_out = sb("w_out", [P, D]), sb("b_out", [P, D])
        U = sb("o_u", [P, BUFS, TB, D])
        R = sb("o_rows", [P, BUFS, TB, ROW])
        YS, ZT = sb("o_ys", [P, TB, D]), sb("o_zt", [P, L])
        pZ, pO, pX, pS, pC = ps("pZ", [P, L]), ps("pO", [P, L]), ps("pX", [P, L]), ps("pS", [P, FREE]), ps("pC", [P, FREE])
        w_landed, ys_ready, z_ps, z_ready, o_ps, ub_ready, rows_ready = (
            sem("o_" + x) for x in ("w_landed", "ys_ready", "z_ps", "z_ready", "o_ps", "ub_ready", "rows_ready"))
        u_landed, stored = ([sem(f"o_{x}{k}") for k in range(BUFS)] for x in ("u_landed", "stored"))
        rt = Router(nc, ctx, TB, BUFS, R, keep["gatew"], scr["slots1"], keep["tables"], pX, pS, pC)
        block = ctx.enter_context(nc.Block())

        def batches(eng, step):
            step(0, 0, 0, True, False)
            with eng.Fori(0, (B - 2) // BUFS) as i:
                for j in range(1, BUFS + 1):
                    step(BUFS * i + j, j % BUFS, i + j // BUFS, False, False)
            step(B - 1, (B - 1) % BUFS, (B - 1) // BUFS, False, True)

        before = lambda k: (k + BUFS - 1) % BUFS
        after = lambda k: (k + 1) % BUFS
        one = lambda ap, b: ap[b] if isinstance(b, int) else ap[bass.ds(b, 1)].rearrange("b p j d -> (b p) j d")

        @block.sync
        def _(sp):
            sp.dma_start(U[:, 0], u[0]).then_inc(u_landed[0], 16)
            sp.dma_start(w_out[:], ins["L0_attn_a_w_out"]).then_inc(w_landed, 16)
            sp.dma_start(b_out[:], row_to_all(ins["L0_attn_a_b_out"], D)).then_inc(w_landed, 16)
            for k in range(BUFS):
                sp.sem_inc(stored[k], 16)

            def step(b, k, n, first, last):
                if not last:
                    sp.dma_start(U[:, after(k)], one(u, b + 1)).then_inc(u_landed[after(k)], 16)
                sp.wait_ge(rows_ready, b + 1)
                sp.dma_start(one(xout, b), R[:, k, :, 0:D]).then_inc(stored[k], 16)

            batches(sp, step)
            for k in range(BUFS):
                sp.wait_ge(stored[k], 16 + 16 * len(range(k, B, BUFS)))

        @block.gpsimd
        def _(pool):
            rt.pool_start(pool)

            def add_bias(b, k, n):
                pool.wait_ge(u_landed[k], 16 * n + 16)
                pool.tensor_tensor(U[:, k], U[:, k], b_out[:].unsqueeze(1).broadcast_to([P, TB, D]), ALU.add).then_inc(ub_ready, 1)

            def step(b, k, n, first, last):
                if not last:
                    add_bias(b + 1, after(k), n + (k == BUFS - 1))
                if not first:
                    rt.pool_send(pool, b - 1, before(k))
                    rt.pool_release(pool, b - 1)

            pool.wait_ge(keep["cleared"], 32)
            pool.wait_ge(w_landed, 32)
            add_bias(0, 0, 0)
            batches(pool, step)
            rt.pool_send(pool, B - 1, (B - 1) % BUFS)
            rt.pool_release(pool, B - 1)

        @block.scalar
        def _(act):
            def copy_y(b):
                act.wait_ge(z_ps, b + 1)
                act.activation(YS[:], Y[:].rearrange("p (j b) d -> p j b d", b=B)[:, :, bass.ds(b, 1), :]
                               .rearrange("p j b d -> p j (b d)"), ACT.Copy).then_inc(ys_ready, 1)

            def step(b, k, n, first, last):
                if not last:
                    copy_y(b + 1)
                rt.act_transposed(act, b)
                if not first:
                    rt.act_tanh(act, b - 1)

            copy_y(0)
            batches(act, step)
            rt.act_tanh(act, B - 1)

        @block.tensor
        def _(pe):
            def transpose_y(b):
                pe.wait_ge(ys_ready, b + 1)
                for j in range(TB):
                    last = pe.transpose(pZ[:, P * j:P * j + P], YS[:, j, :], ident[:])
                last.then_inc(z_ps, 1)

            def step(b, k, n, first, last):
                pe.wait_ge(z_ready, b + 1)
                for j in range(TB):
                    mm = pe.matmul(pO[:, P * j:P * j + P], ZT[:, P * j:P * j + P], w_out[:], start=True, stop=True)
                mm.then_inc(o_ps, 1)
                if not last:
                    transpose_y(b + 1)
                if not first:
                    rt.pe_logits(pe, b - 1)
                rt.pe_transpose(pe, b)
                if not first:
                    rt.pe_counts(pe, b - 1)

            pe.wait_ge(w_landed, 32)
            pe.sem_inc(z_ps, 1)
            transpose_y(0)
            batches(pe, step)
            rt.pe_logits(pe, B - 1)
            rt.pe_counts(pe, B - 1)

        @block.vector
        def _(dve):
            rt.dve_start(dve)

            def gate_y(b):
                dve.wait_ge(z_ps, b + 2)
                nc.vector.scalar_tensor_tensor(
                    ZT[:].rearrange("p (j m) -> p j m", j=TB), reversed_tiles(pZ[:], TB), ascale[:, bass.ds(b, 1)],
                    X0T[:, bass.ds(b * L, L)].rearrange("p (j m) -> p j m", j=TB), ALU.mult, ALU.mult
                ).then_inc(z_ready, 1)

            def step(b, k, n, first, last):
                dve.wait_ge(o_ps, b + 1)
                dve.wait_ge(ub_ready, b + 1)
                dve.wait_ge(stored[k], 16 * n + 16)
                dve.wait_ge(rt.rows_free, b + 1)
                nc.vector.tensor_tensor(R[:, k, :, 0:D], pO[:].rearrange("p (j d) -> p j d", j=TB), U[:, k],
                                        ALU.add).then_inc(rows_ready, 1)
                dve.wait_ge(rows_ready, b + 1)
                rt.dve_norm(dve, b, k)
                if not first:
                    rt.dve_onehot(dve, b - 1)
                if not last:
                    gate_y(b + 1)
                if not first:
                    rt.dve_slots(dve, b - 1, before(k))

            gate_y(0)
            batches(dve, step)
            rt.dve_onehot(dve, B - 1)
            rt.dve_slots(dve, B - 1, (B - 1) % BUFS)


def row_to_all(ap, n):
    return bass.AP(tensor=ap.tensor, offset=ap.offset, ap=[[0, P], [1, n]])


def build_mixer(nc, ins, scr, keep):
    u = ins["L0_attn_a_u"].rearrange("b (j p) d -> b p j d", p=P)
    with ExitStack() as ctx:
        sb = lambda n, s, d=F32: ctx.enter_context(nc.sbuf_tensor(n, s, d))
        sem = lambda n: ctx.enter_context(nc.semaphore(n))
        X0T, ident, cols = keep["X0T"], keep["ident"], keep["cols"]
        Y = keep["Y"]
        VT = sb("VT", [P, 2, TB, B, D], F16)
        toep = sb("toep", [P, RING, CH, 2, TW], F16)
        ascale = keep["ascale"]
        toep_landed = [sem(f"toep_landed{r}") for r in range(RING)]
        filt_written = sem("filt_written")

        def load_toeplitz(eng, g, r):
            a = scr["filt"]
            src = bass.AP(tensor=a.tensor, offset=a.offset + g * (CH * 2 * RW), ap=[[1, P], [RW, 2 * CH], [1, TW]])
            eng.dma_start(toep[:, r].rearrange("p c h x -> p (c h) x"), src).then_inc(toep_landed[r], 16)

        with ExitStack() as c1:
            sb1 = lambda n, s, d=F32: c1.enter_context(nc.sbuf_tensor(n, s, d))
            ps1 = lambda n, s: c1.enter_context(nc.psum_tensor(n, s, F32))
            sem1 = lambda n: c1.enter_context(nc.semaphore(n))
            fw1 = sb1("fw1", [3, FO])
            fw23 = sb1("fw23", [FO, 2, FO])
            fwout = sb1("fwout", [FO, D])
            fparts = sb1("fparts", [P, 2, RW], F16)
            fscale = sb1("fscale", [P, 4])
            vscale = sb1("vscale", [P, 4])
            VP = sb1("VP", [P, 2, L], F16)
            X0TMP = sb1("X0TMP", [P, L])
            ident16 = sb1("ident16", [P, P], F16)
            sfw = sb1("sfw", [P, 3, 3])
            U = sb1("U", [P, 2, TB, D])
            XN = sb1("XN", [P, TB, D])
            XNT = sb1("XNT", [P, L])
            spare = Y[:].rearrange("p n d -> p (n d)")
            TAP = spare[:, 0:3 * L].rearrange("p (g l) -> p g l", g=3)
            VV = spare[:, 3 * L:4 * L]
            w_in = spare[:, TB * B * D - 3 * D:TB * B * D]
            UP = spare[:, 4 * L:4 * L + 3 * (L + 2)].rearrange("p (g l) -> p g l", g=3)
            temp = toep[:, RING - 1].rearrange("p c h x -> p (c h x)").bitcast(F32)
            z, decay, frow = temp[0:3, 0:FL], temp[:, FL:2 * FL], temp[:, 2 * FL:2 * FL + RW]
            fh = temp[0:FO, 4 * FL:6 * FL].rearrange("f (n t) -> f n t", n=2)
            fq = temp[0:FO, 6 * FL:8 * FL].rearrange("f (n t) -> f n t", n=2)
            vecs = temp[0:N_VEC, 8 * FL:8 * FL + P]
            st = sb1("st", [P, TB, 6])
            sm = sb1("sm", [P, 4, TB])
            pT = ps1("pT", [P, 2 * FREE])
            pV = pT[:].bitcast(F16).rearrange("p (h j d) -> p h j d", h=2, j=TB)
            pP = [ps1(f"pP{g}", [P, 2 * FREE]) for g in range(3)]

            zeroed, consts_in = sem1("zeroed"), sem1("consts_in")
            cols_ps, cols_ready, fl_ps, fl_ready = (sem1(n) for n in ("cols_ps", "cols_ready", "fl_ps", "fl_ready"))
            fl_chain, fl_arg, frow_ready = (sem1(n) for n in ("fl_chain", "fl_arg", "frow_ready"))
            w_landed = sem1("w_landed")
            u_landed = [sem1("u_landed0"), sem1("u_landed1")]
            xn_ready, xnt_ps, xnt_ready, proj_ps, up_ready = (
                sem1(n) for n in ("xn_ready", "xnt_ps", "xnt_ready", "proj_ps", "up_ready"))
            tap0_ready, tap_done, vv_ready, vt_ps, vt_ready = (
                sem1(n) for n in ("tap0_ready", "tap_done", "vv_ready", "vt_ps", "vt_ready"))
            n_chain, t_chain, s_chain, p_chain = (sem1(n) for n in ("n_chain", "t_chain", "s_chain", "p_chain"))
            x0_done, vhi_ready, vlo_ready, vscale_ready = (
                sem1(n) for n in ("x0_done", "vhi_ready", "vlo_ready", "vscale_ready"))
            block = c1.enter_context(nc.Block())
            ORDER = (1, 2, 0)

            @block.sync
            def _(sp):
                for par in range(2):
                    sp.dma_start(U[:, par], u[par]).then_inc(u_landed[par], 16)
                sp.wait_ge(zeroed, 1)
                row = lambda name, r, n: sp.dma_start(
                    vecs[r:r + n, :], ins[name].rearrange("(k p) -> k p", p=P)).then_inc(consts_in, 16)
                sp.dma_start(ident[:], ins["c_ident"]).then_inc(consts_in, 16)
                row("L0_attn_a_b_in", V_BIN, 3)
                row("L0_attn_a_sf_b", V_SFB, 3)
                row("L0_attn_a_filt_bias", V_FBIAS, 1)
                row("L0_attn_b_b1", V_B1, EC)
                row("L0_attn_b_b2", V_B2, EC)
                row("L0_attn_b_bz", V_BZ, EC)
                row("L0_attn_b_bh", V_BH, EC)
                sp.dma_start(vecs[V_FFN:V_FFN + NE * HC, :],
                             ins["L0_ffn_b1"].rearrange("e (k p) -> (e k) p", p=P)).then_inc(consts_in, 16)
                sp.dma_start(vecs[V_FB2:V_FB2 + NE, :], ins["L0_ffn_b2"]).then_inc(consts_in, 16)
                row("L0_attn_b_bo", V_BO, 1)
                for n, name in enumerate(("f_b1", "freq1", "f_b2", "freq2", "f_b3", "freq3")):
                    sp.dma_start(vecs[V_F + n:V_F + n + 1, 0:FO],
                                 ins["L0_attn_a_" + name].rearrange("(a n) -> a n", a=1)).then_inc(consts_in, 16)

                def load_u(b):
                    sp.wait_ge(xn_ready, 2 * b - 2)
                    sp.dma_start(U[:, b % 2], u[b]).then_inc(u_landed[b % 2], 16)

                load_u(2)
                sp.wait_ge(frow_ready, 1)
                sp.dma_start(scr["filt"], fparts[:]).then_inc(filt_written, 16)
                load_u(3)
                sp.wait_ge(filt_written, 16)
                for r in range(RING):
                    load_toeplitz(sp, r, r)
                    load_u(4 + r)
                for n in ("slots1", "slots2"):
                    sp.dma_start(scr[n].rearrange("(p q) d -> p q d", p=P),
                                 keep["empty"][:].unsqueeze(1).broadcast_to([P, NE * CAP // P, ROW])
                                 ).then_inc(keep["cleared"], 16)


            @block.gpsimd
            def _(pool):
                pool.memset(vecs, 0.0).then_inc(zeroed, 1)
                pool.memset(frow, 0.0).then_inc(zeroed, 1)
                pool.memset(UP[:, :, 0:2], 0.0).then_inc(zeroed, 1)
                pool.wait_ge(w_landed, 16 * N_W_DMAS)
                pool.sem_inc(vv_ready, 1)
                pool.sem_inc(x0_done, 1)
                with pool.Fori(0, B) as b:
                    ch = Chain(pool, p_chain, 3 * b)
                    pool.wait_ge(tap_done, 2 * b + 4)
                    pool.wait_ge(vhi_ready, b + 1)
                    pool.wait_ge(vlo_ready, b + 1)
                    pool.tensor_tensor(VV, TAP[:, 1, :], TAP[:, 2, :], ALU.mult).then_inc(vv_ready, 1)
                    pool.wait_ge(tap0_ready, 3 * b + 3)
                    ch.link(pool.tensor_tensor(X0TMP[:], UP[:, 0, 1:L + 1], sfw[:, 0, 1:2].broadcast_to([P, L]), ALU.mult))
                    ch.link(pool.tensor_tensor(TAP[:, 0, :], TAP[:, 0, :], X0TMP[:], ALU.add))
                    ch.link(pool.tensor_tensor(X0TMP[:], UP[:, 0, 0:L], sfw[:, 0, 0:1].broadcast_to([P, L]), ALU.mult))
                    pool.tensor_tensor(X0T[:, bass.ds(b * L, L)], TAP[:, 0, :], X0TMP[:], ALU.add).then_inc(x0_done, 1)

            @block.tensor
            def _(pe):
                pe.sem_inc(vt_ps, 1)
                pe.sem_inc(xnt_ps, 2)
                pe.sem_inc(proj_ps, 3)

                def filter_layer(n):
                    w, x, outs = ((fw1[:], z, FO), (fw23[:, 0, :], fh[:, 0, :], FO), (fw23[:, 1, :], fh[:, 1, :], FO),
                                  (fwout[:], fh[:, 0, :], P))[n]
                    if n:
                        pe.wait_ge(fl_ready, n)
                    else:
                        pe.wait_ge(w_landed, 16 * N_W_DMAS)
                    pe.matmul(pP[0][0:outs, 0:FL], w, x, start=True, stop=True).then_inc(fl_ps, 1)

                def transpose_x(b, free):
                    for h in range(2):
                        pe.wait_ge(xn_ready, 2 * b + h + 1)
                        if h == 0 and not free:
                            pe.wait_ge(vt_ready, b - 1)
                        for j in range(4 * h, 4 * h + 4):
                            last = pe.transpose(pT[:, P * j:P * j + P], XN[:, j, :], ident[:])
                        last.then_inc(xnt_ps, 1)

                def project(b, ns):
                    for n in ns:
                        g = ORDER[n]
                        pe.wait_ge(up_ready, 3 * b + n + 1)
                        for h in range(2):
                            if n == 0:
                                pe.wait_ge(xnt_ready, 2 * b + h + 1)
                            last = pe.matmul(pP[g][:, FREE * h:FREE * h + FREE], w_in[:, g * D:g * D + D],
                                             XNT[:, FREE * h:FREE * h + FREE], start=True, stop=True)
                        last.then_inc(proj_ps, 1)

                def transpose_v(b):
                    pe.wait_ge(vhi_ready, b + 2)
                    for h in range(2):
                        if h:
                            pe.wait_ge(vlo_ready, b + 2)
                        for j in range(TB):
                            last = pe.transpose(pV[:, h, j, :], VP[:, h, P * j:P * j + P], ident16[:])
                    last.then_inc(vt_ps, 1)

                pe.wait_ge(consts_in, 16 * N_VEC_DMAS)
                pe.transpose(pT[:, 0:N_VEC], vecs, ident[0:N_VEC, 0:N_VEC]).then_inc(cols_ps, 1)
                filter_layer(0)
                pe.wait_ge(cols_ready, 2)
                transpose_x(0, True)
                filter_layer(1)
                project(0, (0, 1))
                filter_layer(2)
                transpose_x(1, True)
                filter_layer(3)
                pe.wait_ge(frow_ready, 1)
                project(0, (2,))
                project(1, range(3))
                with pe.Fori(0, B - 2) as b:
                    transpose_x(b + 2, False)
                    project(b + 2, (0, 1))
                    transpose_v(b)
                    project(b + 2, (2,))
                transpose_v(B - 2)
                pe.wait_ge(vt_ready, B)
                transpose_v(B - 1)

            @block.scalar
            def _(act):
                for dst, name in ((z, "c_z"), (decay, "c_decay"), (fw1[:], "L0_attn_a_f_w1"),
                                  (fw23[:, 0, :], "L0_attn_a_f_w2"), (fw23[:, 1, :], "L0_attn_a_f_w3"),
                                  (fwout[:], "L0_attn_a_f_wout")):
                    act.dma_start(dst, ins[name]).then_inc(w_landed, 16)
                act.dma_start(w_in[:], ins["L0_attn_a_w_in"]).then_inc(w_landed, 16)
                act.dma_start(sfw[:], ins["L0_attn_a_sf_w"].rearrange("(g p) k -> p g k", p=P)).then_inc(w_landed, 16)
                act.sem_inc(vt_ready, 1)
                act.sem_inc(up_ready, 3)
                act.sem_inc(vhi_ready, 1)

                def filter_sin(n):
                    act.wait_ge(fl_arg, n + 1)
                    act.activation(fh[:, n % 2, :], fq[:, 0, :], ACT.Sin).then_inc(fl_ready, 1)

                def columns(b):
                    for h in range(2):
                        act.wait_ge(xnt_ps, 2 * b + h + 3)
                        if h == 0:
                            act.wait_ge(proj_ps, 3 * b + 3)
                        act.activation(XNT[:, FREE * h:FREE * h + FREE], pT[:, FREE * h:FREE * h + FREE],
                                       ACT.Copy).then_inc(xnt_ready, 1)

                def first_taps(b, ns):
                    for n in ns:
                        g = ORDER[n]
                        act.wait_ge(proj_ps, 3 * b + n + 4)
                        if g:
                            act.wait_ge(tap_done, 2 * b + n + 1)
                        else:
                            act.wait_ge(x0_done, b + 1)
                        act.activation(UP[:, g, 2:L + 2], pP[g][:], ACT.Identity,
                                       bias=cols[:, V_BIN + g:V_BIN + g + 1]).then_inc(up_ready, 1)
                        act.wait_ge(up_ready, 3 * b + n + 4)
                        if n == 0:
                            act.wait_ge(vv_ready, b + 1)
                        act.activation(TAP[:, g, :], UP[:, g, 2:L + 2], ACT.Identity, scale=sfw[:, g, 2:3],
                                       bias=cols[:, V_SFB + g:V_SFB + g + 1]).then_inc(tap0_ready, 1)

                def high(b):
                    act.wait_ge(vscale_ready, b + 1)
                    act.wait_ge(vt_ps, b + 1)
                    act.activation(VP[:, 0, :], VV, ACT.Copy, scale=vscale[:, 2:3]).then_inc(vhi_ready, 1)

                def copy_v(b):
                    act.wait_ge(vt_ps, b + 2)
                    act.activation(VT[:, :, :, bass.ds(b, 1), :].rearrange("p h j b d -> p (h j) (b d)"),
                                   pV.rearrange("p h j d -> p (h j) d"), ACT.Copy).then_inc(vt_ready, 1)

                filter_sin(0)
                columns(0)
                filter_sin(1)
                act.wait_ge(cols_ready, 1)
                act.wait_ge(zeroed, 3)
                act.wait_ge(w_landed, 16 * N_W_DMAS)
                first_taps(0, (0, 1))
                filter_sin(2)
                first_taps(0, (2,))
                columns(1)
                with act.Fori(0, B - 2) as b:
                    first_taps(b + 1, (0, 1))
                    columns(b + 2)
                    high(b)
                    first_taps(b + 1, (2,))
                    copy_v(b)
                first_taps(B - 1, (0, 1))
                high(B - 2)
                first_taps(B - 1, (2,))
                copy_v(B - 2)
                high(B - 1)
                copy_v(B - 1)

            @block.vector
            def _(dve):
                def norm(b, par, landed, first=False):
                    ch = Chain(dve, n_chain, b * row_stats_steps(TB))
                    dve.wait_ge(u_landed[par], landed)
                    row_stats(nc, ch, lambda j: U[:, par, j, :], TB, st, sm)
                    assert ch.n == row_stats_steps(TB)
                    if not first:
                        dve.wait_ge(xnt_ps, 2 * b + 2)
                    for j in range(TB):
                        last = nc.vector.tensor_scalar(XN[:, j, :], U[:, par, j, :], sm[:, 0, j:j + 1], sm[:, 1, j:j + 1],
                                                       ALU.subtract, ALU.mult)
                        if j % 4 == 3:
                            last.then_inc(xn_ready, 1)

                ch = Chain(dve, fl_chain)

                def filter_argument(n):
                    fb = cols[0:FO, V_F + 2 * n:V_F + 2 * n + 1]
                    fr = cols[0:FO, V_F + 2 * n + 1:V_F + 2 * n + 2]
                    dve.wait_ge(fl_ps, n + 1)
                    if n:
                        dve.wait_ge(fl_ready, n)
                    ch.link(nc.vector.tensor_scalar(fq[:, 0, :], pP[0][0:FO, 0:FL], fb, fr, ALU.add, ALU.mult))
                    ch.link(nc.vector.tensor_scalar(fq[:, 1, :], fq[:, 0, :], 1.0 / TWO_PI, ROUNDER, ALU.mult, ALU.add))
                    ch.link(nc.vector.tensor_scalar(fq[:, 1, :], fq[:, 1, :], ROUNDER, None, ALU.subtract))
                    for c in TURN_PARTS:
                        ch.link(nc.vector.scalar_tensor_tensor(fq[:, 0, :], fq[:, 1, :], -c, fq[:, 0, :], ALU.mult, ALU.add))
                    nc.vector.tensor_scalar(fq[:, 0, :], fq[:, 0, :], PI_BELOW, -PI_BELOW, ALU.min, ALU.max).then_inc(fl_arg, 1)

                def filter_rows():
                    dve.wait_ge(fl_ps, 4)
                    dve.wait_ge(zeroed, 2)
                    ch.link(nc.vector.tensor_tensor(frow[:, P:P + FL], pP[0][:, 0:FL], decay, ALU.mult))
                    ch.link(nc.vector.tensor_tensor(frow[:, P + FL - 1:P + FL], frow[:, P + FL - 1:P + FL],
                                                    cols[:, V_FBIAS:V_FBIAS + 1], ALU.add))
                    ch.link(nc.vector.tensor_reduce(fscale[:, 0:1], frow[:, P:P + FL], AX.X, ALU.max, apply_absolute_value=True))
                    power_of_two_scale(nc, ch, fscale[:, 0:1], fscale[:, 1:2], fscale[:, 2:3])
                    ch.link(nc.vector.tensor_scalar(fparts[:, 0, :], frow, fscale[:, 2:3], None, ALU.mult))
                    nc.vector.scalar_tensor_tensor(fparts[:, 1, :], frow, fscale[:, 2:3], fparts[:, 0, :],
                                                   ALU.mult, ALU.subtract).then_inc(frow_ready, 1)

                def taps(b):
                    ch = Chain(dve, t_chain, b * TAPS_STEPS)
                    for n, g in enumerate(ORDER[:2]):
                        dve.wait_ge(tap0_ready, 3 * b + n + 1)
                        ch.link(nc.vector.scalar_tensor_tensor(TAP[:, g, :], UP[:, g, 1:L + 1], sfw[:, g, 1:2],
                                                               TAP[:, g, :], ALU.mult, ALU.add))
                        nc.vector.scalar_tensor_tensor(TAP[:, g, :], UP[:, g, 0:L], sfw[:, g, 0:1],
                                                       TAP[:, g, :], ALU.mult, ALU.add).then_inc(tap_done, 1)

                def split(b):
                    ch = Chain(dve, s_chain, b * SPLIT_STEPS)
                    dve.wait_ge(vv_ready, b + 2)
                    ch.link(nc.vector.tensor_reduce(vscale[:, 0:1], VV, AX.X, ALU.max, apply_absolute_value=True))
                    dve.wait_ge(vhi_ready, b + 1)
                    power_of_two_scale(nc, ch, vscale[:, 0:1], vscale[:, 1:2], vscale[:, 2:3])
                    nc.vector.tensor_tensor(ascale[:, bass.ds(b, 1)], vscale[:, 1:2], fscale[:, 1:2], ALU.mult).then_inc(vscale_ready, 1)
                    dve.wait_ge(vhi_ready, b + 2)
                    nc.vector.scalar_tensor_tensor(VP[:, 1, :], VV, vscale[:, 2:3], VP[:, 0, :],
                                                   ALU.mult, ALU.subtract).then_inc(vlo_ready, 1)

                dve.sem_inc(tap_done, 2)
                dve.sem_inc(vlo_ready, 1)
                norm(0, 0, 16, True)
                dve.wait_ge(cols_ps, 1)
                nc.vector.tensor_copy(cols[:], pT[:, 0:N_VEC]).then_inc(cols_ready, 1)
                dve.wait_ge(cols_ready, 1)
                nc.vector.tensor_copy(ident16[:], ident[:]).then_inc(cols_ready, 1)
                filter_argument(0)
                norm(1, 1, 16)
                filter_argument(1)
                taps(0)
                filter_argument(2)
                norm(2, 0, 32)
                filter_rows()
                split(0)
                taps(1)
                norm(3, 1, 32)
                split(1)
                with dve.Fori(1, B // 2 - 1) as i:
                    for par in range(2):
                        taps(2 * i + par)
                        norm(2 * i + par + 2, par, 16 * i + 32)
                        split(2 * i + par)
                for b in (B - 2, B - 1):
                    taps(b)
                    split(b)

        with ExitStack() as c2:
            sem2 = lambda n: c2.enter_context(nc.semaphore(n))
            VG = c2.enter_context(nc.sbuf_tensor("VG", [P, RING, 2, CH, TB * B], F16))
            pY = [c2.enter_context(nc.psum_tensor(f"pY{r}", [P, CH, TB * B], F32)) for r in range(RING)]
            vg_ready, conv_done, y_ready = sem2("vg_ready"), sem2("conv_done"), sem2("y_ready")
            block = c2.enter_context(nc.Block())

            @block.sync
            def _(sp):
                with sp.Fori(1, NG // RING) as i:
                    for r in range(RING):
                        sp.wait_ge(conv_done, RING * (i - 1) + r + 1 + RING)
                        load_toeplitz(sp, RING * i + r, r)

            @block.vector
            def _(dve):
                dve.sem_inc(vg_ready, 1)
                with dve.Fori(0, NG // RING) as i:
                    for r in range(RING):
                        dve.wait_ge(conv_done, RING * i + r + 1)
                        for h in range(2):
                            last = nc.vector.tensor_copy(
                                VG[:, r, h], VT[:, h, :, :, bass.ds((RING * i + r) * CH, CH)].rearrange("p j b c -> p c (j b)"))
                        last.then_inc(vg_ready, 1)

            @block.tensor
            def _(pe):
                pe.sem_inc(conv_done, RING)
                with pe.Fori(0, NG // RING) as i:
                    for r in range(RING):
                        pe.wait_ge(toep_landed[r], 16 * i + 16)
                        pe.wait_ge(vg_ready, RING * i + r + 2)
                        pe.wait_ge(y_ready, RING * i + r + 1)
                        for c in range(CH):
                            for d in range(TB // 2 + 1):
                                for k, v in PARTS:
                                    last = pe.matmul(pY[r][:, c, B * d:], toep[:, r, c, k, FL - P * d:FL - P * d + P],
                                                     VG[:, r, v, c, 0:B * (TB - d)],
                                                     start=d == 0 and (k, v) == PARTS[0],
                                                     stop=d == TB // 2 and (k, v) == PARTS[-1])
                        last.then_inc(conv_done, 1)

            @block.scalar
            def _(act):
                act.sem_inc(y_ready, RING)
                with act.Fori(0, NG // RING) as i:
                    for r in range(RING):
                        act.wait_ge(conv_done, RING * i + r + 1 + RING)
                        act.activation(Y[:, :, bass.ds((RING * i + r) * CH, CH)],
                                       pY[r][:].rearrange("p c n -> p n c"), ACT.Copy).then_inc(y_ready, 1)


def build_experts(nc, ins, slots, out, keep, tag):
    ident, cols = keep["ident"], keep["cols"]
    w1, w2 = ins["L0_ffn_W1"], ins["L0_ffn_W2"].rearrange("e (k p) d -> e p k d", p=P)
    with ExitStack() as ctx:
        sb = lambda n, s, d=F32: ctx.enter_context(nc.sbuf_tensor(tag + n, s, d))
        sem = lambda n: ctx.enter_context(nc.semaphore(tag + n))
        ps = lambda n: ctx.enter_context(nc.psum_tensor(tag + n, [P, FREE], F32))
        parts = lambda n, s: (sb(n + "h", s, F32R), sb(n + "l", s, F32R))
        G = sb("rows", [P, NE, SC, ROW])
        W1F, W2F = sb("w1f", [P, 2, HID]), sb("w2f", [P, 2, HC, D])
        W1, W2, XT, HT = parts("w1", [P, 2, HID]), parts("w2", [P, 2, HC, D]), parts("xt", [P, 2, CAP]), parts("ht", [P, 2, HC, CAP])
        XN, HF, YT, O = sb("xn", [P, SC, D]), sb("hf", [P, HC, CAP]), sb("yt", [P, CAP]), sb("o", [P, 2, SC, D])
        token = sb("token", [P, 2, SC], I32)
        pX, pH, pY, pO = ps("pX"), *([ps(f"{n}{r}") for r in range(2)] for n in ("pH", "pY", "pO"))
        (first_rows, other_rows, xn_ready, xt_ps, x_high, x_low, w1_high, w1_low, w2_high, w2_low, h_ps, h_high, h_low,
         y_ps, y_ready, o_ps, o_ready, sent, rows_free) = (sem(x) for x in (
             "first_rows other_rows xn_ready xt_ps x_high x_low w1_high w1_low w2_high w2_low h_ps h_high h_low "
             "y_ps y_ready o_ps o_ready sent rows_free").split())
        w1_landed, w2_landed = ([sem(x + "0"), sem(x + "1")] for x in ("w1_", "w2_"))
        block = ctx.enter_context(nc.Block())
        rows = slots.rearrange("(e p j) d -> p e j d", e=NE, j=SC)

        def experts(eng, step):
            step(0, 0)
            step(1, 1)
            with eng.Fori(1, NE // 2 - 1) as i:
                step(2 * i, 0)
                step(2 * i + 1, 1)
            step(NE - 2, 0)
            step(NE - 1, 1)

        def exists(e):
            return not isinstance(e, int) or 0 <= e < NE


        @block.sync
        def _(sp):
            sp.dma_start(G[:, 0:2], rows[:, 0:2]).then_inc(first_rows, 16)
            for par in range(2):
                sp.dma_start(W1F[:, par], w1[par]).then_inc(w1_landed[par], 16)
                sp.dma_start(W2F[:, par], w2[par]).then_inc(w2_landed[par], 16)
            sp.dma_start(G[:, 2:NE], rows[:, 2:NE]).then_inc(other_rows, 16)
            with sp.Fori(1, NE // 2) as i:
                for par in range(2):
                    e = 2 * i + par
                    sp.wait_ge(w1_low, e - 1)
                    sp.dma_start(W1F[:, par], w1[bass.ds(e, 1)].rearrange("e p n -> (e p) n")).then_inc(w1_landed[par], 16)
                    sp.wait_ge(w2_low, e - 1)
                    sp.dma_start(W2F[:, par], w2[bass.ds(e, 1)].rearrange("e p k d -> (e p) k d")).then_inc(w2_landed[par], 16)

        @block.gpsimd
        def _(pool):
            limit = pool.alloc_register(tag + "last_token")
            pool.reg_mov(limit, B * L - 1)
            last_token = pool.snap(limit)
            pool.sem_inc(rows_free, 2)
            with pool.Fori(0, NE // 2) as i:
                for par in range(2):
                    e = 2 * i + par
                    pool.wait_ge(o_ready, e + 3)
                    pool.nop(nofuse=True)
                    for j in range(SC):
                        pool.indirect_dma_start(
                            out=out, out_offset=bass.IndirectOffsetOnAxis(ap=token[:, par, j:j + 1], axis=0),
                            in_=O[:, par, j, :], in_offset=None, bounds_check=last_token, oob_is_err=False
                        ).then_inc(sent, 16)
                    pool.wait_ge(sent, 16 * SC * (e + 1))
                    pool.sem_inc(rows_free, 1)

        @block.tensor
        def _(pe):
            def product(dst, w, x, start, stop):
                for n, (i, j) in enumerate(PARTS):
                    last = pe.matmul(dst, w[i], x[j], start=start and n == 0, stop=stop and n == len(PARTS) - 1)
                return last

            def transpose_rows(e):
                pe.wait_ge(xn_ready, e + 1)
                pe.wait_ge(x_low, e + 1)
                for j in range(SC):
                    last = pe.transpose(pX[:, P * j:P * j + P], XN[:, j, :], ident[:])
                last.then_inc(xt_ps, 1)

            def hidden(e, par, k):
                if k == 0:
                    pe.wait_ge(x_low, e + 2)
                    pe.wait_ge(w1_low, e + 1)
                pe.wait_ge(h_high, HC * e + k + 1)
                product(pH[k % 2][:], [w[:, par, P * k:P * k + P] for w in W1], [x[:, par, :] for x in XT],
                        True, True).then_inc(h_ps, 1)

            def outer(e, par, k):
                if k == 0:
                    pe.wait_ge(w2_low, e + 1)
                    pe.wait_ge(y_ready, e + 1)
                pe.wait_ge(h_low, HC * e + k + 1 + HC)
                last = product(pY[par][:], [w[:, par, k, :] for w in W2], [h[:, par, k, :] for h in HT], k == 0, k == HC - 1)
                if k == HC - 1:
                    last.then_inc(y_ps, 1)

            def transpose_out(e, par):
                pe.wait_ge(y_ready, e + 3)
                pe.wait_ge(o_ready, e + 1)
                for j in range(SC):
                    last = pe.transpose(pO[par][:, P * j:P * j + P], YT[:, P * j:P * j + P], ident[:])
                last.then_inc(o_ps, 1)

            def step(e, par):
                for k in range(HC):
                    hidden(e, par, k)
                    if exists(e - 1):
                        outer(e - 1, 1 - par, k)
                    if k == 2 and exists(e - 2):
                        transpose_out(e - 2, par)
                    if k == 1 and exists(e + 1):
                        transpose_rows(e + 1)

            pe.sem_inc(xt_ps, 1)
            transpose_rows(0)
            experts(pe, step)
            for k in range(HC):
                outer(NE - 1, 1, k)
                if k == 2:
                    transpose_out(NE - 2, 0)
            transpose_out(NE - 1, 1)

        @block.scalar
        def _(act):
            act.sem_inc(h_high, 2)
            act.sem_inc(y_ready, 2)

            def columns(e, par):
                act.wait_ge(xt_ps, e + 2)
                act.activation(XT[0][:, par, :], pX[:], ACT.Copy).then_inc(x_high, 1)

            def weights(e, par, landed, raw, split, done):
                act.wait_ge(landed[par], (e - par) * 8 + 16)
                act.activation(split[0][:, par], raw[:, par], ACT.Copy).then_inc(done, 1)

            def relus(e, par, k):
                act.wait_ge(h_ps, HC * e + k + 1)
                act.wait_ge(h_low, HC * e + k + 1)
                bias = cols[:, bass.ds(V_FFN + e * HC + k, 1)]
                act.activation(HF[:, k, :], pH[k % 2][:], ACT.Relu, bias=bias)
                act.activation(HT[0][:, par, k, :], pH[k % 2][:], ACT.Relu, bias=bias).then_inc(h_high, 1)

            def outs(e, par):
                act.wait_ge(y_ps, e + 1)
                act.activation(YT[:], pY[par][:], ACT.Identity, bias=cols[:, bass.ds(V_FB2 + e, 1)]).then_inc(y_ready, 1)

            def step(e, par):
                if exists(e - 2):
                    outs(e - 2, par)
                relus(e, par, 0)
                relus(e, par, 1)
                if exists(e + 1):
                    columns(e + 1, 1 - par)
                    weights(e + 1, 1 - par, w1_landed, W1F, W1, w1_high)
                relus(e, par, 2)
                weights(e, par, w2_landed, W2F, W2, w2_high)
                relus(e, par, 3)

            weights(0, 0, w1_landed, W1F, W1, w1_high)
            columns(0, 0)
            experts(act, step)
            outs(NE - 2, 0)
            outs(NE - 1, 1)

        @block.vector
        def _(dve):
            Ge = G[:].rearrange("p e j d -> p (e j) d")
            dve.sem_inc(x_low, 1)
            dve.sem_inc(h_low, HC)
            dve.sem_inc(o_ready, 2)

            def norm(e):
                dve.wait_ge(xt_ps, e + 1)
                for j in range(SC):
                    g = Ge[:, bass.ds(e * SC + j, 1), :].rearrange("p a d -> p (a d)")
                    last = nc.vector.tensor_scalar(XN[:, j, :], g[:, 0:D], g[:, C_MEAN:C_MEAN + 1], g[:, C_RSTD:C_RSTD + 1],
                                                   ALU.subtract, ALU.mult)
                last.then_inc(xn_ready, 1)

            def low_columns(e, par):
                dve.wait_ge(x_high, e + 1)
                nc.vector.tensor_tensor(XT[1][:, par, :], pX[:], f32(XT[0][:, par, :]), ALU.subtract).then_inc(x_low, 1)

            def low_weights(e, par, raw, split, high, done):
                dve.wait_ge(high, e + 1)
                nc.vector.tensor_tensor(split[1][:, par], raw[:, par], f32(split[0][:, par]), ALU.subtract).then_inc(done, 1)

            def low_hidden(e, par, k):
                dve.wait_ge(h_high, HC * e + k + 3)
                nc.vector.tensor_tensor(HT[1][:, par, k, :], HF[:, k, :], f32(HT[0][:, par, k, :]), ALU.subtract
                                        ).then_inc(h_low, 1)

            def add(e, par):
                dve.wait_ge(o_ps, e + 1)
                dve.wait_ge(rows_free, e + 1)
                nc.vector.tensor_copy(token[:, par, :], Ge[:, bass.ds(e * SC, SC), C_TOK].bitcast(I32))
                for j in range(SC):
                    g = Ge[:, bass.ds(e * SC + j, 1), :].rearrange("p a d -> p (a d)")
                    last = nc.vector.scalar_tensor_tensor(O[:, par, j, :], pO[par][:, P * j:P * j + P], g[:, C_GATE:C_GATE + 1],
                                                          g[:, 0:D], ALU.mult, ALU.add)
                last.then_inc(o_ready, 1)

            def step(e, par):
                low_hidden(e, par, 0)
                low_hidden(e, par, 1)
                if exists(e + 1):
                    low_columns(e + 1, 1 - par)
                    low_weights(e + 1, 1 - par, W1F, W1, w1_high, w1_low)
                low_hidden(e, par, 2)
                low_weights(e, par, W2F, W2, w2_high, w2_low)
                low_hidden(e, par, 3)
                if exists(e + 2):
                    if isinstance(e, int) and e == 0:
                        dve.wait_ge(other_rows, 16)
                    norm(e + 2)
                if exists(e - 2):
                    add(e - 2, par)

            dve.wait_ge(first_rows, 16)
            norm(0)
            low_weights(0, 0, W1F, W1, w1_high, w1_low)
            low_columns(0, 0)
            norm(1)
            experts(dve, step)
            add(NE - 2, 0)
            add(NE - 1, 1)


def build(nc, ins, out):
    x1 = nc.dram_tensor("x1", (B * L, D), F32).ap()
    scr = {"filt": nc.dram_tensor("filt_rows", (P, 2, RW), F16).ap(), "x1": x1,
           "slots1": nc.dram_tensor("slots1", (NE * CAP, ROW), F32).ap(),
           "slots2": nc.dram_tensor("slots2", (NE * CAP, ROW), F32).ap()}
    with ExitStack() as ctx:
        sb = lambda n, s, d=F32: ctx.enter_context(nc.sbuf_tensor(n, s, d))
        ident, cols = sb("ident", [P, P]), sb("cols", [P, N_VEC])
        tables = {"ident": ident, "slot": sb("t_slot", [P, 3 * NE]), "token": sb("t_token", [P, NT], I32),
                  "tri16": sb("t_tri", [P, P], BF16), "ones16": sb("t_ones", [P, P], BF16)}
        gatew = {"gate": sb("gate_w", [P, NE]), "gate_b": sb("gate_b", [P, NE])}
        keep = {"ident": ident, "cols": cols, "tables": tables, "gatew": gatew}
        keep["empty"], keep["cleared"] = sb("empty", [P, ROW]), ctx.enter_context(nc.semaphore("cleared"))
        build_tables(nc, ins, scr, keep)
        with ExitStack() as c1:
            keep["ascale"] = c1.enter_context(nc.sbuf_tensor("ascale", [P, B], F32))
            keep["X0T"] = c1.enter_context(nc.sbuf_tensor("X0T", [P, B * L], F32))
            keep["Y"] = c1.enter_context(nc.sbuf_tensor("Y", [P, TB * B, D], F32))
            build_mixer(nc, ins, scr, keep)
            build_mixer_out(nc, ins, scr, keep)
        build_experts(nc, ins, scr["slots1"], x1, keep, "e1_")
        build_recurrent(nc, ins, x1, out, scr["slots2"], keep)
        build_experts(nc, ins, scr["slots2"], out, keep, "e2_")


def build_tables(nc, ins, scr, keep):
    t, g = keep["tables"], keep["gatew"]
    with ExitStack() as ctx:
        tri = ctx.enter_context(nc.sbuf_tensor("tri", [P, P], F32))
        empty = keep["empty"]
        landed = ctx.enter_context(nc.semaphore("tb_landed"))
        block = ctx.enter_context(nc.Block())

        @block.sync
        def _(sp):
            sp.dma_start(tri[:], ins["c_tri"]).then_inc(landed, 16)
            sp.dma_start(t["slot"][:], ins["c_slot"]).then_inc(landed, 16)
            sp.dma_start(g["gate"][:], ins["L0_ffn_Wg"]).then_inc(landed, 16)
            sp.dma_start(g["gate_b"][:], row_to_all(ins["L0_ffn_bg"], NE)).then_inc(landed, 16)
        @block.gpsimd
        def _(pool):
            pool.memset(empty[:, 0:C_TOK], 0.0)
            pool.memset(t["ones16"][:], 1.0)
            pool.iota(t["token"][:], pattern=[[P, NT]], base=0, channel_multiplier=1)
            pool.iota(empty[:, C_TOK:C_TOK + 1].bitcast(I32), pattern=[[0, 1]], base=NO_TOKEN, channel_multiplier=0)

        @block.vector
        def _(dve):
            dve.wait_ge(landed, 64)
            nc.vector.tensor_copy(t["tri16"][:], tri[:])


def build_recurrent(nc, ins, x, out, slots, keep):
    ident, cols = keep["ident"], keep["cols"]
    CT = 4
    CW = CT * P
    NC = B * L // CW
    xin = x.rearrange("(c j p) d -> c p j d", p=P, j=CT)
    xout = out.rearrange("(c j p) d -> c p j d", p=P, j=CT)
    with ExitStack() as ctx:
        sb = lambda n, s, d=F32: ctx.enter_context(nc.sbuf_tensor("b_" + n, s, d))
        sem = lambda n: ctx.enter_context(nc.semaphore("b_" + n))
        ps = lambda n: ctx.enter_context(nc.psum_tensor("b_" + n, [P, FREE], F32))
        parts = lambda n, s: (sb(n + "h", s, F32R), sb(n + "l", s, F32R))
        W1, W2, WZ, WH, WO = parts("w1", [P, EX]), parts("w2", [P, EX]), parts("wz", [P, EC, EX]), parts("wh", [P, EC, EX]), parts("wo", [P, EC, D])
        XB, XN = sb("xb", [P, 2, CT, D]), sb("xn", [P, CT, D])
        XT, XI, S = parts("xt", [P, 2, CW]), parts("xi", [P, 2, EC, CW]), parts("s", [P, EC, CW])
        XF, SF, YT = sb("xf", [P, EC, CW]), sb("sf", [P, EC, CW]), sb("yt", [P, CW])
        SK, H = sb("sk", [P, 2, EC, CW]), sb("h", [P, 2, EC, CW])
        Z, A, BB = sb("z", [P, EC, CW]), sb("a", [P, EC, CW]), sb("bb", [P, EC, CW])
        R = sb("rows", [P, 2, CT, ROW])
        bz2 = sb("bz2", [P, EC])
        st, sm = sb("st", [P, CT, 6]), sb("sm", [P, 4, CT])
        pX, pU, pZ, pH, pY, pO, pS = ps("pX"), [ps("pU0"), ps("pU1")], ps("pZ"), ps("pH"), ps("pY"), ps("pO"), ps("pS")
        (w_landed, w_high, w_low, xn_ready, xt_ps, xth, xtl, up_ps, up_read, xih, xil, z_ps, z_read, a_ready, h_ps,
         b_done, scan_done, s_done, sh, sl, sum_read, y_ps, y_ready, o_ps, rows_ready, chain) = (sem(n) for n in (
             "w_landed w_high w_low xn_ready xt_ps xth xtl up_ps up_read xih xil z_ps z_read a_ready h_ps "
             "b_done scan_done s_done sh sl sum_read y_ps y_ready o_ps rows_ready chain").split())
        x_landed, r_landed, stored = ([sem(n + "0"), sem(n + "1")] for n in ("x_landed", "r_landed", "stored"))
        rt = Router(nc, ctx, CT, 2, R, keep["gatew"], slots, keep["tables"], pX, pS, pS)
        block = ctx.enter_context(nc.Block())
        raw = ((W1, BB[:, 0, :]), (W2, BB[:, 1, :]), (WO, BB[:, 2, :].rearrange("p (k d) -> p k d", k=EC)), (WZ, Z[:]), (WH, A[:]))
        N_RAW, N_UP = len(raw), 2

        def chunks(eng, step):
            step(0, 0)
            step(1, 1)
            with eng.Fori(1, NC // 2 - 1) as i:
                step(2 * i, 0)
                step(2 * i + 1, 1)
            step(NC - 2, 0)
            step(NC - 1, 1)

        def exists(c):
            return not isinstance(c, int) or 0 <= c < NC

        turn = lambda c, par: (c - par) * 8
        one = lambda ap, c: ap[c] if isinstance(c, int) else ap[bass.ds(c, 1)].rearrange("c p j d -> (c p) j d")

        @block.sync
        def _(sp):
            for par in range(2):
                sp.dma_start(XB[:, par], xin[par]).then_inc(x_landed[par], 16)
            for (w, dst), n in zip(raw, ("W1", "W2", "Wo", "Wz", "Wh")):
                src = ins["L0_attn_b_" + n]
                sp.dma_start(dst, src if n in ("W1", "W2") else src.rearrange("(k p) n -> p k n", p=P)).then_inc(w_landed, 16)
            for par in range(2):
                sp.dma_start(R[:, par, :, 0:D], xin[par]).then_inc(r_landed[par], 16)

            def store(c, par):
                sp.wait_ge(rows_ready, c + 1)
                sp.dma_start(one(xout, c), R[:, par, :, 0:D]).then_inc(stored[par], 16)

            def step(c, par):
                if exists(c + 2):
                    sp.wait_ge(xn_ready, c + 1)
                    sp.dma_start(XB[:, par], one(xin, c + 2)).then_inc(x_landed[par], 16)
                if exists(c - 2):
                    store(c - 2, par)
                    sp.wait_ge(stored[par], turn(c, par))
                    sp.wait_ge(rt.rows_free, c + 1)
                    sp.dma_start(R[:, par, :, 0:D], one(xin, c)).then_inc(r_landed[par], 16)

            chunks(sp, step)
            for par in range(2):
                store(NC - 2 + par, par)
            for par in range(2):
                sp.wait_ge(stored[par], 16 * (NC // 2))

        @block.gpsimd
        def _(pool):
            rt.pool_start(pool)

            def step(c, par):
                for m in range(EC):
                    pool.wait_ge(scan_done, EC * c + m + 1 + EC)
                    pool.tensor_tensor(SF[:, m, :], H[:, par, m, :], SK[:, par, m, :], ALU.add).then_inc(s_done, 1)
                    if m == 1 and exists(c - 2):
                        rt.pool_send(pool, c - 2, par)
                        rt.pool_release(pool, c - 2)

            chunks(pool, step)
            for par in range(2):
                rt.pool_send(pool, NC - 2 + par, par)
                rt.pool_release(pool, NC - 2 + par)

        @block.tensor
        def _(pe):
            def product(dst, w, x, start, stop):
                for n, (i, j) in enumerate(PARTS):
                    last = pe.matmul(dst, w[i], x[j], start=start and n == 0, stop=stop and n == len(PARTS) - 1)
                return last

            def transpose_in(c):
                pe.wait_ge(xn_ready, c + 1)
                for j in range(CT):
                    last = pe.transpose(pX[:, P * j:P * j + P], XN[:, j, :], ident[:])
                last.then_inc(xt_ps, 1)

            def up(c, par, m, q):
                if m == 0 and q == 0:
                    pe.wait_ge(xth, c + 1)
                    pe.wait_ge(xtl, c + 1)
                pe.wait_ge(up_read, 2 * EC * c + 2 * m + q + 1)
                W = (W1, W2)[q]
                product(pU[q][:], [w[:, P * m:P * m + P] for w in W], [x[:, par, :] for x in XT], True, True).then_inc(up_ps, 1)

            def gate_block(c, par, m, W, dst, done):
                for k in range(EC):
                    if m == 0 and W is WZ:
                        pe.wait_ge(xih, EC * c + k + 1)
                        pe.wait_ge(xil, EC * c + k + 1)
                    last = product(dst[:], [w[:, k, P * m:P * m + P] for w in W], [x[:, par, k, :] for x in XI],
                                   k == 0, k == EC - 1)
                last.then_inc(done, 1)

            def down(c, ks):
                for k in ks:
                    pe.wait_ge(sh, EC * c + k + 1)
                    pe.wait_ge(sl, EC * c + k + 1)
                    done = product(pY[:], [w[:, k, :] for w in WO], [x[:, k, :] for x in S], k == 0, k == EC - 1)
                done.then_inc(y_ps if k == EC - 1 else sum_read, 1)

            def transpose_out(c):
                pe.wait_ge(y_ready, c + 1)
                if exists(c - 1):
                    pe.wait_ge(rows_ready, c)
                for j in range(CT):
                    done = pe.transpose(pO[:, P * j:P * j + P], YT[:, P * j:P * j + P], ident[:])
                done.then_inc(o_ps, 1)

            def step(c, par):
                for m in range(EC):
                    pe.wait_ge(z_read, EC * c + m + 1)
                    gate_block(c, par, m, WZ, pZ, z_ps)
                    if exists(c - 1):
                        if m == 0:
                            down(c - 1, range(EC - 1))
                        elif m == 1:
                            down(c - 1, [EC - 1])
                        elif m == 3:
                            rt.pe_transpose(pe, c - 1)
                    if m == 1 and exists(c - 2):
                        rt.pe_counts(pe, c - 2)
                    if exists(c + 1):
                        up(c + 1, 1 - par, m, 0)
                    pe.wait_ge(b_done, EC * c + m + 1)
                    gate_block(c, par, m, WH, pH, h_ps)
                    if exists(c - 1):
                        if m == 1:
                            transpose_out(c - 1)
                        elif m == 3:
                            rt.pe_logits(pe, c - 1)
                    if exists(c + 1):
                        up(c + 1, 1 - par, m, 1)
                if exists(c + 2):
                    transpose_in(c + 2)

            pe.sem_inc(xt_ps, 1)
            transpose_in(0)
            pe.wait_ge(w_high, N_UP)
            pe.wait_ge(w_low, N_UP)
            for m in range(EC):
                for q in range(2):
                    up(0, 0, m, q)
            transpose_in(1)
            pe.wait_ge(w_high, N_RAW)
            pe.wait_ge(w_low, N_RAW)
            chunks(pe, step)
            down(NC - 1, range(EC - 1))
            down(NC - 1, [EC - 1])
            rt.pe_counts(pe, NC - 2)
            transpose_out(NC - 1)
            rt.pe_transpose(pe, NC - 1)
            rt.pe_logits(pe, NC - 1)
            rt.pe_counts(pe, NC - 1)

        @block.scalar
        def _(act):
            act.sem_inc(up_read, 2)
            act.sem_inc(z_read, 1)

            def high_weights(first, last):
                for n in range(first, last):
                    act.wait_ge(w_landed, 16 * N_RAW)
                    act.activation(raw[n][0][0][:], raw[n][1], ACT.Copy).then_inc(w_high, 1)

            def high_in(c, par):
                act.wait_ge(xt_ps, c + 2)
                act.activation(XT[0][:, par, :], pX[:], ACT.Copy).then_inc(xth, 1)

            def silu(c, par, m, q):
                act.wait_ge(up_ps, 2 * EC * c + 2 * m + q + 1)
                dst = SK[:, par, m, :] if q else XF[:, m, :]
                bias = (V_B1, V_B2)[q] + m
                act.activation(dst, pU[q][:], ACT.Silu, bias=cols[:, bias:bias + 1]).then_inc(up_read, 1)
                if q == 0:
                    act.wait_ge(up_read, 2 * EC * c + 2 * m + 3)
                    act.activation(XI[0][:, par, m, :], XF[:, m, :], ACT.Copy).then_inc(xih, 1)

            def high_sum(c, m):
                act.wait_ge(s_done, EC * c + m + 1)
                act.activation(S[0][:, m, :], SF[:, m, :], ACT.Copy).then_inc(sh, 1)

            def output(c):
                act.wait_ge(y_ps, c + 1)
                act.activation(YT[:], pY[:], ACT.Identity, bias=cols[:, V_BO:V_BO + 1]).then_inc(y_ready, 1)

            def step(c, par):
                for m in range(EC):
                    act.wait_ge(z_ps, EC * c + m + 1)
                    act.wait_ge(scan_done, EC * c + m + 1)
                    act.activation(Z[:, m, :], pZ[:], ACT.Tanh, scale=0.5, bias=bz2[:, m:m + 1]).then_inc(z_read, 1)
                    act.wait_ge(z_read, EC * c + m + 2)
                    act.activation(A[:, m, :], Z[:, m, :], ACT.Copy, scale=-0.5, bias=0.5)
                    act.activation(Z[:, m, :], Z[:, m, :], ACT.Copy, scale=0.5, bias=0.5).then_inc(a_ready, 1)
                    if m:
                        if m == 1 and exists(c - 1):
                            act.wait_ge(sum_read, c)
                        high_sum(c, m - 1)
                    elif exists(c - 1):
                        high_sum(c - 1, EC - 1)
                    if m == 1 and exists(c - 1):
                        output(c - 1)
                    if exists(c + 1):
                        silu(c + 1, 1 - par, m, 0)
                    if m == 0 and exists(c - 2):
                        rt.act_tanh(act, c - 2)
                    if m == 3 and exists(c - 1):
                        rt.act_transposed(act, c - 1)
                    if exists(c + 1):
                        silu(c + 1, 1 - par, m, 1)
                if exists(c + 2):
                    high_in(c + 2, par)

            high_weights(0, N_UP)
            high_in(0, 0)
            for m in range(EC):
                for q in range(2):
                    silu(0, 0, m, q)
            high_in(1, 1)
            high_weights(N_UP, N_RAW)
            chunks(act, step)
            high_sum(NC - 1, EC - 1)
            rt.act_tanh(act, NC - 2)
            output(NC - 1)
            rt.act_transposed(act, NC - 1)
            rt.act_tanh(act, NC - 1)

        @block.vector
        def _(dve):
            nc.vector.tensor_scalar(bz2[:], cols[:, V_BZ:V_BZ + EC], 0.5, None, ALU.mult)
            dve.sem_inc(b_done, 1)
            dve.sem_inc(scan_done, EC)
            rt.dve_start(dve)
            steps = row_stats_steps(CT)

            def low_weights(first, last):
                for n in range(first, last):
                    (_, low), src = raw[n]
                    dve.wait_ge(w_high, n + 1)
                    nc.vector.tensor_tensor(low[:], src, f32(raw[n][0][0][:]), ALU.subtract).then_inc(w_low, 1)

            def norm(c, par):
                ch = Chain(dve, chain, c * steps)
                dve.wait_ge(x_landed[par], turn(c, par) + 16)
                row_stats(nc, ch, lambda j: XB[:, par, j, :], CT, st, sm)
                assert ch.n == steps
                dve.wait_ge(xt_ps, c + 1)
                for j in range(CT):
                    last = nc.vector.tensor_scalar(XN[:, j, :], XB[:, par, j, :], sm[:, 0, j:j + 1], sm[:, 1, j:j + 1],
                                                   ALU.subtract, ALU.mult)
                last.then_inc(xn_ready, 1)

            def low_in(c, par):
                dve.wait_ge(xth, c + 1)
                nc.vector.tensor_tensor(XT[1][:, par, :], pX[:], f32(XT[0][:, par, :]), ALU.subtract).then_inc(xtl, 1)

            def low_x(c, par, m):
                dve.wait_ge(xih, EC * c + m + 1)
                nc.vector.tensor_tensor(XI[1][:, par, m, :], XF[:, m, :], f32(XI[0][:, par, m, :]), ALU.subtract).then_inc(xil, 1)

            def low_sum(c, m):
                dve.wait_ge(sh, EC * c + m + 1)
                nc.vector.tensor_tensor(S[1][:, m, :], SF[:, m, :], f32(S[0][:, m, :]), ALU.subtract).then_inc(sl, 1)

            def new_rows(c, par):
                dve.wait_ge(o_ps, c + 1)
                dve.wait_ge(r_landed[par], turn(c, par) + 16)
                nc.vector.tensor_tensor(R[:, par, :, 0:D], pO[:].rearrange("p (j d) -> p j d", j=CT), R[:, par, :, 0:D],
                                        ALU.add).then_inc(rows_ready, 1)
                dve.wait_ge(rows_ready, c + 1)
                rt.dve_norm(dve, c, par)

            def step(c, par):
                if exists(c + 1) and not (isinstance(c, int) and c == 0):
                    low_in(c + 1, 1 - par)
                for m in range(EC):
                    if m == 1 and exists(c + 2):
                        norm(c + 2, par)
                    if m == 2 and exists(c - 1):
                        new_rows(c - 1, 1 - par)
                    if m:
                        low_sum(c, m - 1)
                    elif exists(c - 1):
                        low_sum(c - 1, EC - 1)
                    if exists(c + 1):
                        low_x(c + 1, 1 - par, m)
                    dve.wait_ge(h_ps, EC * c + m + 1)
                    dve.wait_ge(a_ready, EC * c + m + 1)
                    nc.vector.scalar_tensor_tensor(BB[:, m, :], pH[:], cols[:, V_BH + m:V_BH + m + 1], Z[:, m, :],
                                                   ALU.add, ALU.mult).then_inc(b_done, 1)
                    dve.wait_ge(b_done, EC * c + m + 2)
                    dve.wait_ge(scan_done, EC * c + m + 1)
                    start = H[:, 0, m, CW - 1:CW] if par else 0.0
                    nc.vector.tensor_tensor_scan(H[:, par, m, :], A[:, m, :], BB[:, m, :], start, ALU.mult, ALU.add
                                                 ).then_inc(scan_done, 1)
                    if exists(c - 2):
                        if m == 0:
                            rt.dve_onehot(dve, c - 2)
                        elif m == 1:
                            rt.dve_slots(dve, c - 2, par)

            norm(0, 0)
            low_weights(0, N_UP)
            low_in(0, 0)
            norm(1, 1)
            for m in range(EC):
                low_x(0, 0, m)
            low_in(1, 1)
            low_weights(N_UP, N_RAW)
            chunks(dve, step)
            low_sum(NC - 1, EC - 1)
            rt.dve_onehot(dve, NC - 2)
            rt.dve_slots(dve, NC - 2, 0)
            new_rows(NC - 1, 1)
            rt.dve_onehot(dve, NC - 1)
            rt.dve_slots(dve, NC - 1, 1)


INPUTS = """L0_attn_a_u L0_attn_a_w_in L0_attn_a_b_in L0_attn_a_sf_w L0_attn_a_sf_b L0_attn_a_f_w1 L0_attn_a_f_b1
L0_attn_a_freq1 L0_attn_a_f_w2 L0_attn_a_f_b2 L0_attn_a_freq2 L0_attn_a_f_w3 L0_attn_a_f_b3 L0_attn_a_freq3
L0_attn_a_f_wout L0_attn_a_filt_bias L0_attn_a_w_out L0_attn_a_b_out L0_attn_b_W1 L0_attn_b_b1 L0_attn_b_W2
L0_attn_b_b2 L0_attn_b_Wz L0_attn_b_bz L0_attn_b_Wh L0_attn_b_bh L0_attn_b_Wo L0_attn_b_bo L0_ffn_Wg L0_ffn_bg
L0_ffn_W1 L0_ffn_b1 L0_ffn_W2 L0_ffn_b2""".split()


def kernel(**inputs):
    import concourse.bacc as bacc
    from concourse.bass_utils import run_bass_kernel_spmd

    nc = bacc.Bacc("TRN2", target_bir_lowering=False, num_devices=1)
    arrays = {n: np.ascontiguousarray(inputs[n]) for n in INPUTS}
    arrays.update(constants())
    ins = {n: nc.dram_tensor("in_" + n, a.shape, mybir.dt.from_np(a.dtype), kind="ExternalInput").ap()
           for n, a in arrays.items()}
    out = nc.dram_tensor("out_0", (B * L, D), F32, kind="ExternalOutput").ap()
    build(nc, ins, out)
    r = run_bass_kernel_spmd(nc, [{"in_" + n: a for n, a in arrays.items()}], core_ids=[0])
    return r.results[0]["out_0"].reshape(B, L, D)
```

```python
import math
from contextlib import ExitStack

import numpy as np

import concourse.bass as bass
from concourse import mybir

F32 = mybir.dt.float32
F32R = mybir.dt.float32r
BF16 = mybir.dt.bfloat16
F16 = mybir.dt.float16
I32 = mybir.dt.int32
ALU = mybir.AluOpType
ACT = mybir.ActivationFunctionType
AX = mybir.AxisListType

P = 128
B, L, D = 8, 1024, 128
PARTS = ((0, 0), (0, 1), (1, 0))
NT = B * L // P
TB = L // P
FL, FO = 512, 64
SHIFT = 0.05
EPS = 1e-5
NE, CAP, HID = 16, 512, 512
HC = HID // P
SC = CAP // P
ROW = 132
C_MEAN, C_RSTD, C_GATE, C_TOK = 128, 129, 130, 131
NO_TOKEN = 1 << 20
EX = 512
EC = EX // P
CH = 8
NG = D // CH
RING = 4
RW = 768
TW = 640
HP = P // 2
FREE = 512

V_BIN, V_SFB, V_FBIAS, V_B1, V_B2, V_BZ, V_BH, V_FFN, V_F, V_FB2, V_BO = 0, 3, 6, 7, 11, 15, 19, 23, 87, 93, 109
N_VEC = 110
N_VEC_DMAS = 1 + 3 + 4 + 3 + 6
N_W_DMAS = 6 + 2
TWO_PI = 2.0 * math.pi
TURN_PARTS = (6.28125, float(np.float32(TWO_PI - 6.28125)))
ROUNDER = 1.5 * 2.0 ** 23
PI_BELOW = 3.1415925


def constants():
    t = np.linspace(0.0, 1.0, FL).astype(np.float32)
    tr = np.linspace(0.0, FL - 1.0, FL).astype(np.float32)
    w = (np.float32(2.0 * np.pi) * tr / np.float32(FL)).astype(np.float32)
    fw = (np.float32(1e-4) * w).astype(np.float32)
    z = np.stack([t, np.cos(fw), -np.sin(fw)]).astype(np.float32)
    deltas = np.abs(np.linspace(math.log(0.01) / 1.5, math.log(0.01) / 0.3, D).astype(np.float32))
    decay = (np.exp(-t[None, :] * deltas[:, None]) + np.float32(SHIFT)).astype(np.float32)
    e = np.arange(NE, dtype=np.float32)
    slot0 = np.concatenate([CAP * e - 1, CAP * (e + 1) - 1, NE - e])
    return {
        "c_z": np.ascontiguousarray(z[:, ::-1]),
        "c_decay": np.ascontiguousarray(decay[:, ::-1]),
        "c_ident": np.eye(P, dtype=np.float32),
        "c_tri": np.triu(np.ones((P, P), np.float32)),
        "c_slot": np.ascontiguousarray(np.broadcast_to(slot0, (P, 3 * NE)).astype(np.float32)),
    }


class Chain:

    def __init__(self, eng, sem, base=0):
        self.eng, self.sem, self.base, self.n = eng, sem, base, 0

    def step(self, ins):
        self.n += 1
        ins.then_inc(self.sem, 1)

    def wait(self):
        self.eng.wait_ge(self.sem, self.base + self.n)

    def link(self, ins):
        self.step(ins)
        self.wait()


def f32(ap):
    return ap.bitcast(F32)


def reversed_tiles(ap2, n):
    a = ap2.rearrange("p (j m) -> p j m", j=n)
    return bass.AP(tensor=a.tensor, offset=a.offset + P - 1,
                   ap=[list(a.ap[0]), list(a.ap[1]), [-1, P]])


def rsqrt_steps(nc, ch, y, t, v, half_magic=1597463007.0):
    vi, yi = v.bitcast(I32), y.bitcast(I32)
    ch.link(nc.vector.tensor_scalar(yi, vi, 1, None, ALU.logical_shift_right))
    ch.link(nc.vector.tensor_scalar(yi, yi, -1.0, half_magic, ALU.mult, ALU.add))
    for _ in range(3):
        ch.link(nc.vector.tensor_tensor(t, y, y, ALU.mult))
        ch.link(nc.vector.scalar_tensor_tensor(t, t, -0.5, v, ALU.mult, ALU.mult))
        ch.link(nc.vector.scalar_tensor_tensor(y, t, 1.5, y, ALU.add, ALU.mult))


RSQRT_STEPS = 11


def power_of_two_scale(nc, ch, top, p, scale):
    ch.link(nc.vector.tensor_scalar(p, top, 2.0 ** -100, None, ALU.max))
    ch.link(nc.vector.tensor_scalar(p.bitcast(I32), p.bitcast(I32), 0x7F800000, None, ALU.bitwise_and))
    ch.link(nc.vector.tensor_scalar(p, p, 2.0 ** -13, None, ALU.mult))
    ch.link(nc.vector.reciprocal(scale, p))


SCALE_STEPS = 4


def row_stats(nc, ch, x_of, n, st, sm):
    row_sums(nc, ch, x_of, n, st)
    row_stats_end(nc, ch, st, sm)


def row_sums(nc, ch, x_of, n, st):
    for j in range(n):
        ch.step(nc.vector.bn_stats(st[:, j, :], x_of(j)))


def row_stats_end(nc, ch, st, sm):
    ch.wait()
    mean, rstd, var, tmp = (sm[:, k, :] for k in range(4))
    ch.step(nc.vector.tensor_tensor(mean, st[:, :, 1], st[:, :, 4], ALU.add))
    ch.step(nc.vector.tensor_tensor(tmp, st[:, :, 1], st[:, :, 4], ALU.subtract))
    ch.link(nc.vector.tensor_tensor(var, st[:, :, 2], st[:, :, 5], ALU.add))
    ch.step(nc.vector.tensor_scalar(mean, mean, 0.5, None, ALU.mult))
    ch.step(nc.vector.tensor_tensor(tmp, tmp, tmp, ALU.mult))
    ch.link(nc.vector.tensor_scalar(var, var, 1.0 / D, EPS, ALU.mult, ALU.add))
    ch.link(nc.vector.scalar_tensor_tensor(var, tmp, 0.25, var, ALU.mult, ALU.add))
    rsqrt_steps(nc, ch, rstd, tmp, var)
    ch.link(nc.vector.scalar_tensor_tensor(var, mean, -1.0, rstd, ALU.mult, ALU.mult))


TAPS_STEPS = 2
SPLIT_STEPS = 1 + SCALE_STEPS


def row_stats_steps(n):
    return n + 8 + RSQRT_STEPS


class Router:

    def __init__(self, nc, ctx, n, bufs, R, w, slots, tables, pT, pL, pC, scalar_norm):
        self.scalar_norm = scalar_norm
        sb = lambda name, shape, d=F32: ctx.enter_context(nc.sbuf_tensor(f"{name}{n}", shape, d))
        sem = lambda name: ctx.enter_context(nc.semaphore(f"{name}_{n}"))
        self.bufs = bufs
        self.nc, self.n, self.R, self.w, self.slots, self.t = nc, n, R, w, slots, tables
        self.pT = pT
        self.pL = pL[:, 0:n * NE].rearrange("p (j e) -> p j e", e=NE)
        self.pC = pC[:, 128:128 + n * NE]
        self.pD = pC[:, 256:256 + NE]
        self.XN = sb("r_xn", [P, n, D])
        self.XNT = sb("r_xnt", [P, n * P])
        self.st = sb("r_st", [P, n, 6])
        self.sm = sb("r_sm", [P, 8, n])
        self.lg = sb("r_lg", [P, 4, n, NE])
        self.oh = sb("r_oh", [P, n * NE], BF16)
        self.base = sb("r_base", [P, NE])
        self.idx = sb("r_idx", [P, bufs, n], I32)
        self.stats, self.xn, self.xt_ps, self.xt, self.lg_ps, self.small, self.onehot, self.expin, self.exped, \
            self.count_ps, self.done = (sem("r_" + x) for x in (
                "stats", "xn", "xt_ps", "xt", "lg_ps", "small", "onehot", "expin", "exped", "count_ps", "done"))
        self.sent, self.rows_free = sem("r_sent"), sem("r_rows_free")

    STEPS2 = 5
    STEPS3 = 8

    def dve_start(self, dve):
        self.nc.vector.tensor_copy(self.base[:], self.t["slot"][:, 0:NE]).then_inc(self.small, 1)
        dve.wait_ge(self.small, 1)

    def dve_norm(self, dve, r, par):
        nc, n, R = self.nc, self.n, self.R[:, par]
        steps = row_stats_steps(n)
        if self.scalar_norm and not (isinstance(r, int) and r == 0):
            dve.wait_ge(self.xn, r)
        ch = Chain(dve, self.stats, r * steps)
        row_stats(nc, ch, lambda j: R[:, j, 0:D], n, self.st, self.sm)
        assert ch.n == steps
        if not self.scalar_norm:
            for j in range(n):
                last = nc.vector.tensor_scalar(self.XN[:, j, :], R[:, j, 0:D], self.sm[:, 0, j:j + 1], self.sm[:, 1, j:j + 1],
                                               ALU.subtract, ALU.mult)
            last.then_inc(self.xn, 1)
        nc.vector.tensor_copy(R[:, :, C_MEAN], self.sm[:, 0, :])
        nc.vector.tensor_copy(R[:, :, C_RSTD], self.sm[:, 1, :])
        nc.vector.tensor_copy(R[:, :, C_TOK].bitcast(I32), self.t["token"][:, bass.ds(r * n, n)])

    def pe_start(self, pe):
        pe.sem_inc(self.xt_ps, 1)

    def pe_transpose(self, pe, r):
        pe.wait_ge(self.xn, r + 1)
        for j in range(self.n):
            last = pe.transpose(self.pT[:, P * j:P * j + P], self.XN[:, j, :], self.t["ident"][:])
        last.then_inc(self.xt_ps, 1)

    def pe_logits(self, pe, r):
        pe.wait_ge(self.xt, r + 1)
        for j in range(self.n):
            last = pe.matmul(self.pL[:, j, :], self.XNT[:, P * j:P * j + P], self.w["gate"][:], start=True, stop=True)
        last.then_inc(self.lg_ps, 1)

    def act_norm(self, act, r, par):
        act.wait_ge(self.stats, (r + 1) * row_stats_steps(self.n))
        act.wait_ge(self.xt_ps, r + 1)
        for j in range(self.n):
            last = act.activation(self.XN[:, j, :], self.R[:, par, j, 0:D], ACT.Identity,
                                  scale=self.sm[:, 1, j:j + 1], bias=self.sm[:, 2, j:j + 1])
        last.then_inc(self.xn, 1)

    def act_transposed(self, act, r):
        act.wait_ge(self.xt_ps, r + 2)
        act.activation(self.XNT[:], self.pT[:], ACT.Copy).then_inc(self.xt, 1)

    def dve_onehot(self, dve, r):
        nc, n, t = self.nc, self.n, self.t
        wide = lambda ap: ap.unsqueeze(1).broadcast_to([P, n, NE])
        tall = lambda ap: ap.unsqueeze(2).broadcast_to([P, n, NE])
        lg, top, first = self.lg, self.sm[:, 4, :], self.sm[:, 5, :]
        ch = Chain(dve, self.small, 1 + r * (self.STEPS2 + self.STEPS3 + 1))
        dve.wait_ge(self.lg_ps, r + 1)
        ch.link(nc.vector.tensor_tensor(lg[:, 0], self.pL, wide(self.w["gate_b"][:]), ALU.add))
        ch.link(nc.vector.tensor_reduce(top, lg[:, 0], AX.X, ALU.max))
        nc.vector.tensor_tensor(lg[:, 1], lg[:, 0], tall(top), ALU.subtract).then_inc(self.expin, 1)
        ch.link(nc.vector.tensor_tensor(lg[:, 2], lg[:, 0], tall(top), ALU.is_equal))
        ch.link(nc.vector.tensor_tensor(lg[:, 2], lg[:, 2], wide(t["slot"][:, 2 * NE:3 * NE]), ALU.mult))
        ch.link(nc.vector.tensor_reduce(first, lg[:, 2], AX.X, ALU.max))
        assert ch.n == self.STEPS2
        nc.vector.tensor_tensor(self.oh[:].rearrange("p (j e) -> p j e", e=NE), lg[:, 2], tall(first),
                                ALU.is_equal).then_inc(self.onehot, 1)

    def act_tanh(self, act, r):
        act.wait_ge(self.expin, r + 1)
        act.activation(self.lg[:, 1], self.lg[:, 1], ACT.Tanh, scale=0.5).then_inc(self.exped, 1)

    def pe_counts(self, pe, r):
        pe.wait_ge(self.onehot, r + 1)
        n, oh, t = self.n, self.oh, self.t
        for k in range(n):
            pe.matmul(self.pC[:, NE * k:], t["tri16"][:] if k == 0 else t["ones16"][:], oh[:, 0:NE * (n - k)],
                      start=k == 0, stop=k == n - 1)
        for k in range(n):
            last = pe.matmul(self.pD, t["ones16"][:], oh[:, NE * k:NE * k + NE], start=k == 0, stop=k == n - 1)
        last.then_inc(self.count_ps, 1)

    def dve_slots(self, dve, r, par):
        nc, n, t, lg = self.nc, self.n, self.t, self.lg
        wide = lambda ap: ap.unsqueeze(1).broadcast_to([P, n, NE])
        base = 1 + r * (self.STEPS2 + self.STEPS3 + 1) + self.STEPS2
        ch = Chain(dve, self.small, base)
        q, over = lg[:, 2], lg[:, 3]
        dve.wait_ge(self.exped, r + 1)
        dve.wait_ge(self.count_ps, r + 1)
        ch.link(nc.vector.tensor_scalar(q, lg[:, 1], -1.0, 1.0, ALU.mult, ALU.add))
        ch.link(nc.vector.reciprocal(over, q))
        ch.link(nc.vector.scalar_tensor_tensor(over, lg[:, 1], 1.0, over, ALU.add, ALU.mult))
        ch.link(nc.vector.tensor_reduce(self.sm[:, 6, :], over, AX.X, ALU.add))
        nc.vector.reciprocal(self.R[:, par, :, C_GATE], self.sm[:, 6, :])
        ch.link(nc.vector.tensor_tensor(q, self.pC.rearrange("p (j e) -> p j e", e=NE), wide(self.base[:]), ALU.add))
        ch.step(nc.vector.tensor_tensor(self.base[:], self.base[:], self.pD, ALU.add))
        ch.link(nc.vector.tensor_tensor(over, q, wide(t["slot"][:, NE:2 * NE]), ALU.is_gt))
        ch.link(nc.vector.scalar_tensor_tensor(q, over, float(NO_TOKEN), q, ALU.mult, ALU.add))
        assert ch.n == self.STEPS3
        ch.link(nc.vector.tensor_tensor(q, q, self.oh[:].rearrange("p (j e) -> p j e", e=NE), ALU.mult))
        nc.vector.tensor_reduce(self.idx[:, par, :], q, AX.X, ALU.max).then_inc(self.done, 1)

    def pool_start(self, pool):
        limit = pool.alloc_register(f"last_slot{self.n}")
        pool.reg_mov(limit, NE * CAP - 1)
        self.last_slot = pool.snap(limit)
        pool.sem_inc(self.rows_free, self.bufs)

    def pool_send(self, pool, r, par):
        pool.wait_ge(self.done, r + 1)
        pool.nop(nofuse=True)
        for j in range(self.n):
            pool.indirect_dma_start(out=self.slots, out_offset=bass.IndirectOffsetOnAxis(ap=self.idx[:, par, j:j + 1], axis=0),
                                    in_=self.R[:, par, j, :], in_offset=None, bounds_check=self.last_slot,
                                    oob_is_err=False).then_inc(self.sent, 16)

    def pool_release(self, pool, r):
        pool.wait_ge(self.sent, 16 * self.n * (r + 1))
        pool.sem_inc(self.rows_free, 1)


def build_mixer_out(nc, ins, scr, keep):
    X0T, Y, ident, ascale = keep["X0T"], keep["Y"], keep["ident"], keep["ascale"]
    u = ins["L0_attn_a_u"].rearrange("b (j p) d -> b p j d", p=P)
    xout = scr["x1"].rearrange("(b j p) d -> b p j d", p=P, j=TB)
    BUFS = 3
    with ExitStack() as ctx:
        sb = lambda n, s, d=F32: ctx.enter_context(nc.sbuf_tensor(n, s, d))
        sem = lambda n: ctx.enter_context(nc.semaphore(n))
        ps = lambda n, s: ctx.enter_context(nc.psum_tensor(n, s, F32))
        w_out, b_out = sb("w_out", [P, D]), sb("b_out", [P, D])
        U = sb("o_u", [P, BUFS, TB, D])
        R = sb("o_rows", [P, BUFS, TB, ROW])
        YS, ZT = sb("o_ys", [P, TB, D]), sb("o_zt", [P, L])
        pZ, pO, pX, pS, pC = ps("pZ", [P, L]), ps("pO", [P, L]), ps("pX", [P, L]), ps("pS", [P, FREE]), ps("pC", [P, FREE])
        w_landed, ys_ready, z_ps, z_ready, o_ps, ub_ready, rows_ready = (
            sem("o_" + x) for x in ("w_landed", "ys_ready", "z_ps", "z_ready", "o_ps", "ub_ready", "rows_ready"))
        u_landed, stored = ([sem(f"o_{x}{k}") for k in range(BUFS)] for x in ("u_landed", "stored"))
        rt = Router(nc, ctx, TB, BUFS, R, keep["gatew"], scr["slots1"], keep["tables"], pX, pS, pC, True)
        block = ctx.enter_context(nc.Block())

        def batches(eng, step):
            step(0, 0, 0, True, False)
            with eng.Fori(0, (B - 2) // BUFS) as i:
                for j in range(1, BUFS + 1):
                    step(BUFS * i + j, j % BUFS, i + j // BUFS, False, False)
            step(B - 1, (B - 1) % BUFS, (B - 1) // BUFS, False, True)

        before = lambda k: (k + BUFS - 1) % BUFS
        after = lambda k: (k + 1) % BUFS
        one = lambda ap, b: ap[b] if isinstance(b, int) else ap[bass.ds(b, 1)].rearrange("b p j d -> (b p) j d")

        @block.sync
        def _(sp):
            sp.dma_start(U[:, 0], u[0]).then_inc(u_landed[0], 16)
            sp.dma_start(w_out[:], ins["L0_attn_a_w_out"]).then_inc(w_landed, 16)
            sp.dma_start(b_out[:], row_to_all(ins["L0_attn_a_b_out"], D)).then_inc(w_landed, 16)
            for k in range(BUFS):
                sp.sem_inc(stored[k], 16)

            def step(b, k, n, first, last):
                if not last:
                    sp.dma_start(U[:, after(k)], one(u, b + 1)).then_inc(u_landed[after(k)], 16)
                sp.wait_ge(rows_ready, b + 1)
                sp.dma_start(one(xout, b), R[:, k, :, 0:D]).then_inc(stored[k], 16)

            batches(sp, step)
            for k in range(BUFS):
                sp.wait_ge(stored[k], 16 + 16 * len(range(k, B, BUFS)))

        @block.gpsimd
        def _(pool):
            rt.pool_start(pool)

            def add_bias(b, k, n):
                pool.wait_ge(u_landed[k], 16 * n + 16)
                pool.tensor_tensor(U[:, k], U[:, k], b_out[:].unsqueeze(1).broadcast_to([P, TB, D]), ALU.add).then_inc(ub_ready, 1)

            def step(b, k, n, first, last):
                if not last:
                    add_bias(b + 1, after(k), n + (k == BUFS - 1))
                if not first:
                    rt.pool_send(pool, b - 1, before(k))
                    rt.pool_release(pool, b - 1)

            pool.wait_ge(keep["cleared"], 32)
            pool.wait_ge(w_landed, 32)
            add_bias(0, 0, 0)
            batches(pool, step)
            rt.pool_send(pool, B - 1, (B - 1) % BUFS)
            rt.pool_release(pool, B - 1)

        @block.scalar
        def _(act):
            def copy_y(b):
                act.wait_ge(z_ps, b + 1)
                act.activation(YS[:], Y[:].rearrange("p (j b) d -> p j b d", b=B)[:, :, bass.ds(b, 1), :]
                               .rearrange("p j b d -> p j (b d)"), ACT.Copy).then_inc(ys_ready, 1)

            def step(b, k, n, first, last):
                if not first:
                    rt.act_transposed(act, b - 1)
                if not last:
                    copy_y(b + 1)
                rt.act_norm(act, b, k)
                if not first:
                    rt.act_tanh(act, b - 1)

            copy_y(0)
            batches(act, step)
            rt.act_transposed(act, B - 1)
            rt.act_tanh(act, B - 1)

        @block.tensor
        def _(pe):
            def transpose_y(b):
                pe.wait_ge(ys_ready, b + 1)
                for j in range(TB):
                    last = pe.transpose(pZ[:, P * j:P * j + P], YS[:, j, :], ident[:])
                last.then_inc(z_ps, 1)

            def step(b, k, n, first, last):
                pe.wait_ge(z_ready, b + 1)
                for j in range(TB):
                    mm = pe.matmul(pO[:, P * j:P * j + P], ZT[:, P * j:P * j + P], w_out[:], start=True, stop=True)
                mm.then_inc(o_ps, 1)
                if not first:
                    rt.pe_transpose(pe, b - 1)
                if not last:
                    transpose_y(b + 1)
                if not first:
                    rt.pe_logits(pe, b - 1)
                    rt.pe_counts(pe, b - 1)

            pe.sem_inc(z_ps, 1)
            rt.pe_start(pe)
            pe.wait_ge(w_landed, 32)
            transpose_y(0)
            batches(pe, step)
            rt.pe_transpose(pe, B - 1)
            rt.pe_logits(pe, B - 1)
            rt.pe_counts(pe, B - 1)

        @block.vector
        def _(dve):
            rt.dve_start(dve)

            def gate_y(b):
                dve.wait_ge(z_ps, b + 2)
                nc.vector.scalar_tensor_tensor(
                    ZT[:].rearrange("p (j m) -> p j m", j=TB), reversed_tiles(pZ[:], TB), ascale[:, bass.ds(b, 1)],
                    X0T[:, bass.ds(b * L, L)].rearrange("p (j m) -> p j m", j=TB), ALU.mult, ALU.mult
                ).then_inc(z_ready, 1)

            def step(b, k, n, first, last):
                dve.wait_ge(o_ps, b + 1)
                dve.wait_ge(ub_ready, b + 1)
                dve.wait_ge(stored[k], 16 * n + 16)
                dve.wait_ge(rt.rows_free, b + 1)
                nc.vector.tensor_tensor(R[:, k, :, 0:D], pO[:].rearrange("p (j d) -> p j d", j=TB), U[:, k],
                                        ALU.add).then_inc(rows_ready, 1)
                dve.wait_ge(rows_ready, b + 1)
                rt.dve_norm(dve, b, k)
                if not first:
                    rt.dve_onehot(dve, b - 1)
                if not last:
                    gate_y(b + 1)
                if not first:
                    rt.dve_slots(dve, b - 1, before(k))

            gate_y(0)
            batches(dve, step)
            rt.dve_onehot(dve, B - 1)
            rt.dve_slots(dve, B - 1, (B - 1) % BUFS)


def row_to_all(ap, n):
    return bass.AP(tensor=ap.tensor, offset=ap.offset, ap=[[0, P], [1, n]])


def build_mixer(nc, ins, scr, keep):
    u = ins["L0_attn_a_u"].rearrange("b (j p) d -> b p j d", p=P)
    with ExitStack() as ctx:
        sb = lambda n, s, d=F32: ctx.enter_context(nc.sbuf_tensor(n, s, d))
        sem = lambda n: ctx.enter_context(nc.semaphore(n))
        X0T, ident, cols = keep["X0T"], keep["ident"], keep["cols"]
        Y = keep["Y"]
        VT = sb("VT", [P, 2, TB, B, D], F16)
        toep = sb("toep", [P, RING, CH, 2, TW + HP], F16)
        ascale = keep["ascale"]
        toep_landed = [sem(f"toep_landed{r}") for r in range(RING)]

        def load_toeplitz(eng, g, r):
            a = scr["filt"]
            src = bass.AP(tensor=a.tensor, offset=a.offset + g * (CH * 2 * RW), ap=[[1, HP], [RW, 2 * CH], [1, TW + HP]])
            p = HP * (r % 2)
            eng.dma_start(toep[p:p + HP, r].rearrange("p c h x -> p (c h) x"), src).then_inc(toep_landed[r], 16)

        def fill_toeplitz(r):
            tiles = toep[:, r].rearrange("p c h x -> p (c h) x")
            if r % 2:
                nc.vector.tensor_copy(tiles[0:HP, :, HP:HP + TW], tiles[HP:P, :, 0:TW])
            else:
                nc.vector.tensor_copy(tiles[HP:P, :, 0:TW], tiles[0:HP, :, HP:HP + TW])

        with ExitStack() as c1:
            sb1 = lambda n, s, d=F32: c1.enter_context(nc.sbuf_tensor(n, s, d))
            ps1 = lambda n, s: c1.enter_context(nc.psum_tensor(n, s, F32))
            sem1 = lambda n: c1.enter_context(nc.semaphore(n))
            fscale = sb1("fscale", [P, 4])
            vscale = sb1("vscale", [P, 4])
            VP = sb1("VP", [P, 2, L], F16)
            X0TMP = sb1("X0TMP", [P, L])
            ident16 = sb1("ident16", [P, P], F16)
            sfw = sb1("sfw", [P, 3, 3])
            U = sb1("U", [P, 2, TB, D])
            XN = sb1("XN", [P, TB, D])
            XNT = X0T[:, (B - 1) * L:B * L]
            spare = Y[:].rearrange("p n d -> p (n d)")
            TAP = spare[:, 0:3 * L].rearrange("p (g l) -> p g l", g=3)
            VV = spare[:, 3 * L:4 * L]
            w_in = spare[:, TB * B * D - 3 * D:TB * B * D]
            UP = spare[:, 4 * L:4 * L + 3 * (L + 2)].rearrange("p (g l) -> p g l", g=3)
            temp = toep[:, RING - 1].rearrange("p c h x -> p (c h x)").bitcast(F32)
            z, decay, frow = temp[0:3, 0:FL], temp[:, FL:2 * FL], temp[:, 2 * FL:2 * FL + RW]
            fh = temp[0:FO, 4 * FL:6 * FL].rearrange("f (n t) -> f n t", n=2)
            fq = temp[0:FO, 6 * FL:8 * FL].rearrange("f (n t) -> f n t", n=2)
            vecs = temp[0:N_VEC, 8 * FL:8 * FL + P]
            at = 8 * FL + P
            fparts = temp[:, at:at + RW].bitcast(F16).rearrange("p (h x) -> p h x", h=2)
            at += RW
            fw1, fw23 = temp[0:3, at:at + FO], temp[0:FO, at + FO:at + 3 * FO].rearrange("f (n o) -> f n o", n=2)
            fwout = temp[0:FO, at + 3 * FO:at + 3 * FO + D]
            st = sb1("st", [P, TB, 6])
            sm = sb1("sm", [P, 4, TB])
            pT = ps1("pT", [P, 2 * FREE])
            pV = pT[:].bitcast(F16).rearrange("p (h j d) -> p h j d", h=2, j=TB)
            pP = [ps1(f"pP{g}", [P, 2 * FREE]) for g in range(3)]

            zeroed, consts_in = sem1("zeroed"), sem1("consts_in")
            cols_ps, cols_ready, fl_ps, fl_ready = (sem1(n) for n in ("cols_ps", "cols_ready", "fl_ps", "fl_ready"))
            fl_chain, fl_arg, frow_ready = (sem1(n) for n in ("fl_chain", "fl_arg", "frow_ready"))
            w_landed = sem1("w_landed")
            u_landed = [sem1("u_landed0"), sem1("u_landed1")]
            xn_ready, xnt_ps, xnt_ready, proj_ps, up_ready = (
                sem1(n) for n in ("xn_ready", "xnt_ps", "xnt_ready", "proj_ps", "up_ready"))
            tap0_ready, tap_done, vv_ready, vt_ps, vt_ready = (
                sem1(n) for n in ("tap0_ready", "tap_done", "vv_ready", "vt_ps", "vt_ready"))
            n_chain, t_chain, s_chain, p_chain = (sem1(n) for n in ("n_chain", "t_chain", "s_chain", "p_chain"))
            x0_done, vhi_ready, vlo_ready = (
                sem1(n) for n in ("x0_done", "vhi_ready", "vlo_ready"))
            block = c1.enter_context(nc.Block())
            ORDER = (1, 2, 0)

            @block.sync
            def _(sp):
                for par in range(2):
                    sp.dma_start(U[:, par], u[par]).then_inc(u_landed[par], 16)
                sp.wait_ge(zeroed, 1)
                row = lambda name, r, n: sp.dma_start(
                    vecs[r:r + n, :], ins[name].rearrange("(k p) -> k p", p=P)).then_inc(consts_in, 16)
                sp.dma_start(ident[:], ins["c_ident"]).then_inc(consts_in, 16)
                row("L0_attn_a_b_in", V_BIN, 3)
                row("L0_attn_a_sf_b", V_SFB, 3)
                row("L0_attn_a_filt_bias", V_FBIAS, 1)
                row("L0_attn_b_b1", V_B1, EC)
                row("L0_attn_b_b2", V_B2, EC)
                row("L0_attn_b_bz", V_BZ, EC)
                row("L0_attn_b_bh", V_BH, EC)
                sp.dma_start(vecs[V_FFN:V_FFN + NE * HC, :],
                             ins["L0_ffn_b1"].rearrange("e (k p) -> (e k) p", p=P)).then_inc(consts_in, 16)
                sp.dma_start(vecs[V_FB2:V_FB2 + NE, :], ins["L0_ffn_b2"]).then_inc(consts_in, 16)
                row("L0_attn_b_bo", V_BO, 1)
                for n, name in enumerate(("f_b1", "freq1", "f_b2", "freq2", "f_b3", "freq3")):
                    sp.dma_start(vecs[V_F + n:V_F + n + 1, 0:FO],
                                 ins["L0_attn_a_" + name].rearrange("(a n) -> a n", a=1)).then_inc(consts_in, 16)

                def load_u(b):
                    sp.wait_ge(xn_ready, 2 * b - 2)
                    sp.dma_start(U[:, b % 2], u[b]).then_inc(u_landed[b % 2], 16)

                load_u(2)
                sp.wait_ge(frow_ready, 1)
                sp.dma_start(scr["filt"], fparts).then_inc(consts_in, 16)
                load_u(3)
                sp.wait_ge(consts_in, 16 * N_VEC_DMAS + 16)
                for r in range(RING):
                    load_toeplitz(sp, r, r)
                    load_u(4 + r)
                for n in ("slots1", "slots2"):
                    sp.dma_start(scr[n].rearrange("(p q) d -> p q d", p=P),
                                 keep["empty"][:].unsqueeze(1).broadcast_to([P, NE * CAP // P, ROW])
                                 ).then_inc(keep["cleared"], 16)


            @block.gpsimd
            def _(pool):
                pool.memset(vecs, 0.0).then_inc(zeroed, 1)
                pool.memset(frow, 0.0).then_inc(zeroed, 1)
                pool.memset(UP[:, :, 0:2], 0.0).then_inc(zeroed, 1)
                pool.wait_ge(w_landed, 16 * N_W_DMAS)
                pool.sem_inc(vv_ready, 1)
                pool.sem_inc(x0_done, 1)
                with pool.Fori(0, B) as b:
                    ch = Chain(pool, p_chain, 3 * b)
                    pool.wait_ge(tap_done, 2 * b + 4)
                    pool.wait_ge(vhi_ready, b + 1)
                    pool.wait_ge(vlo_ready, b + 1)
                    pool.tensor_tensor(VV, TAP[:, 1, :], TAP[:, 2, :], ALU.mult).then_inc(vv_ready, 1)
                    pool.wait_ge(tap0_ready, 3 * b + 3)
                    ch.link(pool.tensor_tensor(X0TMP[:], UP[:, 0, 1:L + 1], sfw[:, 0, 1:2].broadcast_to([P, L]), ALU.mult))
                    ch.link(pool.tensor_tensor(TAP[:, 0, :], TAP[:, 0, :], X0TMP[:], ALU.add))
                    ch.link(pool.tensor_tensor(X0TMP[:], UP[:, 0, 0:L], sfw[:, 0, 0:1].broadcast_to([P, L]), ALU.mult))
                    pool.tensor_tensor(X0T[:, bass.ds(b * L, L)], TAP[:, 0, :], X0TMP[:], ALU.add).then_inc(x0_done, 1)

            @block.tensor
            def _(pe):
                pe.sem_inc(vt_ps, 1)
                pe.sem_inc(xnt_ps, 2)
                pe.sem_inc(proj_ps, 3)

                def filter_layer(n):
                    w, x, outs = ((fw1, z, FO), (fw23[:, 0, :], fh[:, 0, :], FO), (fw23[:, 1, :], fh[:, 1, :], FO),
                                  (fwout, fh[:, 0, :], P))[n]
                    if n:
                        pe.wait_ge(fl_ready, n)
                    else:
                        pe.wait_ge(w_landed, 16 * N_W_DMAS)
                    pe.matmul(pP[0][0:outs, 0:FL], w, x, start=True, stop=True).then_inc(fl_ps, 1)

                def transpose_x(b, free):
                    pe.wait_ge(xn_ready, 2 * b + 2)
                    if not free:
                        pe.wait_ge(vt_ready, b - 1)
                    for h in range(2):
                        for j in range(4 * h, 4 * h + 4):
                            last = pe.transpose(pT[:, P * j:P * j + P], XN[:, j, :], ident[:])
                        last.then_inc(xnt_ps, 1)

                def project(b, ns):
                    for n in ns:
                        g = ORDER[n]
                        pe.wait_ge(up_ready, 3 * b + n + 1)
                        for h in range(2):
                            if n == 0:
                                pe.wait_ge(xnt_ready, 2 * b + h + 1)
                            last = pe.matmul(pP[g][:, FREE * h:FREE * h + FREE], w_in[:, g * D:g * D + D],
                                             XNT[:, FREE * h:FREE * h + FREE], start=True, stop=True)
                        last.then_inc(proj_ps, 1)

                def transpose_v(b):
                    pe.wait_ge(vhi_ready, b + 2)
                    for h in range(2):
                        if h:
                            pe.wait_ge(vlo_ready, b + 2)
                        for j in range(TB):
                            last = pe.transpose(pV[:, h, j, :], VP[:, h, P * j:P * j + P], ident16[:])
                    last.then_inc(vt_ps, 1)

                pe.wait_ge(consts_in, 16 * N_VEC_DMAS)
                pe.transpose(pT[:, 0:N_VEC], vecs, ident[0:N_VEC, 0:N_VEC]).then_inc(cols_ps, 1)
                filter_layer(0)
                pe.wait_ge(cols_ready, 2)
                transpose_x(0, True)
                filter_layer(1)
                project(0, (0, 1))
                pe.wait_ge(fl_arg, 2)
                project(0, (2,))
                transpose_x(1, True)
                project(1, (0, 1))
                pe.wait_ge(up_ready, 6)
                filter_layer(2)
                filter_layer(3)
                pe.wait_ge(frow_ready, 1)
                project(1, (2,))
                with pe.Fori(0, B - 2) as b:
                    transpose_x(b + 2, False)
                    pe.wait_ge(xnt_ready, 2 * b + 6)
                    transpose_v(b)
                    project(b + 2, range(3))
                transpose_v(B - 2)
                pe.wait_ge(vt_ready, B)
                transpose_v(B - 1)

            @block.scalar
            def _(act):
                for dst, name in ((z, "c_z"), (decay, "c_decay"), (fw1, "L0_attn_a_f_w1"),
                                  (fw23[:, 0, :], "L0_attn_a_f_w2"), (fw23[:, 1, :], "L0_attn_a_f_w3"),
                                  (fwout, "L0_attn_a_f_wout")):
                    act.dma_start(dst, ins[name]).then_inc(w_landed, 16)
                act.dma_start(w_in[:], ins["L0_attn_a_w_in"]).then_inc(w_landed, 16)
                act.dma_start(sfw[:], ins["L0_attn_a_sf_w"].rearrange("(g p) k -> p g k", p=P)).then_inc(w_landed, 16)
                act.sem_inc(vt_ready, 1)
                act.sem_inc(up_ready, 3)
                act.sem_inc(vhi_ready, 1)

                def filter_sin(n):
                    act.wait_ge(fl_arg, n + 1)
                    act.activation(fh[:, n % 2, :], fq[:, 0, :], ACT.Sin).then_inc(fl_ready, 1)

                def norm(b, par):
                    act.wait_ge(n_chain, (b + 1) * row_stats_steps(TB))
                    act.wait_ge(xnt_ps, 2 * b + 2)
                    for j in range(TB // 2, TB):
                        last = act.activation(XN[:, j, :], U[:, par, j, :], ACT.Identity,
                                              scale=sm[:, 1, j:j + 1], bias=sm[:, 2, j:j + 1])
                    last.then_inc(xn_ready, 1)

                def columns(b):
                    for h in range(2):
                        act.wait_ge(xnt_ps, 2 * b + h + 3)
                        if h == 0:
                            act.wait_ge(proj_ps, 3 * b + 3)
                        act.activation(XNT[:, FREE * h:FREE * h + FREE], pT[:, FREE * h:FREE * h + FREE],
                                       ACT.Copy).then_inc(xnt_ready, 1)

                def first_taps(b, ns):
                    for n in ns:
                        g = ORDER[n]
                        act.wait_ge(proj_ps, 3 * b + n + 4)
                        if g:
                            act.wait_ge(tap_done, 2 * b + n + 1)
                        else:
                            act.wait_ge(x0_done, b + 1)
                        act.activation(UP[:, g, 2:L + 2], pP[g][:], ACT.Identity,
                                       bias=cols[:, V_BIN + g:V_BIN + g + 1]).then_inc(up_ready, 1)
                        act.wait_ge(up_ready, 3 * b + n + 4)
                        if n == 0:
                            act.wait_ge(vv_ready, b + 1)
                        act.activation(TAP[:, g, :], UP[:, g, 2:L + 2], ACT.Identity, scale=sfw[:, g, 2:3],
                                       bias=cols[:, V_SFB + g:V_SFB + g + 1]).then_inc(tap0_ready, 1)

                def high(b):
                    act.wait_ge(s_chain, (b + 1) * SPLIT_STEPS)
                    act.wait_ge(vt_ps, b + 1)
                    act.activation(VP[:, 0, :], VV, ACT.Copy, scale=vscale[:, 2:3]).then_inc(vhi_ready, 1)

                def copy_v(b):
                    act.wait_ge(vt_ps, b + 2)
                    act.activation(VT[:, :, :, bass.ds(b, 1), :].rearrange("p h j b d -> p (h j) (b d)"),
                                   pV.rearrange("p h j d -> p (h j) d"), ACT.Copy).then_inc(vt_ready, 1)

                norm(0, 0)
                filter_sin(0)
                columns(0)
                norm(1, 1)
                filter_sin(1)
                act.wait_ge(cols_ready, 1)
                act.wait_ge(zeroed, 3)
                act.wait_ge(w_landed, 16 * N_W_DMAS)
                first_taps(0, range(3))
                columns(1)
                norm(2, 0)
                filter_sin(2)

                def step(b, par):
                    first_taps(b + 1, (0, 1))
                    high(b)
                    if not (isinstance(b, int) and b == 0):
                        norm(b + 2, par)
                    columns(b + 2)
                    first_taps(b + 1, (2,))
                    copy_v(b)

                step(0, 0)
                step(1, 1)
                with act.Fori(1, B // 2 - 1) as i:
                    for par in range(2):
                        step(2 * i + par, par)
                first_taps(B - 1, (0, 1))
                high(B - 2)
                first_taps(B - 1, (2,))
                copy_v(B - 2)
                high(B - 1)
                copy_v(B - 1)

            @block.vector
            def _(dve):
                def sums(b, par, landed, first=False):
                    if not first:
                        dve.wait_ge(xn_ready, 2 * b)
                    ch = Chain(dve, n_chain, b * row_stats_steps(TB))
                    dve.wait_ge(u_landed[par], landed)
                    row_sums(nc, ch, lambda j: U[:, par, j, :], TB, st)
                    return ch

                def norm(b, par, ch, first=False):
                    row_stats_end(nc, ch, st, sm)
                    assert ch.n == row_stats_steps(TB)
                    if not first:
                        dve.wait_ge(xnt_ps, 2 * b + 2)
                    for j in range(TB // 2):
                        last = nc.vector.tensor_scalar(XN[:, j, :], U[:, par, j, :], sm[:, 0, j:j + 1], sm[:, 1, j:j + 1],
                                                       ALU.subtract, ALU.mult)
                    last.then_inc(xn_ready, 1)

                ch = Chain(dve, fl_chain)

                def filter_argument(n):
                    fb = cols[0:FO, V_F + 2 * n:V_F + 2 * n + 1]
                    fr = cols[0:FO, V_F + 2 * n + 1:V_F + 2 * n + 2]
                    dve.wait_ge(fl_ps, n + 1)
                    if n:
                        dve.wait_ge(fl_ready, n)
                    ch.link(nc.vector.tensor_scalar(fq[:, 0, :], pP[0][0:FO, 0:FL], fb, fr, ALU.add, ALU.mult))
                    ch.link(nc.vector.tensor_scalar(fq[:, 1, :], fq[:, 0, :], 1.0 / TWO_PI, ROUNDER, ALU.mult, ALU.add))
                    ch.link(nc.vector.tensor_scalar(fq[:, 1, :], fq[:, 1, :], ROUNDER, None, ALU.subtract))
                    for c in TURN_PARTS:
                        ch.link(nc.vector.scalar_tensor_tensor(fq[:, 0, :], fq[:, 1, :], -c, fq[:, 0, :], ALU.mult, ALU.add))
                    nc.vector.tensor_scalar(fq[:, 0, :], fq[:, 0, :], PI_BELOW, -PI_BELOW, ALU.min, ALU.max).then_inc(fl_arg, 1)

                def filter_rows():
                    dve.wait_ge(fl_ps, 4)
                    dve.wait_ge(zeroed, 2)
                    ch.link(nc.vector.tensor_tensor(frow[:, P:P + FL], pP[0][:, 0:FL], decay, ALU.mult))
                    ch.link(nc.vector.tensor_tensor(frow[:, P + FL - 1:P + FL], frow[:, P + FL - 1:P + FL],
                                                    cols[:, V_FBIAS:V_FBIAS + 1], ALU.add))
                    ch.link(nc.vector.tensor_reduce(fscale[:, 0:1], frow[:, P:P + FL], AX.X, ALU.max, apply_absolute_value=True))
                    power_of_two_scale(nc, ch, fscale[:, 0:1], fscale[:, 1:2], fscale[:, 2:3])
                    ch.link(nc.vector.tensor_scalar(fparts[:, 0, :], frow, fscale[:, 2:3], None, ALU.mult))
                    nc.vector.scalar_tensor_tensor(fparts[:, 1, :], frow, fscale[:, 2:3], fparts[:, 0, :],
                                                   ALU.mult, ALU.subtract).then_inc(frow_ready, 1)

                def taps(b):
                    ch = Chain(dve, t_chain, b * TAPS_STEPS)
                    for n, g in enumerate(ORDER[:2]):
                        dve.wait_ge(tap0_ready, 3 * b + n + 1)
                        ch.link(nc.vector.scalar_tensor_tensor(TAP[:, g, :], UP[:, g, 1:L + 1], sfw[:, g, 1:2],
                                                               TAP[:, g, :], ALU.mult, ALU.add))
                        nc.vector.scalar_tensor_tensor(TAP[:, g, :], UP[:, g, 0:L], sfw[:, g, 0:1],
                                                       TAP[:, g, :], ALU.mult, ALU.add).then_inc(tap_done, 1)

                def scale(b):
                    ch = Chain(dve, s_chain, b * SPLIT_STEPS)
                    dve.wait_ge(vv_ready, b + 2)
                    ch.link(nc.vector.tensor_reduce(vscale[:, 0:1], VV, AX.X, ALU.max, apply_absolute_value=True))
                    dve.wait_ge(vhi_ready, b + 1)
                    power_of_two_scale(nc, ch, vscale[:, 0:1], vscale[:, 1:2], vscale[:, 2:3])
                    assert ch.n == SPLIT_STEPS

                def weigh(b):
                    nc.vector.tensor_tensor(ascale[:, bass.ds(b, 1)], vscale[:, 1:2], fscale[:, 1:2], ALU.mult)

                def low(b):
                    dve.wait_ge(vhi_ready, b + 2)
                    nc.vector.scalar_tensor_tensor(VP[:, 1, :], VV, vscale[:, 2:3], VP[:, 0, :],
                                                   ALU.mult, ALU.subtract).then_inc(vlo_ready, 1)

                dve.sem_inc(tap_done, 2)
                dve.sem_inc(vlo_ready, 1)
                norm(0, 0, sums(0, 0, 16, True), True)
                dve.wait_ge(cols_ps, 1)
                nc.vector.tensor_copy(cols[:], pT[:, 0:N_VEC]).then_inc(cols_ready, 1)
                dve.wait_ge(cols_ready, 1)
                nc.vector.tensor_copy(ident16[:], ident[:]).then_inc(cols_ready, 1)
                filter_argument(0)
                norm(1, 1, sums(1, 1, 16))
                filter_argument(1)
                taps(0)
                norm(2, 0, sums(2, 0, 32))
                filter_argument(2)
                scale(0)
                filter_rows()
                weigh(0)
                low(0)

                def step(b, par, landed):
                    taps(b)
                    ch = sums(b + 2, par, landed)
                    scale(b)
                    weigh(b)
                    norm(b + 2, par, ch)
                    low(b)

                step(1, 1, 32)
                with dve.Fori(1, B // 2 - 1) as i:
                    for par in range(2):
                        step(2 * i + par, par, 16 * i + 32)
                for b in (B - 2, B - 1):
                    taps(b)
                    scale(b)
                    weigh(b)
                    low(b)

        with ExitStack() as c2:
            sem2 = lambda n: c2.enter_context(nc.semaphore(n))
            VG = c2.enter_context(nc.sbuf_tensor("VG", [P, RING, 2, CH, TB * B], F16))
            pY = [c2.enter_context(nc.psum_tensor(f"pY{r}", [P, CH, TB * B], F32)) for r in range(RING)]
            vg_ready, conv_done, y_ready = sem2("vg_ready"), sem2("conv_done"), sem2("y_ready")
            block = c2.enter_context(nc.Block())

            @block.sync
            def _(sp):
                with sp.Fori(1, NG // RING) as i:
                    for r in range(RING):
                        sp.wait_ge(conv_done, RING * (i - 1) + r + 1 + RING)
                        load_toeplitz(sp, RING * i + r, r)

            @block.vector
            def _(dve):
                dve.sem_inc(vg_ready, 1)
                with dve.Fori(0, NG // RING) as i:
                    for r in range(RING):
                        dve.wait_ge(conv_done, RING * i + r + 1)
                        dve.wait_ge(toep_landed[r], 16 * i + 16)
                        fill_toeplitz(r)
                        for h in range(2):
                            last = nc.vector.tensor_copy(
                                VG[:, r, h], VT[:, h, :, :, bass.ds((RING * i + r) * CH, CH)].rearrange("p j b c -> p c (j b)"))
                        last.then_inc(vg_ready, 1)

            @block.tensor
            def _(pe):
                pe.sem_inc(conv_done, RING)
                with pe.Fori(0, NG // RING) as i:
                    for r in range(RING):
                        pe.wait_ge(vg_ready, RING * i + r + 2)
                        pe.wait_ge(y_ready, RING * i + r + 1)
                        x0 = FL + HP * (r % 2)
                        for c in range(CH):
                            for d in range(TB // 2 + 1):
                                for k, v in PARTS:
                                    last = pe.matmul(pY[r][:, c, B * d:], toep[:, r, c, k, x0 - P * d:x0 - P * d + P],
                                                     VG[:, r, v, c, 0:B * (TB - d)],
                                                     start=d == 0 and (k, v) == PARTS[0],
                                                     stop=d == TB // 2 and (k, v) == PARTS[-1])
                        last.then_inc(conv_done, 1)

            @block.scalar
            def _(act):
                act.sem_inc(y_ready, RING)
                with act.Fori(0, NG // RING) as i:
                    for r in range(RING):
                        act.wait_ge(conv_done, RING * i + r + 1 + RING)
                        act.activation(Y[:, :, bass.ds((RING * i + r) * CH, CH)],
                                       pY[r][:].rearrange("p c n -> p n c"), ACT.Copy).then_inc(y_ready, 1)


class RecurrentWeights:

    NAMES = ("W1", "W2", "Wo", "Wz", "Wh")

    def __init__(self, nc, ctx):
        self.nc = nc
        shapes = [[P, EX], [P, EX], [P, EC, D], [P, EC, EX], [P, EC, EX]]
        self.parts = [[ctx.enter_context(nc.sbuf_tensor(f"b_{n}_{x}", s, F32R)) for x in ("high", "low")]
                      for n, s in zip(self.NAMES, shapes)]
        self.shapes = shapes

    def open(self, ctx):
        self.raw = [ctx.enter_context(self.nc.sbuf_tensor(f"b_{n}_raw", s, F32)) for n, s in zip(self.NAMES, self.shapes)]
        self.landed, self.high = (ctx.enter_context(self.nc.semaphore("bw_" + n)) for n in ("landed", "high"))

    def load(self, sp, ins):
        for raw, n in zip(self.raw, self.NAMES):
            src = ins["L0_attn_b_" + n]
            sp.dma_start(raw[:], src if n in ("W1", "W2") else src.rearrange("(k p) n -> p k n", p=P)).then_inc(self.landed, 16)

    def split_high(self, act):
        act.wait_ge(self.landed, 16 * len(self.raw))
        for raw, (high, _) in zip(self.raw, self.parts):
            act.activation(high[:], raw[:], ACT.Copy).then_inc(self.high, 1)

    def split_low(self, dve):
        for n, (raw, (high, low)) in enumerate(zip(self.raw, self.parts)):
            dve.wait_ge(self.high, n + 1)
            self.nc.vector.tensor_tensor(low[:], raw[:], f32(high[:]), ALU.subtract)


def build_experts(nc, ins, slots, out, keep, tag, ahead=None):
    ident, cols = keep["ident"], keep["cols"]
    w1, w2 = ins["L0_ffn_W1"], ins["L0_ffn_W2"].rearrange("e (k p) d -> e p k d", p=P)
    with ExitStack() as ctx:
        sb = lambda n, s, d=F32: ctx.enter_context(nc.sbuf_tensor(tag + n, s, d))
        sem = lambda n: ctx.enter_context(nc.semaphore(tag + n))
        ps = lambda n: ctx.enter_context(nc.psum_tensor(tag + n, [P, FREE], F32))
        parts = lambda n, s: (sb(n + "h", s, F32R), sb(n + "l", s, F32R))
        G = sb("rows", [P, NE, SC, ROW])
        W1F, W2F = sb("w1f", [P, 2, HID]), sb("w2f", [P, 2, HC, D])
        W1, W2, XT, HT = parts("w1", [P, 2, HID]), parts("w2", [P, 2, HC, D]), parts("xt", [P, 2, CAP]), parts("ht", [P, 2, HC, CAP])
        XN, HF, YT, O = sb("xn", [P, SC, D]), sb("hf", [P, HC, CAP]), sb("yt", [P, CAP]), sb("o", [P, 2, SC, D])
        token = sb("token", [P, 2, SC], I32)
        pX, pH, pY, pO = ps("pX"), *([ps(f"{n}{r}") for r in range(2)] for n in ("pH", "pY", "pO"))
        (first_rows, other_rows, xn_ready, xt_ps, x_high, x_low, w1_high, w1_low, w2_high, w2_low, h_ps, h_high, h_low,
         y_ps, y_ready, o_ps, o_ready, rows_free) = (sem(x) for x in (
             "first_rows other_rows xn_ready xt_ps x_high x_low w1_high w1_low w2_high w2_low h_ps h_high h_low "
             "y_ps y_ready o_ps o_ready rows_free").split())
        sent = [sem("sent0"), sem("sent1")]
        w1_landed, w2_landed = ([sem(x + "0"), sem(x + "1")] for x in ("w1_", "w2_"))
        if ahead:
            ahead.open(ctx)
        block = ctx.enter_context(nc.Block())
        rows = slots.rearrange("(e p j) d -> p e j d", e=NE, j=SC)

        def experts(eng, step):
            step(0, 0)
            step(1, 1)
            with eng.Fori(1, NE // 2 - 1) as i:
                step(2 * i, 0)
                step(2 * i + 1, 1)
            step(NE - 2, 0)
            step(NE - 1, 1)

        def exists(e):
            return not isinstance(e, int) or 0 <= e < NE


        @block.sync
        def _(sp):
            sp.dma_start(G[:, 0:2], rows[:, 0:2]).then_inc(first_rows, 16)
            for par in range(2):
                sp.dma_start(W1F[:, par], w1[par]).then_inc(w1_landed[par], 16)
                sp.dma_start(W2F[:, par], w2[par]).then_inc(w2_landed[par], 16)
            sp.dma_start(G[:, 2:NE], rows[:, 2:NE]).then_inc(other_rows, 16)
            with sp.Fori(1, NE // 2) as i:
                for par in range(2):
                    e = 2 * i + par
                    sp.wait_ge(w1_low, e - 1)
                    sp.dma_start(W1F[:, par], w1[bass.ds(e, 1)].rearrange("e p n -> (e p) n")).then_inc(w1_landed[par], 16)
                    sp.wait_ge(w2_low, e - 1)
                    sp.dma_start(W2F[:, par], w2[bass.ds(e, 1)].rearrange("e p k d -> (e p) k d")).then_inc(w2_landed[par], 16)
            if ahead:
                ahead.load(sp, ins)

        @block.gpsimd
        def _(pool):
            limit = pool.alloc_register(tag + "last_token")
            pool.reg_mov(limit, B * L - 1)
            last_token = pool.snap(limit)
            pool.sem_inc(rows_free, 2)

            def release(e, par):
                pool.wait_ge(sent[par], 8 * SC * (e - par) + 16 * SC)
                pool.sem_inc(rows_free, 1)

            def step(e, par):
                pool.wait_ge(o_ready, e + 3)
                pool.nop(nofuse=True)
                for j in range(SC):
                    pool.indirect_dma_start(
                        out=out, out_offset=bass.IndirectOffsetOnAxis(ap=token[:, par, j:j + 1], axis=0),
                        in_=O[:, par, j, :], in_offset=None, bounds_check=last_token, oob_is_err=False
                    ).then_inc(sent[par], 16)
                    if j == 1 and exists(e - 1):
                        release(e - 1, 1 - par)

            experts(pool, step)
            release(NE - 1, 1)

        @block.tensor
        def _(pe):
            def product(dst, w, x, start, stop):
                for n, (i, j) in enumerate(PARTS):
                    last = pe.matmul(dst, w[i], x[j], start=start and n == 0, stop=stop and n == len(PARTS) - 1)
                return last

            def transpose_rows(e):
                pe.wait_ge(xn_ready, e + 1)
                pe.wait_ge(x_low, e + 1)
                for j in range(SC):
                    last = pe.transpose(pX[:, P * j:P * j + P], XN[:, j, :], ident[:])
                last.then_inc(xt_ps, 1)

            def hidden(e, par, k):
                if k == 0:
                    pe.wait_ge(x_low, e + 2)
                    pe.wait_ge(w1_low, e + 1)
                pe.wait_ge(h_high, HC * e + k + 1)
                product(pH[k % 2][:], [w[:, par, P * k:P * k + P] for w in W1], [x[:, par, :] for x in XT],
                        True, True).then_inc(h_ps, 1)

            def outer(e, par, k):
                if k == 0:
                    pe.wait_ge(w2_low, e + 1)
                    pe.wait_ge(y_ready, e + 1)
                pe.wait_ge(h_low, HC * e + k + 1 + HC)
                last = product(pY[par][:], [w[:, par, k, :] for w in W2], [h[:, par, k, :] for h in HT], k == 0, k == HC - 1)
                if k == HC - 1:
                    last.then_inc(y_ps, 1)

            def transpose_out(e, par):
                pe.wait_ge(y_ready, e + 3)
                pe.wait_ge(o_ready, e + 1)
                for j in range(SC):
                    last = pe.transpose(pO[par][:, P * j:P * j + P], YT[:, P * j:P * j + P], ident[:])
                last.then_inc(o_ps, 1)

            def step(e, par):
                for k in range(HC):
                    hidden(e, par, k)
                    if exists(e - 1):
                        outer(e - 1, 1 - par, k)
                    if k == 2 and exists(e - 2):
                        transpose_out(e - 2, par)
                    if k == 1 and exists(e + 1):
                        transpose_rows(e + 1)

            pe.sem_inc(xt_ps, 1)
            transpose_rows(0)
            experts(pe, step)
            for k in range(HC):
                outer(NE - 1, 1, k)
                if k == 2:
                    transpose_out(NE - 2, 0)
            transpose_out(NE - 1, 1)

        @block.scalar
        def _(act):
            act.sem_inc(h_high, 2)
            act.sem_inc(y_ready, 2)

            def columns(e, par):
                act.wait_ge(xt_ps, e + 2)
                act.activation(XT[0][:, par, :], pX[:], ACT.Copy).then_inc(x_high, 1)

            def weights(e, par, landed, raw, split, done):
                act.wait_ge(landed[par], (e - par) * 8 + 16)
                act.activation(split[0][:, par], raw[:, par], ACT.Copy).then_inc(done, 1)

            def relus(e, par, k):
                act.wait_ge(h_ps, HC * e + k + 1)
                act.wait_ge(h_low, HC * e + k + 1)
                bias = cols[:, bass.ds(V_FFN + e * HC + k, 1)]
                act.activation(HF[:, k, :], pH[k % 2][:], ACT.Relu, bias=bias)
                act.activation(HT[0][:, par, k, :], pH[k % 2][:], ACT.Relu, bias=bias).then_inc(h_high, 1)

            def outs(e, par):
                act.wait_ge(y_ps, e + 1)
                act.activation(YT[:], pY[par][:], ACT.Identity, bias=cols[:, bass.ds(V_FB2 + e, 1)]).then_inc(y_ready, 1)

            def step(e, par):
                if exists(e - 2):
                    outs(e - 2, par)
                relus(e, par, 0)
                relus(e, par, 1)
                if exists(e + 1):
                    columns(e + 1, 1 - par)
                    weights(e + 1, 1 - par, w1_landed, W1F, W1, w1_high)
                relus(e, par, 2)
                weights(e, par, w2_landed, W2F, W2, w2_high)
                relus(e, par, 3)

            weights(0, 0, w1_landed, W1F, W1, w1_high)
            columns(0, 0)
            experts(act, step)
            outs(NE - 2, 0)
            outs(NE - 1, 1)
            if ahead:
                ahead.split_high(act)

        @block.vector
        def _(dve):
            Ge = G[:].rearrange("p e j d -> p (e j) d")
            dve.sem_inc(x_low, 1)
            dve.sem_inc(h_low, HC)
            dve.sem_inc(o_ready, 2)

            def norm(e):
                dve.wait_ge(xt_ps, e + 1)
                for j in range(SC):
                    g = Ge[:, bass.ds(e * SC + j, 1), :].rearrange("p a d -> p (a d)")
                    last = nc.vector.tensor_scalar(XN[:, j, :], g[:, 0:D], g[:, C_MEAN:C_MEAN + 1], g[:, C_RSTD:C_RSTD + 1],
                                                   ALU.subtract, ALU.mult)
                last.then_inc(xn_ready, 1)

            def low_columns(e, par):
                dve.wait_ge(x_high, e + 1)
                nc.vector.tensor_tensor(XT[1][:, par, :], pX[:], f32(XT[0][:, par, :]), ALU.subtract).then_inc(x_low, 1)

            def low_weights(e, par, raw, split, high, done):
                dve.wait_ge(high, e + 1)
                nc.vector.tensor_tensor(split[1][:, par], raw[:, par], f32(split[0][:, par]), ALU.subtract).then_inc(done, 1)

            def low_hidden(e, par, k):
                dve.wait_ge(h_high, HC * e + k + 3)
                nc.vector.tensor_tensor(HT[1][:, par, k, :], HF[:, k, :], f32(HT[0][:, par, k, :]), ALU.subtract
                                        ).then_inc(h_low, 1)

            def add(e, par):
                dve.wait_ge(o_ps, e + 1)
                dve.wait_ge(rows_free, e + 1)
                nc.vector.tensor_copy(token[:, par, :], Ge[:, bass.ds(e * SC, SC), C_TOK].bitcast(I32))
                for j in range(SC):
                    g = Ge[:, bass.ds(e * SC + j, 1), :].rearrange("p a d -> p (a d)")
                    last = nc.vector.scalar_tensor_tensor(O[:, par, j, :], pO[par][:, P * j:P * j + P], g[:, C_GATE:C_GATE + 1],
                                                          g[:, 0:D], ALU.mult, ALU.add)
                last.then_inc(o_ready, 1)

            def step(e, par):
                low_hidden(e, par, 0)
                low_hidden(e, par, 1)
                if exists(e + 1):
                    low_columns(e + 1, 1 - par)
                    low_weights(e + 1, 1 - par, W1F, W1, w1_high, w1_low)
                low_hidden(e, par, 2)
                low_weights(e, par, W2F, W2, w2_high, w2_low)
                low_hidden(e, par, 3)
                if exists(e + 2):
                    if isinstance(e, int) and e == 0:
                        dve.wait_ge(other_rows, 16)
                    norm(e + 2)
                if exists(e - 2):
                    add(e - 2, par)

            dve.wait_ge(first_rows, 16)
            norm(0)
            low_weights(0, 0, W1F, W1, w1_high, w1_low)
            low_columns(0, 0)
            norm(1)
            experts(dve, step)
            add(NE - 2, 0)
            add(NE - 1, 1)
            if ahead:
                ahead.split_low(dve)


def build(nc, ins, out):
    x1 = nc.dram_tensor("x1", (B * L, D), F32).ap()
    scr = {"filt": nc.dram_tensor("filt_rows", (P, 2, RW), F16).ap(), "x1": x1,
           "slots1": nc.dram_tensor("slots1", (NE * CAP, ROW), F32).ap(),
           "slots2": nc.dram_tensor("slots2", (NE * CAP, ROW), F32).ap()}
    with ExitStack() as ctx:
        sb = lambda n, s, d=F32: ctx.enter_context(nc.sbuf_tensor(n, s, d))
        ident, cols = sb("ident", [P, P]), sb("cols", [P, N_VEC])
        tables = {"ident": ident, "slot": sb("t_slot", [P, 3 * NE]), "token": sb("t_token", [P, NT], I32),
                  "tri16": sb("t_tri", [P, P], BF16), "ones16": sb("t_ones", [P, P], BF16)}
        gatew = {"gate": sb("gate_w", [P, NE]), "gate_b": sb("gate_b", [P, NE])}
        keep = {"ident": ident, "cols": cols, "tables": tables, "gatew": gatew}
        keep["empty"], keep["cleared"] = sb("empty", [P, ROW]), ctx.enter_context(nc.semaphore("cleared"))
        build_tables(nc, ins, keep)
        with ExitStack() as c1:
            keep["ascale"] = c1.enter_context(nc.sbuf_tensor("ascale", [P, B], F32))
            keep["X0T"] = c1.enter_context(nc.sbuf_tensor("X0T", [P, B * L], F32))
            keep["Y"] = c1.enter_context(nc.sbuf_tensor("Y", [P, TB * B, D], F32))
            build_mixer(nc, ins, scr, keep)
            build_mixer_out(nc, ins, scr, keep)
        with ExitStack() as c2:
            weights = RecurrentWeights(nc, c2)
            build_experts(nc, ins, scr["slots1"], x1, keep, "e1_", weights)
            build_recurrent(nc, weights, x1, out, scr["slots2"], keep)
        build_experts(nc, ins, scr["slots2"], out, keep, "e2_")


def build_tables(nc, ins, keep):
    t, g = keep["tables"], keep["gatew"]
    with ExitStack() as ctx:
        tri = ctx.enter_context(nc.sbuf_tensor("tri", [P, P], F32))
        empty = keep["empty"]
        landed = ctx.enter_context(nc.semaphore("tb_landed"))
        block = ctx.enter_context(nc.Block())

        @block.sync
        def _(sp):
            sp.dma_start(tri[:], ins["c_tri"]).then_inc(landed, 16)
            sp.dma_start(t["slot"][:], ins["c_slot"]).then_inc(landed, 16)
            sp.dma_start(g["gate"][:], ins["L0_ffn_Wg"]).then_inc(landed, 16)
            sp.dma_start(g["gate_b"][:], row_to_all(ins["L0_ffn_bg"], NE)).then_inc(landed, 16)

        @block.gpsimd
        def _(pool):
            pool.memset(empty[:, 0:C_TOK], 0.0)
            pool.memset(t["ones16"][:], 1.0)
            pool.iota(t["token"][:], pattern=[[P, NT]], base=0, channel_multiplier=1)
            pool.iota(empty[:, C_TOK:C_TOK + 1].bitcast(I32), pattern=[[0, 1]], base=NO_TOKEN, channel_multiplier=0)

        @block.vector
        def _(dve):
            dve.wait_ge(landed, 64)
            nc.vector.tensor_copy(t["tri16"][:], tri[:])


def build_recurrent(nc, weights, x, out, slots, keep):
    ident, cols = keep["ident"], keep["cols"]
    CT = 4
    CW = CT * P
    NC = B * L // CW
    xin = x.rearrange("(c j p) d -> c p j d", p=P, j=CT)
    xout = out.rearrange("(c j p) d -> c p j d", p=P, j=CT)
    with ExitStack() as ctx:
        sb = lambda n, s, d=F32: ctx.enter_context(nc.sbuf_tensor("b_" + n, s, d))
        sem = lambda n: ctx.enter_context(nc.semaphore("b_" + n))
        ps = lambda n: ctx.enter_context(nc.psum_tensor("b_" + n, [P, FREE], F32))
        parts = lambda n, s: (sb(n + "h", s, F32R), sb(n + "l", s, F32R))
        W1, W2, WO, WZ, WH = weights.parts
        XB, XN = sb("xb", [P, 2, CT, D]), sb("xn", [P, CT, D])
        XT, XI, S = parts("xt", [P, 2, CW]), parts("xi", [P, 2, EC, CW]), parts("s", [P, EC, CW])
        XF, SF, YT = sb("xf", [P, EC, CW]), sb("sf", [P, EC, CW]), sb("yt", [P, CW])
        SK, H = sb("sk", [P, 2, EC, CW]), sb("h", [P, 2, EC, CW])
        Z, A, BB = sb("z", [P, EC, CW]), sb("a", [P, EC, CW]), sb("bb", [P, EC, CW])
        R = sb("rows", [P, 2, CT, ROW])
        bz2 = sb("bz2", [P, EC])
        st, sm = sb("st", [P, CT, 6]), sb("sm", [P, 4, CT])
        pX, pU, pZ, pH, pY, pO, pS = ps("pX"), [ps("pU0"), ps("pU1")], ps("pZ"), ps("pH"), ps("pY"), ps("pO"), ps("pS")
        (xn_ready, xt_ps, xth, xtl, up_ps, up_read, xih, xil, z_ps, z_read, a_ready, h_ps,
         b_done, scan_done, s_done, sh, sl, sum_read, y_ps, y_ready, o_ps, rows_ready, chain) = (sem(n) for n in (
             "xn_ready xt_ps xth xtl up_ps up_read xih xil z_ps z_read a_ready h_ps "
             "b_done scan_done s_done sh sl sum_read y_ps y_ready o_ps rows_ready chain").split())
        x_landed, r_landed, stored = ([sem(n + "0"), sem(n + "1")] for n in ("x_landed", "r_landed", "stored"))
        rt = Router(nc, ctx, CT, 2, R, keep["gatew"], slots, keep["tables"], pX, pS, pS, False)
        block = ctx.enter_context(nc.Block())

        def chunks(eng, step, last=2):
            step(0, 0)
            step(1, 1)
            with eng.Fori(1, (NC - last) // 2) as i:
                step(2 * i, 0)
                step(2 * i + 1, 1)
            for c in range(NC - last, NC):
                step(c, c % 2)

        def exists(c):
            return not isinstance(c, int) or 0 <= c < NC

        turn = lambda c, par: (c - par) * 8
        one = lambda ap, c: ap[c] if isinstance(c, int) else ap[bass.ds(c, 1)].rearrange("c p j d -> (c p) j d")

        @block.sync
        def _(sp):
            for par in range(2):
                sp.dma_start(XB[:, par], xin[par]).then_inc(x_landed[par], 16)
            for par in range(2):
                sp.dma_start(R[:, par, :, 0:D], xin[par]).then_inc(r_landed[par], 16)
            sp.wait_ge(xn_ready, 1)
            sp.dma_start(XB[:, 0], xin[2]).then_inc(x_landed[0], 16)

            def store(c, par):
                sp.wait_ge(rows_ready, c + 1)
                sp.dma_start(one(xout, c), R[:, par, :, 0:D]).then_inc(stored[par], 16)

            def step(c, par):
                if exists(c - 2):
                    store(c - 2, par)
                if exists(c + 3):
                    sp.wait_ge(xn_ready, c + 2)
                    sp.dma_start(XB[:, 1 - par], one(xin, c + 3)).then_inc(x_landed[1 - par], 16)
                if exists(c - 2):
                    sp.wait_ge(stored[par], turn(c, par))
                    sp.nop(nofuse=True)
                    sp.wait_ge(rt.rows_free, c + 1)
                    sp.dma_start(R[:, par, :, 0:D], one(xin, c)).then_inc(r_landed[par], 16)

            chunks(sp, step, last=4)
            for par in range(2):
                store(NC - 2 + par, par)
            for par in range(2):
                sp.wait_ge(stored[par], 16 * (NC // 2))

        @block.gpsimd
        def _(pool):
            rt.pool_start(pool)

            def step(c, par):
                for m in range(EC):
                    pool.wait_ge(scan_done, EC * c + m + 1 + EC)
                    pool.tensor_tensor(SF[:, m, :], H[:, par, m, :], SK[:, par, m, :], ALU.add).then_inc(s_done, 1)
                if exists(c - 2):
                    rt.pool_send(pool, c - 2, par)
                    rt.pool_release(pool, c - 2)

            chunks(pool, step)
            for par in range(2):
                rt.pool_send(pool, NC - 2 + par, par)
                rt.pool_release(pool, NC - 2 + par)

        @block.tensor
        def _(pe):
            def product(dst, w, x, start, stop):
                for n, (i, j) in enumerate(PARTS):
                    last = pe.matmul(dst, w[i], x[j], start=start and n == 0, stop=stop and n == len(PARTS) - 1)
                return last

            def transpose_in(c):
                pe.wait_ge(xn_ready, c + 1)
                for j in range(CT):
                    last = pe.transpose(pX[:, P * j:P * j + P], XN[:, j, :], ident[:])
                last.then_inc(xt_ps, 1)

            def up(c, par, m, q):
                if m == 0 and q == 0:
                    pe.wait_ge(xth, c + 1)
                    pe.wait_ge(xtl, c + 1)
                pe.wait_ge(up_read, 2 * EC * c + 2 * m + q + 1)
                W = (W1, W2)[q]
                product(pU[q][:], [w[:, P * m:P * m + P] for w in W], [x[:, par, :] for x in XT], True, True).then_inc(up_ps, 1)

            def gate_block(c, par, m, W, dst, done):
                for k in range(EC):
                    if m == 0 and W is WZ:
                        pe.wait_ge(xih, EC * c + k + 1)
                        pe.wait_ge(xil, EC * c + k + 1)
                    last = product(dst[:], [w[:, k, P * m:P * m + P] for w in W], [x[:, par, k, :] for x in XI],
                                   k == 0, k == EC - 1)
                last.then_inc(done, 1)

            def down(c, ks):
                for k in ks:
                    pe.wait_ge(sh, EC * c + k + 1)
                    pe.wait_ge(sl, EC * c + k + 1)
                    done = product(pY[:], [w[:, k, :] for w in WO], [x[:, k, :] for x in S], k == 0, k == EC - 1)
                done.then_inc(y_ps if k == EC - 1 else sum_read, 1)

            def transpose_out(c):
                pe.wait_ge(y_ready, c + 1)
                if exists(c - 1):
                    pe.wait_ge(rows_ready, c)
                for j in range(CT):
                    done = pe.transpose(pO[:, P * j:P * j + P], YT[:, P * j:P * j + P], ident[:])
                done.then_inc(o_ps, 1)

            def step(c, par):
                for m in range(EC):
                    pe.wait_ge(z_read, EC * c + m + 1)
                    gate_block(c, par, m, WZ, pZ, z_ps)
                    if m == 0 and exists(c + 1):
                        transpose_in(c + 1)
                    if exists(c - 1):
                        if m == 0:
                            down(c - 1, range(EC - 1))
                        elif m == 1:
                            down(c - 1, [EC - 1])
                    if exists(c + 1):
                        up(c + 1, 1 - par, m, 0)
                    if exists(c - 2):
                        if m == 0:
                            if exists(c + 1):
                                pe.wait_ge(xtl, c + 2)
                            rt.pe_transpose(pe, c - 2)
                        elif m == 2:
                            rt.pe_counts(pe, c - 2)
                    pe.wait_ge(b_done, EC * c + m + 1)
                    gate_block(c, par, m, WH, pH, h_ps)
                    if m == 0 and exists(c - 2):
                        pe.wait_ge(sl, EC * c)
                        rt.pe_logits(pe, c - 2)
                    if m == 1 and exists(c - 1):
                        transpose_out(c - 1)
                    if exists(c + 1):
                        up(c + 1, 1 - par, m, 1)

            pe.sem_inc(xt_ps, 1)
            rt.pe_start(pe)
            transpose_in(0)
            for m in range(EC):
                for q in range(2):
                    up(0, 0, m, q)
            chunks(pe, step)
            rt.pe_transpose(pe, NC - 2)
            down(NC - 1, range(EC - 1))
            down(NC - 1, [EC - 1])
            rt.pe_logits(pe, NC - 2)
            rt.pe_counts(pe, NC - 2)
            transpose_out(NC - 1)
            rt.pe_transpose(pe, NC - 1)
            rt.pe_logits(pe, NC - 1)
            rt.pe_counts(pe, NC - 1)

        @block.scalar
        def _(act):
            act.sem_inc(up_read, 2)
            act.sem_inc(z_read, 1)

            def high_in(c, par):
                act.wait_ge(xt_ps, c + 2)
                act.activation(XT[0][:, par, :], pX[:], ACT.Copy).then_inc(xth, 1)

            def silu(c, par, m, q):
                act.wait_ge(up_ps, 2 * EC * c + 2 * m + q + 1)
                dst = SK[:, par, m, :] if q else XF[:, m, :]
                bias = (V_B1, V_B2)[q] + m
                act.activation(dst, pU[q][:], ACT.Silu, bias=cols[:, bias:bias + 1]).then_inc(up_read, 1)
                if q == 0:
                    act.wait_ge(up_read, 2 * EC * c + 2 * m + 3)
                    act.activation(XI[0][:, par, m, :], XF[:, m, :], ACT.Copy).then_inc(xih, 1)

            def high_sum(c, m):
                act.wait_ge(s_done, EC * c + m + 1)
                act.activation(S[0][:, m, :], SF[:, m, :], ACT.Copy).then_inc(sh, 1)

            def output(c):
                act.wait_ge(y_ps, c + 1)
                act.activation(YT[:], pY[:], ACT.Identity, bias=cols[:, V_BO:V_BO + 1]).then_inc(y_ready, 1)

            def step(c, par):
                for m in range(EC):
                    if m == 0 and exists(c + 1):
                        high_in(c + 1, 1 - par)
                    act.wait_ge(z_ps, EC * c + m + 1)
                    act.wait_ge(scan_done, EC * c + m + 1)
                    act.activation(Z[:, m, :], pZ[:], ACT.Tanh, scale=0.5, bias=bz2[:, m:m + 1]).then_inc(z_read, 1)
                    act.wait_ge(z_read, EC * c + m + 2)
                    act.activation(A[:, m, :], Z[:, m, :], ACT.Copy, scale=-0.5, bias=0.5)
                    act.activation(Z[:, m, :], Z[:, m, :], ACT.Copy, scale=0.5, bias=0.5).then_inc(a_ready, 1)
                    if m:
                        if m == 1 and exists(c - 1):
                            act.wait_ge(sum_read, c)
                        high_sum(c, m - 1)
                    elif exists(c - 1):
                        high_sum(c - 1, EC - 1)
                    if m == 1 and exists(c - 1):
                        output(c - 1)
                    if m == 2 and exists(c - 2):
                        rt.act_tanh(act, c - 2)
                    if exists(c + 1):
                        silu(c + 1, 1 - par, m, 0)
                    if m == 0 and exists(c - 2):
                        rt.act_transposed(act, c - 2)
                    if exists(c + 1):
                        silu(c + 1, 1 - par, m, 1)

            high_in(0, 0)
            for m in range(EC):
                for q in range(2):
                    silu(0, 0, m, q)
            chunks(act, step)
            rt.act_transposed(act, NC - 2)
            high_sum(NC - 1, EC - 1)
            rt.act_tanh(act, NC - 2)
            output(NC - 1)
            rt.act_transposed(act, NC - 1)
            rt.act_tanh(act, NC - 1)

        @block.vector
        def _(dve):
            nc.vector.tensor_scalar(bz2[:], cols[:, V_BZ:V_BZ + EC], 0.5, None, ALU.mult)
            dve.sem_inc(b_done, 1)
            dve.sem_inc(scan_done, EC)
            rt.dve_start(dve)
            steps = row_stats_steps(CT)

            def norm_stats(c, par):
                ch = Chain(dve, chain, c * steps)
                dve.wait_ge(x_landed[par], turn(c, par) + 16)
                row_stats(nc, ch, lambda j: XB[:, par, j, :], CT, st, sm)
                assert ch.n == steps

            def norm(c, par):
                dve.wait_ge(xt_ps, c + 1)
                for j in range(CT):
                    last = nc.vector.tensor_scalar(XN[:, j, :], XB[:, par, j, :], sm[:, 0, j:j + 1], sm[:, 1, j:j + 1],
                                                   ALU.subtract, ALU.mult)
                last.then_inc(xn_ready, 1)

            def low_in(c, par):
                dve.wait_ge(xth, c + 1)
                nc.vector.tensor_tensor(XT[1][:, par, :], pX[:], f32(XT[0][:, par, :]), ALU.subtract).then_inc(xtl, 1)

            def low_x(c, par, m):
                dve.wait_ge(xih, EC * c + m + 1)
                nc.vector.tensor_tensor(XI[1][:, par, m, :], XF[:, m, :], f32(XI[0][:, par, m, :]), ALU.subtract).then_inc(xil, 1)

            def low_sum(c, m):
                dve.wait_ge(sh, EC * c + m + 1)
                nc.vector.tensor_tensor(S[1][:, m, :], SF[:, m, :], f32(S[0][:, m, :]), ALU.subtract).then_inc(sl, 1)

            def new_rows(c, par):
                dve.wait_ge(o_ps, c + 1)
                dve.wait_ge(r_landed[par], turn(c, par) + 16)
                nc.vector.tensor_tensor(R[:, par, :, 0:D], pO[:].rearrange("p (j d) -> p j d", j=CT), R[:, par, :, 0:D],
                                        ALU.add).then_inc(rows_ready, 1)
                dve.wait_ge(rows_ready, c + 1)
                rt.dve_norm(dve, c, par)

            def gate(c, m):
                dve.wait_ge(h_ps, EC * c + m + 1)
                dve.wait_ge(a_ready, EC * c + m + 1)
                nc.vector.scalar_tensor_tensor(BB[:, m, :], pH[:], cols[:, V_BH + m:V_BH + m + 1], Z[:, m, :],
                                               ALU.add, ALU.mult).then_inc(b_done, 1)

            def scan(c, par, m):
                dve.wait_ge(b_done, EC * c + m + 2)
                dve.wait_ge(scan_done, EC * c + m + 1)
                start = H[:, 0, m, CW - 1:CW] if par else 0.0
                nc.vector.tensor_tensor_scan(H[:, par, m, :], A[:, m, :], BB[:, m, :], start, ALU.mult, ALU.add
                                             ).then_inc(scan_done, 1)

            def step(c, par):
                if exists(c - 1):
                    low_sum(c - 1, EC - 1)
                for m in range(EC - 1):
                    if m == 2 and exists(c - 1):
                        new_rows(c - 1, 1 - par)
                    if m:
                        low_sum(c, m - 1)
                    if exists(c + 1):
                        low_x(c + 1, 1 - par, m)
                    gate(c, m)
                    scan(c, par, m)
                    if m == 0 and exists(c - 2):
                        rt.dve_onehot(dve, c - 2)
                if exists(c + 2):
                    norm_stats(c + 2, par)
                if exists(c + 1):
                    low_x(c + 1, 1 - par, EC - 1)
                if exists(c + 2):
                    norm(c + 2, par)
                gate(c, EC - 1)
                low_sum(c, EC - 2)
                if exists(c + 2):
                    low_in(c + 2, par)
                scan(c, par, EC - 1)
                if exists(c - 2):
                    rt.dve_slots(dve, c - 2, par)

            norm_stats(0, 0)
            norm(0, 0)
            low_in(0, 0)
            norm_stats(1, 1)
            norm(1, 1)
            for m in range(EC):
                low_x(0, 0, m)
            low_in(1, 1)
            chunks(dve, step)
            low_sum(NC - 1, EC - 1)
            rt.dve_onehot(dve, NC - 2)
            rt.dve_slots(dve, NC - 2, 0)
            new_rows(NC - 1, 1)
            rt.dve_onehot(dve, NC - 1)
            rt.dve_slots(dve, NC - 1, 1)


INPUTS = """L0_attn_a_u L0_attn_a_w_in L0_attn_a_b_in L0_attn_a_sf_w L0_attn_a_sf_b L0_attn_a_f_w1 L0_attn_a_f_b1
L0_attn_a_freq1 L0_attn_a_f_w2 L0_attn_a_f_b2 L0_attn_a_freq2 L0_attn_a_f_w3 L0_attn_a_f_b3 L0_attn_a_freq3
L0_attn_a_f_wout L0_attn_a_filt_bias L0_attn_a_w_out L0_attn_a_b_out L0_attn_b_W1 L0_attn_b_b1 L0_attn_b_W2
L0_attn_b_b2 L0_attn_b_Wz L0_attn_b_bz L0_attn_b_Wh L0_attn_b_bh L0_attn_b_Wo L0_attn_b_bo L0_ffn_Wg L0_ffn_bg
L0_ffn_W1 L0_ffn_b1 L0_ffn_W2 L0_ffn_b2""".split()


def kernel(**inputs):
    import concourse.bacc as bacc
    from concourse.bass_utils import run_bass_kernel_spmd

    nc = bacc.Bacc("TRN2", target_bir_lowering=False, num_devices=1)
    arrays = {n: np.ascontiguousarray(inputs[n]) for n in INPUTS}
    arrays.update(constants())
    ins = {n: nc.dram_tensor("in_" + n, a.shape, mybir.dt.from_np(a.dtype), kind="ExternalInput").ap()
           for n, a in arrays.items()}
    out = nc.dram_tensor("out_0", (B * L, D), F32, kind="ExternalOutput").ap()
    build(nc, ins, out)
    r = run_bass_kernel_spmd(nc, [{"in_" + n: a for n, a in arrays.items()}], core_ids=[0])
    return r.results[0]["out_0"].reshape(B, L, D)
```
